# Optimizing a Trainium2 kernel written in Bass

```python
import numpy as np
import jax
import jax.numpy as jnp

def _softmax(x, axis=-1):
    return jax.nn.softmax(x, axis=axis)

def _gelu(x):
    return jax.nn.gelu(x, approximate=True)

def _silu(x):
    return jax.nn.silu(x)

def _sigmoid(x):
    return jax.nn.sigmoid(x)

def _layernorm(x, axis=-1, eps=1e-05):
    m = jnp.mean(x, axis=axis, keepdims=True)
    v = jnp.var(x, axis=axis, keepdims=True)
    return (x - m) / jnp.sqrt(v + eps)

def _scatter_add(tgt, idx, src, axis=0):
    return tgt.at[idx].add(src)

def _segment_sum(src, seg, n):
    return jax.ops.segment_sum(src, seg, n)
kernel_name = 'mk_gnn_resnorm_d4_gnn_r8_539920'

def setup_inputs(seed: int=0):
    np.random.seed(seed)
    _w = jnp.asarray

    def _rec_inputs():
        import jax
        import jax.numpy as jnp
        _gk = jax.random.key(seed)
        x = -0.0002117 + 1 * jax.random.normal(jax.random.fold_in(_gk, 1), (1250, 512), jnp.float32)
        src = jax.random.randint(jax.random.fold_in(_gk, 2), (20000,), 0, 1250, jnp.int32)
        dst = jax.random.randint(jax.random.fold_in(_gk, 3), (20000,), 0, 1250, jnp.int32)
        _o = jnp.argsort(dst, stable=True)
        src = src[_o]
        dst = dst[_o]
        edge_weight = jax.random.uniform(jax.random.fold_in(_gk, 13), (20000,), jnp.float32, 0.0, 0.999998)
        node_vec1 = jax.random.uniform(jax.random.fold_in(_gk, 14), (1250, 1), jnp.float32, 0.0, 0.999957)
        return (x, src, dst, edge_weight, node_vec1)
    x, src, dst, edge_weight, node_vec1 = _rec_inputs()

    def _L0_gnn_setup():
        import jax, jax.numpy as jnp
        import numpy as np
        N_NODES = 6250
        N_EDGES = 100000
        M_IN = 512
        H_OUT = 512
        key = jax.random.key(seed)
        k1, k2, k3, k4, k5 = jax.random.split(key, 5)
        X = jax.random.normal(k1, (N_NODES, M_IN), dtype=jnp.float32)
        limit = float(np.sqrt(6.0 / (M_IN + H_OUT)))
        W = jax.random.uniform(k2, (M_IN, H_OUT), dtype=jnp.float32, minval=-limit, maxval=limit)
        edge_src = jax.random.randint(k3, (N_EDGES,), 0, N_NODES, dtype=jnp.int64 if jax.config.jax_enable_x64 else jnp.int32)
        edge_dst = jax.random.randint(k4, (N_EDGES,), 0, N_NODES, dtype=jnp.int64 if jax.config.jax_enable_x64 else jnp.int32)
        edge_vals = jax.random.uniform(k5, (N_EDGES,), dtype=jnp.float32, minval=0.0, maxval=1.0)
        return {'X': X, 'W': W, 'edge_src': edge_src, 'edge_dst': edge_dst, 'edge_vals': edge_vals}
    _L0_gnn_all = _L0_gnn_setup()
    _L0_gnn_in = {k: v for k, v in _L0_gnn_all.items() if k in ('W',)}
    del _L0_gnn_all

    def _L1_gnn_setup():
        import jax, jax.numpy as jnp
        import numpy as np
        N_NODES = 40962
        LATENT_DIM = 512
        N_EDGES = 81924
        NUM_BLOCKS = 4
        NUM_HEADS = 4
        NUM_FREQ = 32
        BASE_PERIOD = 16
        NOISE_EMB_DIM = 16
        EPS = 1e-05

        def _cond_layer_norm(x, cond, sw, sb, bw, bb):
            mu = jnp.mean(x, axis=-1, keepdims=True)
            var = jnp.var(x, axis=-1, keepdims=True)
            xn = (x - mu) * jax.lax.rsqrt(var + EPS)
            scale = cond @ sw + sb
            bias = cond @ bw + bb
            return xn * (1.0 + scale) + bias

        def _sparse_attention(x, src, dst, wq, bq, wk, bk, wv, bv, wo, bo):
            N, D = x.shape
            H, Dh = (NUM_HEADS, D // NUM_HEADS)
            q = (x @ wq + bq).reshape(N, H, Dh) * Dh ** (-0.5)
            k = (x @ wk + bk).reshape(N, H, Dh)
            v = (x @ wv + bv).reshape(N, H, Dh)
            scores = jnp.einsum('ehd,ehd->eh', q[src], k[dst])
            smax = jax.ops.segment_max(scores, src, num_segments=N)
            ex = jnp.exp(scores - smax[src])
            denom = jax.ops.segment_sum(ex, src, num_segments=N)
            attn = ex / denom[src]
            out = jax.ops.segment_sum(attn[:, :, None] * v[dst], src, num_segments=N)
            return out.reshape(N, D) @ wo + bo

        def _forward(x, edge_index, noise_levels, f_w1, f_b1, f_w2, f_b2, s1_w, s1_b, b1_w, b1_b, wq, bq, wk, bk, wv, bv, wo, bo, s2_w, s2_b, b2_w, b2_b, m_w1, m_b1, m_w2, m_b2):
            src, dst = (edge_index[0], edge_index[1])
            freqs = jnp.arange(1, NUM_FREQ + 1, dtype=x.dtype) * (2.0 * np.pi / BASE_PERIOD)
            ph = noise_levels * freqs
            emb = jnp.concatenate([jnp.sin(ph), jnp.cos(ph)], axis=-1)
            cond = jax.nn.silu(emb @ f_w1 + f_b1) @ f_w2 + f_b2
            for i in range(NUM_BLOCKS):
                y = _cond_layer_norm(x, cond, s1_w[i], s1_b[i], b1_w[i], b1_b[i])
                y = _sparse_attention(y, src, dst, wq[i], bq[i], wk[i], bk[i], wv[i], bv[i], wo[i], bo[i])
                x = x + y
                y = _cond_layer_norm(x, cond, s2_w[i], s2_b[i], b2_w[i], b2_b[i])
                y = jax.nn.relu(y @ m_w1[i] + m_b1[i]) @ m_w2[i] + m_b2[i]
                x = x + y
            return x
        key = jax.random.key(seed)
        ks = jax.random.split(key, 20)

        def w(k, shape, s=0.02):
            return jax.random.normal(k, shape, dtype=jnp.float32) * s
        D, B, C = (LATENT_DIM, NUM_BLOCKS, NOISE_EMB_DIM)
        z = lambda *s: jnp.zeros(s, jnp.float32)
        return {'latent_mesh_nodes': jax.random.normal(ks[0], (N_NODES, D), dtype=jnp.float32), 'edge_index': jax.random.randint(ks[1], (2, N_EDGES), 0, N_NODES, dtype=jnp.int32), 'noise_levels': jax.random.uniform(ks[2], (N_NODES, 1), dtype=jnp.float32), 'f_w1': w(ks[3], (2 * NUM_FREQ, C)), 'f_b1': z(C), 'f_w2': w(ks[4], (C, C)), 'f_b2': z(C), 's1_w': w(ks[5], (B, C, D)), 's1_b': z(B, D), 'b1_w': w(ks[6], (B, C, D)), 'b1_b': z(B, D), 'wq': w(ks[7], (B, D, D)), 'bq': z(B, D), 'wk': w(ks[8], (B, D, D)), 'bk': z(B, D), 'wv': w(ks[9], (B, D, D)), 'bv': z(B, D), 'wo': w(ks[10], (B, D, D)), 'bo': z(B, D), 's2_w': w(ks[11], (B, C, D)), 's2_b': z(B, D), 'b2_w': w(ks[12], (B, C, D)), 'b2_b': z(B, D), 'm_w1': w(ks[13], (B, D, D)), 'm_b1': z(B, D), 'm_w2': w(ks[14], (B, D, D)), 'm_b2': z(B, D)}
    _L1_gnn_all = _L1_gnn_setup()
    _L1_gnn_in = {k: v for k, v in _L1_gnn_all.items() if k in ('f_w1', 'f_b1', 'f_w2', 'f_b2', 's1_w', 's1_b', 'b1_w', 'b1_b', 'wq', 'bq', 'wk', 'bk', 'wv', 'bv', 'wo', 'bo', 's2_w', 's2_b', 'b2_w', 'b2_b', 'm_w1', 'm_b1', 'm_w2', 'm_b2')}
    del _L1_gnn_all

    def _L2_gnn_setup():
        import jax, jax.numpy as jnp
        import numpy as np
        N, E, D = (6250, 100000, 512)
        BN_EPS = 1e-05

        def _batchnorm(h, gamma, beta):
            mu = jnp.mean(h, axis=0)
            var = jnp.var(h, axis=0)
            return (h - mu) * jax.lax.rsqrt(var + BN_EPS) * gamma + beta
        key = jax.random.key(seed)
        ks = jax.random.split(key, 8)
        scale = 1.0 / np.sqrt(D)
        return {'x': jax.random.normal(ks[0], (N, D), dtype=jnp.float32), 'edge_index': jax.random.randint(ks[1], (2, E), 0, N, dtype=jnp.int64), 'eps': jnp.zeros((1,), dtype=jnp.float32), 'W1': jax.random.normal(ks[2], (D, D), dtype=jnp.float32) * scale, 'b1': jnp.zeros((D,), dtype=jnp.float32), 'gamma1': jnp.ones((D,), dtype=jnp.float32), 'beta1': jnp.zeros((D,), dtype=jnp.float32), 'W2': jax.random.normal(ks[3], (D, D), dtype=jnp.float32) * scale, 'b2': jnp.zeros((D,), dtype=jnp.float32), 'gamma2': jnp.ones((D,), dtype=jnp.float32), 'beta2': jnp.zeros((D,), dtype=jnp.float32)}
    _L2_gnn_all = _L2_gnn_setup()
    _L2_gnn_in = {k: v for k, v in _L2_gnn_all.items() if k in ('eps', 'W1', 'b1', 'gamma1', 'beta1', 'W2', 'b2', 'gamma2', 'beta2')}
    del _L2_gnn_all

    def _L3_gnn_setup():
        import jax, jax.numpy as jnp
        import numpy as np
        N, E, H, D_IN, D_PRIME = (6250, 100000, 8, 512, 64)

        def _segment_softmax(scores, seg, num_segments):
            smax = jax.ops.segment_max(scores, seg, num_segments=num_segments)
            ex = jnp.exp(scores - smax[seg])
            denom = jax.ops.segment_sum(ex, seg, num_segments=num_segments)
            return ex / denom[seg]
        key = jax.random.key(seed)
        ks = jax.random.split(key, 6)
        x = jax.random.normal(ks[0], (N, D_IN), dtype=jnp.float32)
        edge_index = jax.random.randint(ks[1], (2, E), 0, N)
        Ws = jax.random.normal(ks[2], (H, D_IN, D_PRIME), dtype=jnp.float32) * 0.05
        Wb = jax.random.normal(ks[3], (H, D_PRIME), dtype=jnp.float32) * 0.05
        a_w = jax.random.normal(ks[4], (H, 2 * D_PRIME), dtype=jnp.float32) * 0.05
        a_b = jax.random.normal(ks[5], (H,), dtype=jnp.float32) * 0.05
        return dict(x=x, edge_index=edge_index, Ws=Ws, Wb=Wb, a_w=a_w, a_b=a_b)
    _L3_gnn_all = _L3_gnn_setup()
    _L3_gnn_in = {k: v for k, v in _L3_gnn_all.items() if k in ('Ws', 'Wb', 'a_w', 'a_b')}
    del _L3_gnn_all
    return {'x': x, 'src': src, 'dst': dst, 'edge_weight': edge_weight, 'node_vec1': node_vec1, 'L0_gnn_W': _L0_gnn_in['W'], 'L1_gnn_f_w1': _L1_gnn_in['f_w1'], 'L1_gnn_f_b1': _L1_gnn_in['f_b1'], 'L1_gnn_f_w2': _L1_gnn_in['f_w2'], 'L1_gnn_f_b2': _L1_gnn_in['f_b2'], 'L1_gnn_s1_w': _L1_gnn_in['s1_w'], 'L1_gnn_s1_b': _L1_gnn_in['s1_b'], 'L1_gnn_b1_w': _L1_gnn_in['b1_w'], 'L1_gnn_b1_b': _L1_gnn_in['b1_b'], 'L1_gnn_wq': _L1_gnn_in['wq'], 'L1_gnn_bq': _L1_gnn_in['bq'], 'L1_gnn_wk': _L1_gnn_in['wk'], 'L1_gnn_bk': _L1_gnn_in['bk'], 'L1_gnn_wv': _L1_gnn_in['wv'], 'L1_gnn_bv': _L1_gnn_in['bv'], 'L1_gnn_wo': _L1_gnn_in['wo'], 'L1_gnn_bo': _L1_gnn_in['bo'], 'L1_gnn_s2_w': _L1_gnn_in['s2_w'], 'L1_gnn_s2_b': _L1_gnn_in['s2_b'], 'L1_gnn_b2_w': _L1_gnn_in['b2_w'], 'L1_gnn_b2_b': _L1_gnn_in['b2_b'], 'L1_gnn_m_w1': _L1_gnn_in['m_w1'], 'L1_gnn_m_b1': _L1_gnn_in['m_b1'], 'L1_gnn_m_w2': _L1_gnn_in['m_w2'], 'L1_gnn_m_b2': _L1_gnn_in['m_b2'], 'L2_gnn_eps': _L2_gnn_in['eps'], 'L2_gnn_W1': _L2_gnn_in['W1'], 'L2_gnn_b1': _L2_gnn_in['b1'], 'L2_gnn_gamma1': _L2_gnn_in['gamma1'], 'L2_gnn_beta1': _L2_gnn_in['beta1'], 'L2_gnn_W2': _L2_gnn_in['W2'], 'L2_gnn_b2': _L2_gnn_in['b2'], 'L2_gnn_gamma2': _L2_gnn_in['gamma2'], 'L2_gnn_beta2': _L2_gnn_in['beta2'], 'L3_gnn_Ws': _L3_gnn_in['Ws'], 'L3_gnn_Wb': _L3_gnn_in['Wb'], 'L3_gnn_a_w': _L3_gnn_in['a_w'], 'L3_gnn_a_b': _L3_gnn_in['a_b']}

def reference(x, src, dst, edge_weight, node_vec1, L0_gnn_W, L1_gnn_f_w1, L1_gnn_f_b1, L1_gnn_f_w2, L1_gnn_f_b2, L1_gnn_s1_w, L1_gnn_s1_b, L1_gnn_b1_w, L1_gnn_b1_b, L1_gnn_wq, L1_gnn_bq, L1_gnn_wk, L1_gnn_bk, L1_gnn_wv, L1_gnn_bv, L1_gnn_wo, L1_gnn_bo, L1_gnn_s2_w, L1_gnn_s2_b, L1_gnn_b2_w, L1_gnn_b2_b, L1_gnn_m_w1, L1_gnn_m_b1, L1_gnn_m_w2, L1_gnn_m_b2, L2_gnn_eps, L2_gnn_W1, L2_gnn_b1, L2_gnn_gamma1, L2_gnn_beta1, L2_gnn_W2, L2_gnn_b2, L2_gnn_gamma2, L2_gnn_beta2, L3_gnn_Ws, L3_gnn_Wb, L3_gnn_a_w, L3_gnn_a_b):
    import jax
    import jax.numpy as jnp

    def _L0_gnn_ref(X, W, edge_src, edge_dst, edge_vals):
        import jax, jax.numpy as jnp
        import numpy as np
        N_NODES = 6250
        N_EDGES = 100000
        M_IN = 512
        H_OUT = 512
        Z = jnp.matmul(X, W)
        msg = Z[edge_src] * edge_vals[:, None]
        agg = jax.ops.segment_sum(msg, edge_dst, num_segments=X.shape[0])
        return jax.nn.relu(agg)

    def _L1_gnn_ref(latent_mesh_nodes, edge_index, noise_levels, f_w1, f_b1, f_w2, f_b2, s1_w, s1_b, b1_w, b1_b, wq, bq, wk, bk, wv, bv, wo, bo, s2_w, s2_b, b2_w, b2_b, m_w1, m_b1, m_w2, m_b2):
        import jax, jax.numpy as jnp
        import numpy as np
        N_NODES = 40962
        LATENT_DIM = 512
        N_EDGES = 81924
        NUM_BLOCKS = 4
        NUM_HEADS = 4
        NUM_FREQ = 32
        BASE_PERIOD = 16
        NOISE_EMB_DIM = 16
        EPS = 1e-05

        def _cond_layer_norm(x, cond, sw, sb, bw, bb):
            mu = jnp.mean(x, axis=-1, keepdims=True)
            var = jnp.var(x, axis=-1, keepdims=True)
            xn = (x - mu) * jax.lax.rsqrt(var + EPS)
            scale = cond @ sw + sb
            bias = cond @ bw + bb
            return xn * (1.0 + scale) + bias

        def _sparse_attention(x, src, dst, wq, bq, wk, bk, wv, bv, wo, bo):
            N, D = x.shape
            H, Dh = (NUM_HEADS, D // NUM_HEADS)
            q = (x @ wq + bq).reshape(N, H, Dh) * Dh ** (-0.5)
            k = (x @ wk + bk).reshape(N, H, Dh)
            v = (x @ wv + bv).reshape(N, H, Dh)
            scores = jnp.einsum('ehd,ehd->eh', q[src], k[dst])
            smax = jax.ops.segment_max(scores, src, num_segments=N)
            ex = jnp.exp(scores - smax[src])
            denom = jax.ops.segment_sum(ex, src, num_segments=N)
            attn = ex / denom[src]
            out = jax.ops.segment_sum(attn[:, :, None] * v[dst], src, num_segments=N)
            return out.reshape(N, D) @ wo + bo

        def _forward(x, edge_index, noise_levels, f_w1, f_b1, f_w2, f_b2, s1_w, s1_b, b1_w, b1_b, wq, bq, wk, bk, wv, bv, wo, bo, s2_w, s2_b, b2_w, b2_b, m_w1, m_b1, m_w2, m_b2):
            src, dst = (edge_index[0], edge_index[1])
            freqs = jnp.arange(1, NUM_FREQ + 1, dtype=x.dtype) * (2.0 * np.pi / BASE_PERIOD)
            ph = noise_levels * freqs
            emb = jnp.concatenate([jnp.sin(ph), jnp.cos(ph)], axis=-1)
            cond = jax.nn.silu(emb @ f_w1 + f_b1) @ f_w2 + f_b2
            for i in range(NUM_BLOCKS):
                y = _cond_layer_norm(x, cond, s1_w[i], s1_b[i], b1_w[i], b1_b[i])
                y = _sparse_attention(y, src, dst, wq[i], bq[i], wk[i], bk[i], wv[i], bv[i], wo[i], bo[i])
                x = x + y
                y = _cond_layer_norm(x, cond, s2_w[i], s2_b[i], b2_w[i], b2_b[i])
                y = jax.nn.relu(y @ m_w1[i] + m_b1[i]) @ m_w2[i] + m_b2[i]
                x = x + y
            return x
        return _forward(latent_mesh_nodes, edge_index, noise_levels, f_w1, f_b1, f_w2, f_b2, s1_w, s1_b, b1_w, b1_b, wq, bq, wk, bk, wv, bv, wo, bo, s2_w, s2_b, b2_w, b2_b, m_w1, m_b1, m_w2, m_b2)

    def _L2_gnn_ref(x, edge_index, eps, W1, b1, gamma1, beta1, W2, b2, gamma2, beta2):
        import jax, jax.numpy as jnp
        import numpy as np
        N, E, D = (6250, 100000, 512)
        BN_EPS = 1e-05

        def _batchnorm(h, gamma, beta):
            mu = jnp.mean(h, axis=0)
            var = jnp.var(h, axis=0)
            return (h - mu) * jax.lax.rsqrt(var + BN_EPS) * gamma + beta
        row, col = (edge_index[0], edge_index[1])
        agg = jax.ops.segment_sum(x[col], row, num_segments=x.shape[0])
        h = (1.0 + eps) * x + agg
        h = _batchnorm(h @ W1 + b1, gamma1, beta1)
        h = jax.nn.relu(h)
        h = _batchnorm(h @ W2 + b2, gamma2, beta2)
        return h

    def _L3_gnn_ref(x, edge_index, Ws, Wb, a_w, a_b):
        import jax, jax.numpy as jnp
        import numpy as np
        N, E, H, D_IN, D_PRIME = (6250, 100000, 8, 512, 64)

        def _segment_softmax(scores, seg, num_segments):
            smax = jax.ops.segment_max(scores, seg, num_segments=num_segments)
            ex = jnp.exp(scores - smax[seg])
            denom = jax.ops.segment_sum(ex, seg, num_segments=num_segments)
            return ex / denom[seg]
        v_src, v_tgt = (edge_index[0], edge_index[1])
        n = x.shape[0]
        outs = []
        for h in range(Ws.shape[0]):
            Wx = x @ Ws[h] + Wb[h]
            d = Wx.shape[-1]
            s = Wx[v_tgt] @ a_w[h, :d] + Wx[v_src] @ a_w[h, d:] + a_b[h]
            s = jax.nn.leaky_relu(s, negative_slope=0.2)
            alpha = _segment_softmax(s, v_tgt, n)
            outs.append(jax.ops.segment_sum(alpha[:, None] * Wx[v_src], v_tgt, num_segments=n))
        return jnp.stack(outs, axis=1).reshape(n, -1)
    edge_index = jnp.stack([src, dst])
    x = _layernorm(x + _L0_gnn_ref(x, L0_gnn_W, src, dst, edge_weight), axis=-1)
    x = _layernorm(x + _L1_gnn_ref(x, edge_index, node_vec1, L1_gnn_f_w1, L1_gnn_f_b1, L1_gnn_f_w2, L1_gnn_f_b2, L1_gnn_s1_w, L1_gnn_s1_b, L1_gnn_b1_w, L1_gnn_b1_b, L1_gnn_wq, L1_gnn_bq, L1_gnn_wk, L1_gnn_bk, L1_gnn_wv, L1_gnn_bv, L1_gnn_wo, L1_gnn_bo, L1_gnn_s2_w, L1_gnn_s2_b, L1_gnn_b2_w, L1_gnn_b2_b, L1_gnn_m_w1, L1_gnn_m_b1, L1_gnn_m_w2, L1_gnn_m_b2), axis=-1)
    x = _layernorm(x + _L2_gnn_ref(x, edge_index, L2_gnn_eps, L2_gnn_W1, L2_gnn_b1, L2_gnn_gamma1, L2_gnn_beta1, L2_gnn_W2, L2_gnn_b2, L2_gnn_gamma2, L2_gnn_beta2), axis=-1)
    x = _layernorm(x + _L3_gnn_ref(x, edge_index, L3_gnn_Ws, L3_gnn_Wb, L3_gnn_a_w, L3_gnn_a_b), axis=-1)
    return x

_drawn_inputs = setup_inputs


def setup_inputs(seed=0):
    import zlib

    import numpy as np

    out = dict(_drawn_inputs(seed))
    spreads = {'L1_gnn_f_b1': (0.0, 0.8),
     'L1_gnn_f_b2': (0.0, 0.8),
     'L1_gnn_s1_b': (0.0, 0.8),
     'L1_gnn_b1_b': (0.0, 0.336),
     'L1_gnn_bq': (0.0, 0.8),
     'L1_gnn_bk': (0.0, 0.8),
     'L1_gnn_bv': (0.0, 0.1),
     'L1_gnn_bo': (0.0, 0.1),
     'L1_gnn_s2_b': (0.0, 0.518),
     'L1_gnn_b2_b': (0.0, 0.503),
     'L1_gnn_m_b1': (0.0, 0.1),
     'L1_gnn_m_b2': (0.0, 0.1),
     'L2_gnn_b1': (0.0, 0.8),
     'L2_gnn_gamma1': (1.0, 0.2),
     'L2_gnn_beta1': (0.0, 0.1),
     'L2_gnn_b2': (0.0, 0.8),
     'L2_gnn_gamma2': (1.0, 0.2),
     'L2_gnn_beta2': (0.0, 0.1)}
    factors = {'node_vec1': 8.0,
     'L1_gnn_f_w1': 8.0,
     'L1_gnn_f_w2': 8.0,
     'L1_gnn_s1_w': 8.0,
     'L1_gnn_b1_w': 8.0,
     'L1_gnn_wq': 5.39,
     'L1_gnn_wk': 5.251,
     'L1_gnn_s2_w': 8.0,
     'L1_gnn_b2_w': 8.0,
     'L3_gnn_a_b': 8.0}
    for name, (base, spread) in spreads.items():
        noise = np.random.default_rng([zlib.crc32(name.encode()), seed]).standard_normal(out[name].shape)
        drawn = base * np.exp(spread * noise) if base else spread * noise
        out[name] = jnp.asarray(drawn.astype(out[name].dtype))
    for name, factor in factors.items():
        out[name] = (out[name] * factor).astype(out[name].dtype)
    return out
```

```python
from contextlib import ExitStack

import numpy as np

import concourse.bass as bass
from concourse import mybir

ALU = mybir.AluOpType
ACT = mybir.ActivationFunctionType
AX = mybir.AxisListType
F32 = mybir.dt.float32
F32R = mybir.dt.float32r
BF16 = mybir.dt.bfloat16
F16 = mybir.dt.float16
I32 = mybir.dt.int32

NODES, DIM, EDGES = 1250, 512, 20000
TILE = 125
TILES = NODES // TILE
ETILES = EDGES // TILE
BAND = 32
BANDS = -(-NODES // BAND)
WIDE = BANDS * BAND
CHUNKS = DIM // 128
BANK = 512
CUTS = [(0, 512), (512, 1024), (1024, NODES)]
MASKED = -1.0e30
EPS = 1e-5
LAYERS1, HEADS1, HDIM1 = 4, 4, 128
COND, FREQS = 16, 32
HEADS3, HDIM3 = 8, 64
SBUF_BASE = 16512


WORK1 = 2 * TILES * WIDE * 4


def packer(nc, start):
    at = [start]

    def place(name, shape, dtype):
        size = int(np.prod(shape[1:])) * (2 if dtype in (BF16, F16) else 4)
        t = nc.alloc_sbuf_tensor_at(name, shape, dtype, offset=SBUF_BASE + at[0])
        at[0] += -(-size // 32) * 32
        return t

    return place


def edge_bands(nc, fx, psum, src, dst, weight, count_rows):
    with ExitStack() as ctx:
        def sem(name):
            return ctx.enter_context(nc.semaphore(name))

        place = packer(nc, WORK1)
        rows_i = place("edge_rows_int", [128, 2, 2, TILE], I32)
        rows_w = place("edge_rows_weight", [128, 2, TILE], F32)
        rows_f = place("edge_rows_float", [128, 3, 2, TILE], F32)
        cols = place("edge_columns", [128, 3, ETILES], F32)
        parts = place("weight_parts", [128, ETILES, 3], BF16)
        rest = place("weight_rest", [128, 2, ETILES], F32)
        ids_i = place("node_ids_int", [128, WIDE], I32)
        ids = place("node_ids", [128, WIDE], F16)
        onehot = place("onehot_source", [128, 2, NODES], BF16)
        station = place("onehot_band", [128, 2, 4, BAND], BF16)
        bands = place("band_products", [128, 2, NODES], F32)
        split = place("band_weight_parts", [128, 2, TILES, 3, BAND], F32)
        pair = place("band_weight_pair", [128, 2, TILES, BAND], F32)
        ext = place("tile_extremes", [128, 2, 2], F32)
        ext_b = place("tile_extremes_spread", [128, 2, 2, BANDS], F32)
        hit = place("band_meets_tile", [128, 3, ETILES], F32)
        band_at = place("band_start", [128, 2], F32)
        band_at_i = place("band_start_int", [128, 1], I32)
        up = place("tile_number_up", [128, 2, ETILES], F32)
        up_i = place("tile_number_int", [128, ETILES], I32)
        span = place("band_span_columns", [128, 4], F32)
        row = place("band_span_rows", [1, 6, BANDS], F32)
        row_i = place("band_span_registers", [1, 3, BANDS], I32)
        count_src, weight_src, ident, ones = fx.count_src, fx.weight_src, fx.ident, fx.ones

        loaded = sem("edges_loaded")
        consts = sem("constants_ready")
        floats = sem("edge_floats_ready")
        turned = sem("edges_turned")
        spread = sem("extremes_spread")
        colsok = sem("edge_columns_ready")
        own = sem("vector_setup_step")
        spanned = sem("spans_turned")
        ready = sem("spans_ready")
        band_half = sem("onehot_band_plain")
        oh_ready = sem("onehots_ready")
        oh_free = sem("onehots_used")
        band_copied = sem("band_copied")
        turn = sem("band_turned")
        unturn = sem("turned_copied")
        summed = sem("weights_summed")
        stored = [sem(f"counts_stored_{s}") for s in range(2)]

        def region(s):
            return psum[:, s * 3 * BANK:s * 3 * BANK + NODES]

        def unit(v):
            return psum[:, (6 + v % 2) * BANK:(7 + v % 2) * BANK]

        def span_of(eng, b):
            begin = eng.value_load(row_i[0:1, 0, bass.ds(b, 1)], min_val=0, max_val=BANDS * ETILES)
            end = eng.value_load(row_i[0:1, 1, bass.ds(b, 1)], min_val=2, max_val=BANDS * ETILES)
            skew = eng.value_load(row_i[0:1, 2, bass.ds(b, 1)], min_val=0, max_val=(BANDS + 1) * ETILES)
            return begin, end, skew

        block = ctx.enter_context(nc.Block())

        @block.sync
        def _(sp):
            for a, v in enumerate((src, dst)):
                r = v.rearrange("(t e) -> t e", e=TILE)
                sp.dma_start(rows_i[:, a, 0, :], r[0:128, :]).then_inc(loaded, 16)
                sp.dma_start(rows_i[0:32, a, 1, :], r[128:ETILES, :]).then_inc(loaded, 16)
            r = weight.rearrange("(t e) -> t e", e=TILE)
            sp.dma_start(rows_w[:, 0, :], r[0:128, :]).then_inc(loaded, 16)
            sp.dma_start(rows_w[0:32, 1, :], r[128:ETILES, :]).then_inc(loaded, 16)

            def store(i):
                for s in range(2):
                    b = 2 * i + s
                    sp.wait_ge(band_copied, b + 1)
                    sp.dma_start(count_rows[bass.ds(b * BAND, BAND), :], bands[0:BAND, s, :]).then_inc(stored[s], 16)

            with sp.Fori(0, BANDS // 2) as i:
                store(i)
            for s in range(2):
                sp.wait_ge(stored[s], 16 * (BANDS // 2))

        @block.gpsimd
        def _(pool):
            pool.memset(ident[:, :], 0.0).then_inc(consts, 1)
            pool.wait_ge(consts, 1)
            pool.affine_select(out=ident[:, :], in_=ident[:, :], compare_op=ALU.not_equal, fill=1.0,
                               base=0, pattern=[[-1, 128]], channel_multiplier=1).then_inc(consts, 1)
            pool.memset(ones[:, :], 1.0).then_inc(consts, 1)
            pool.iota(ids_i[:, :], [[1, WIDE]], base=0, channel_multiplier=0).then_inc(consts, 1)
            pool.iota(band_at_i[:, :], [[0, 1]], base=0, channel_multiplier=BAND).then_inc(consts, 1)
            pool.iota(up_i[:, :], [[1, ETILES]], base=0, channel_multiplier=0).then_inc(consts, 1)

            def sums(i, first):
                for s in range(2):
                    b = 2 * i + s
                    pool.wait_ge(unturn, 6 * i + 3 * s + 3)
                    nc.gpsimd.tensor_tensor(pair[0:TILE, s], split[0:TILE, s, :, 0, :], split[0:TILE, s, :, 1, :],
                                            ALU.add).then_inc(summed, 1)
                    pool.wait_ge(summed, 2 * b + 1)
                    nc.gpsimd.tensor_tensor(weight_src[0:TILE, :, bass.ds(b * BAND, BAND)], pair[0:TILE, s],
                                            split[0:TILE, s, :, 2, :], ALU.add).then_inc(summed, 1)

            sums(0, True)
            with pool.Fori(1, BANDS // 2) as i:
                sums(i, False)

        @block.vector
        def _(dve):
            steps = [0]

            def step(ins):
                steps[0] += 1
                ins.then_inc(own, 1)
                dve.wait_ge(own, steps[0])

            v = nc.vector
            dve.wait_ge(loaded, 96)
            for a in range(3):
                for c, n in ((0, 128), (1, 32)):
                    src_rows = rows_i[0:n, a, c, :] if a < 2 else rows_w[0:n, c, :]
                    v.tensor_copy(rows_f[0:n, a, c, :], src_rows).then_inc(floats, 1)
            dve.wait_ge(floats, 6)
            for c, n in ((0, 128), (1, 32)):
                for e, op in ((0, ALU.min), (1, ALU.max)):
                    step(v.tensor_reduce(ext[0:n, e, c:c + 1], rows_f[0:n, 1, c, :], AX.X, op))
            dve.wait_ge(consts, 6)
            for c, n in ((0, 128), (1, 32)):
                for e in range(2):
                    v.tensor_scalar(ext_b[0:n, e, c, :], ones[0:n, 0:BANDS], ext[0:n, e, c:c + 1], None,
                                    ALU.mult).then_inc(spread, 1)
            v.tensor_copy(ids[:, :], ids_i[:, :])
            step(v.tensor_copy(band_at[:, 0:1], band_at_i[:, :]))
            v.tensor_scalar(band_at[:, 1:2], band_at[:, 0:1], float(BAND - 1), None, ALU.add)
            v.tensor_scalar(up[:, 0, :], up_i[:, :], 1.0, None, ALU.add)
            step(v.tensor_scalar(up[:, 1, :], up_i[:, :], -1.0, float(ETILES), ALU.mult, ALU.add))
            dve.wait_ge(turned, 6)
            for a in range(3):
                step(v.tensor_copy(cols[0:TILE, a, :], psum[0:TILE, a * BANK:a * BANK + ETILES]))
            w, r = cols[0:TILE, 2, :], rest[0:TILE]
            step(v.tensor_copy(parts[0:TILE, :, 0], w))
            step(v.tensor_tensor(r[:, 0, :], w, parts[0:TILE, :, 0], ALU.subtract))
            step(v.tensor_copy(parts[0:TILE, :, 1], r[:, 0, :]))
            step(v.tensor_tensor(r[:, 1, :], r[:, 0, :], parts[0:TILE, :, 1], ALU.subtract))
            step(v.tensor_copy(parts[0:TILE, :, 2], r[:, 1, :]))
            dve.wait_ge(spread, 8)
            low = psum[0:BANDS, 3 * BANK:3 * BANK + ETILES]
            high = psum[0:BANDS, 4 * BANK:4 * BANK + ETILES]
            h = hit[0:BANDS]
            step(v.tensor_scalar(h[:, 0, :], high, band_at[0:BANDS, 0:1], None, ALU.is_ge))
            step(v.scalar_tensor_tensor(h[:, 1, :], low, band_at[0:BANDS, 1:2], h[:, 0, :], ALU.is_le, ALU.mult))
            step(v.tensor_tensor(h[:, 0, :], h[:, 1, :], up[0:BANDS, 1, :], ALU.mult))
            step(v.tensor_tensor(h[:, 2, :], h[:, 1, :], up[0:BANDS, 0, :], ALU.mult))
            step(v.tensor_reduce(span[0:BANDS, 2:3], h[:, 0, :], AX.X, ALU.max))
            step(v.tensor_reduce(span[0:BANDS, 3:4], h[:, 2, :], AX.X, ALU.max))
            step(v.tensor_scalar(span[0:BANDS, 2:3], span[0:BANDS, 2:3], -1.0, float(ETILES), ALU.mult, ALU.add))
            step(v.tensor_scalar(span[0:BANDS, 0:1], span[0:BANDS, 2:3], float(ETILES - 2), None, ALU.min))
            step(v.tensor_scalar(span[0:BANDS, 2:3], span[0:BANDS, 0:1], 2.0, None, ALU.add))
            v.tensor_tensor(span[0:BANDS, 1:2], span[0:BANDS, 2:3], span[0:BANDS, 3:4], ALU.max).then_inc(spanned, 1)
            dve.wait_ge(spanned, 3)
            for k in range(2):
                step(v.tensor_copy(row[0:1, k, :], psum[0:1, 5 * BANK + 64 * k:5 * BANK + 64 * k + BANDS]))
            step(v.tensor_tensor(row[0:1, 2, :], row[0:1, 1, :], row[0:1, 0, :], ALU.subtract))
            step(v.memset(row[0:1, 3, :], 1.0))
            step(v.tensor_tensor_scan(row[0:1, 4, :], row[0:1, 3, :], row[0:1, 2, :], 0.0, ALU.mult, ALU.add))
            step(v.tensor_tensor(row[0:1, 5, :], row[0:1, 4, :], row[0:1, 2, :], ALU.subtract))
            step(v.tensor_tensor(row[0:1, 2, :], row[0:1, 5, :], row[0:1, 0, :], ALU.subtract))
            step(v.tensor_scalar(row[0:1, 2, :], row[0:1, 2, :], float(ETILES), None, ALU.add))
            step(v.tensor_copy(row_i[0:1, 0, :], row[0:1, 5, :]))
            step(v.tensor_copy(row_i[0:1, 1, :], row[0:1, 4, :]))
            step(v.tensor_copy(row_i[0:1, 2, :], row[0:1, 2, :]))
            v.memset(row[0:1, 3, :], 1.0).then_inc(ready, 1)

            def tiles(i):
                for s in range(2):
                    b = 2 * i + s
                    begin, end, skew = span_of(dve, b)
                    with dve.Fori(begin, end) as n:
                        nth, at = n + 1, n % 2
                        t = nc.s_assert_within(n + ETILES - skew, 0, ETILES - 1,
                                               skip_runtime_bounds_check_because="n runs over the tiles of the band")
                        dve.wait_ge(oh_free, nth)
                        v.tensor_scalar(station[0:TILE, bass.ds(at, 1), 0, :], ids[0:TILE, bass.ds(b * BAND, BAND)],
                                        cols[0:TILE, 1, bass.ds(t, 1)], None, ALU.is_equal).then_inc(band_half, 1)
                        v.tensor_scalar(onehot[0:TILE, bass.ds(at, 1), :], ids[0:TILE, 0:NODES],
                                        cols[0:TILE, 0, bass.ds(t, 1)], None, ALU.is_equal).then_inc(oh_ready, 1)
                        dve.wait_ge(band_half, nth)
                        v.tensor_tensor(
                            station[0:TILE, bass.ds(at, 1), 1:4, :].rearrange("p a k j -> p (a k) j"),
                            station[0:TILE, bass.ds(at, 1), 0, :].broadcast_to([TILE, 3, BAND]),
                            parts[0:TILE, bass.ds(t, 1), :].rearrange("p a k -> p (a k)").unsqueeze(2).broadcast_to([TILE, 3, BAND]),
                            ALU.mult).then_inc(oh_ready, 1)

            with dve.Fori(0, BANDS // 2) as i:
                tiles(i)

        @block.tensor
        def _(pe):
            pe.wait_ge(consts, 3)
            pe.wait_ge(floats, 6)
            for a in range(3):
                pe.transpose(psum[0:TILE, a * BANK:a * BANK + 128], rows_f[:, a, 0, :], ident[:, :]).then_inc(turned, 1)
                pe.transpose(psum[0:TILE, a * BANK + 128:a * BANK + ETILES], rows_f[0:32, a, 1, :],
                             ident[0:32, 0:32]).then_inc(turned, 1)
            pe.wait_ge(spread, 4)
            for e in range(2):
                for c, n in ((0, 128), (1, 32)):
                    pe.matmul(psum[0:BANDS, (3 + e) * BANK + 128 * c:(3 + e) * BANK + 128 * c + n], ext_b[0:n, e, c, :],
                              ident[0:n, 0:n], start=True, stop=True).then_inc(spread, 1)
            pe.wait_ge(spanned, 1)
            for k in range(2):
                mm = pe.matmul(psum[0:1, 5 * BANK + 64 * k:5 * BANK + 64 * k + BANDS], span[0:BANDS, k:k + 1],
                               ident[0:BANDS, 0:BANDS], start=True, stop=True)
                mm.then_inc(spanned, 1)
            pe.wait_ge(ready, 1)
            pe.wait_ge(oh_free, 2)

            def product(s, at, start):
                for a, z in CUTS:
                    mm = pe.matmul(region(s)[:, a:z], station[0:TILE, bass.ds(at, 1), :, :].rearrange("p a k j -> p (a k j)"),
                                   onehot[0:TILE, bass.ds(at, 1), a:z], start=start, stop=True, skip_group_check=True)
                mm.then_inc(oh_free, 1)

            def both(i, first_pair):
                for s in range(2):
                    begin, end, _ = span_of(pe, 2 * i + s)
                    pe.wait_ge(oh_ready, 2 * begin + 2)
                    product(s, begin % 2, True)
                    with pe.Fori(begin + 1, end) as n:
                        pe.wait_ge(oh_ready, 2 * n + 2)
                        product(s, n % 2, False)
                for s in range(2):
                    pe.wait_ge(band_copied, 2 * i + s + 1)
                    for u in range(3):
                        v = 3 * s + u
                        if v >= 2 or not first_pair:
                            pe.wait_ge(unturn, 6 * i + v - 1)
                        for j in range(4 * u, min(4 * u + 4, TILES)):
                            mm = pe.transpose(unit(v)[0:TILE, (j % 4) * 128:(j % 4) * 128 + 128],
                                              bands[:, s, j * TILE:(j + 1) * TILE], ident[:, :])
                        mm.then_inc(turn, 1)

            both(0, True)
            with pe.Fori(1, BANDS // 2) as i:
                both(i, False)

        @block.scalar
        def _(act):
            act.wait_ge(consts, 3)
            for k in range(2):
                nc.scalar.activation(bands[0:1, k, 0:1], ones[0:1, 0:1], ACT.Copy).then_inc(oh_free, 1)
            act.wait_ge(ready, 1)

            def pair_of(i, first_pair):
                for s in range(2):
                    b = 2 * i + s
                    _, end, _ = span_of(act, b)
                    if not first_pair:
                        act.wait_ge(stored[s], 16 * i)
                        act.wait_ge(turn, 6 * i - 3 + 3 * s)
                    act.wait_ge(oh_free, end + 2)
                    nc.scalar.activation(bands[:, s, :], region(s), ACT.Copy).then_inc(band_copied, 1)
                for s in range(2):
                    b = 2 * i + s
                    if not first_pair:
                        act.wait_ge(summed, 4 * i - 2 + 2 * s)
                    for u in range(3):
                        v = 3 * s + u
                        act.wait_ge(turn, 6 * i + v + 1)
                        n = min(4, TILES - 4 * u)
                        view = unit(v)[0:TILE, 0:n * 128].rearrange("p (j k d) -> p j k d", k=4, d=BAND)
                        nc.scalar.activation(count_src[0:TILE, 4 * u:4 * u + n, bass.ds(b * BAND, BAND)], view[:, :, 0, :],
                                             ACT.Copy)
                        nc.scalar.activation(split[0:TILE, s, 4 * u:4 * u + n, :, :], view[:, :, 1:4, :],
                                             ACT.Copy).then_inc(unturn, 1)

            pair_of(0, True)
            with act.Fori(1, BANDS // 2) as i:
                pair_of(i, False)


PLANE = CHUNKS * NODES * 4
LOGS_AT = 0
TURNED_AT = LOGS_AT + TILES * WIDE * 4
SLOT_A_AT = TURNED_AT + 2 * PLANE
SLOT_B_AT = SLOT_A_AT + PLANE
VALUES_AT = SLOT_B_AT + 4 * 5024
WORK_AT = VALUES_AT + TILES * DIM * 4
WORK_SIZE = 33280
HEADW_AT = WORK_AT + WORK_SIZE
CONDS_AT = HEADW_AT + 8192
FIXED_AT = CONDS_AT + 5024 + 4096 + 4096 + 4096
ROW_TAIL = 2 * CHUNKS * DIM * 4
PI = float(np.pi)


class Fixed:

    def __init__(self, nc):
        place = packer(nc, FIXED_AT)
        self.passed = nc.alloc_semaphore("waits_passed")
        self.ident = place("identity", [128, 128], F32)
        self.ones = place("all_ones", [128, 128], F32)
        self.eps = place("norm_eps", [128, 1], F32)
        self.tiny = place("log_floor", [128, 1], F32)
        self.stats = place("norm_stats", [128, 2, 6], F32)
        self.moments = place("norm_moments", [128, 2, 2], F32)
        self.std = place("norm_std", [128, 2], F32)
        self.rstd = place("norm_rstd", [128, 2], F32)
        self.qkb = place("head_biases", [128, 3, LAYERS1 * HEADS1], F32)
        self.peak = place("row_peaks", [128, 2, 2], F32)
        self.mass = place("row_masses", [128, TILES, 3], F32)
        self.nodes = packer(nc, WORK_AT)("nodes", [128, TILES, DIM], F32)
        self.count_src = packer(nc, LOGS_AT)("counts", [128, TILES, WIDE], F32)
        self.weight_src = packer(nc, TURNED_AT)("weights", [128, TILES, WIDE], F32)
        self.cond = packer(nc, CONDS_AT)("condition_parts", [96, NODES], F32R)


def wait_apart(eng, fx, sem, value):
    eng.wait_ge(sem, value)
    eng.sem_inc(fx.passed, 1)


def norm_stats(dve, fx, at, rows, own, own_value, var_ready):
    dve.bn_stats(fx.stats[0:TILE, at, :], rows).then_inc(own, 1)
    wait_apart(dve, fx, own, own_value)
    dve.bn_aggr(fx.moments[0:TILE, at, :], fx.stats[0:TILE, at, :]).then_inc(var_ready, 1)


def norm_std(nc, fx, at, std_ready):
    nc.scalar.activation(fx.std[0:TILE, at:at + 1], fx.moments[0:TILE, at, 1:2], ACT.Sqrt,
                         bias=fx.eps[0:TILE, :]).then_inc(std_ready, 1)


def norm_rows(dve, fx, at, out, rows, own, own_value):
    dve.reciprocal(fx.rstd[0:TILE, at:at + 1], fx.std[0:TILE, at:at + 1]).then_inc(own, 1)
    dve.wait_ge(own, own_value)
    return dve.tensor_scalar(out, rows, fx.moments[0:TILE, at, 0:1], fx.rstd[0:TILE, at:at + 1],
                             ALU.subtract, ALU.mult)


def log_counts(dve, counts, logs, scale, ready, own, steps):
    steps[0] += 1
    dve.tensor_scalar(logs, logs, scale, None, ALU.mult).then_inc(own, 1)
    dve.wait_ge(own, steps[0])
    steps[0] += 1
    dve.tensor_scalar(counts, counts, 0.0, MASKED, ALU.is_equal, ALU.mult).then_inc(own, 1)
    dve.wait_ge(own, steps[0])
    dve.tensor_tensor(counts, counts, logs, ALU.add).then_inc(ready, 1)


def first_layer(nc, fx, psum, x, w0, noise, f_w1, f_b1, f_w2, f_b2, bq, bk, b1, kept):
    with ExitStack() as ctx:
        def sem(name):
            return ctx.enter_context(nc.semaphore(name))

        place = packer(nc, TURNED_AT + TILES * WIDE * 4)
        sum_t = place("edge_sums_turned", [128, CHUNKS, NODES], F32)
        w_sb = place("first_weight", [128, CHUNKS, DIM], F32)
        place = packer(nc, VALUES_AT)
        phase = place("noise_phase", [2 * FREQS, NODES], F32)
        turns = place("noise_turns", [2 * FREQS, NODES], F32)
        inner = place("condition_inner", [COND, NODES], F32)
        plain = place("condition_plain", [96, NODES], F32)
        logs = packer(nc, WORK_AT + TILES * DIM * 4)("plain_logs", [128, 2, NODES], F32)
        place = packer(nc, HEADW_AT)
        fw1 = place("noise_weight_1", [2 * FREQS, COND], F32)
        fw2 = place("noise_weight_2", [COND, 96], F32)
        fb1 = place("noise_bias_1", [COND, 1], F32)
        fb2 = place("noise_bias_2", [96, 1], F32)
        lane_i = place("lane_number_int", [2 * FREQS, 1], I32)
        lane = place("lane_number", [2 * FREQS, 4], F32)

        loaded = sem("x_loaded")
        w_loaded = sem("first_weight_loaded")
        n_loaded = sem("noise_loaded")
        zeroed = sem("noise_buffers_set")
        small = sem("biases_loaded")
        own = sem("noise_step")
        emb_ready = sem("embedding_ready")
        inner_prod = sem("inner_product")
        inner_ready = sem("inner_ready")
        cond_prod = sem("condition_product")
        cond_ready = sem("condition_plain_ready")
        log_plain = sem("logs_plain")
        log_ready = sem("logs_ready")
        sums = sem("edge_sums")
        sums_ready = sem("edge_sums_copied")
        prod = sem("first_products")
        added = sem("relu_added")
        stat_own = sem("stats_step")
        var_ready = sem("variance_ready")
        std_ready = sem("std_ready")
        rstd_own = sem("rstd_step")
        normed = sem("nodes_normed")
        stored = sem("nodes_kept")

        block = ctx.enter_context(nc.Block())

        @block.sync
        def _(sp):
            xr = x.rearrange("(t p) d -> p t d", p=TILE)
            sp.dma_start(fx.nodes[0:TILE], xr).then_inc(loaded, 16)
            sp.wait_ge(zeroed, 2)
            sp.dma_start(phase[:, :], noise.rearrange("n a -> a n").broadcast_to([2 * FREQS, NODES])).then_inc(n_loaded, 16)
            sp.dma_start(fw1[:, :], f_w1).then_inc(n_loaded, 16)
            sp.dma_start(fb1[:, :], f_b1.rearrange("(p a) -> p a", a=1)).then_inc(n_loaded, 16)
            for g in range(3):
                sp.dma_start(fw2[:, 32 * g:32 * g + COND], f_w2).then_inc(n_loaded, 16)
                sp.dma_start(fb2[32 * g:32 * g + COND, :], f_b2.rearrange("(p a) -> p a", a=1)).then_inc(n_loaded, 16)
            sp.dma_start(w_sb[:, :, :], w0.rearrange("(c p) n -> p c n", p=128)).then_inc(w_loaded, 16)
            for k, v in enumerate((bq, bk, b1)):
                sp.dma_start(fx.qkb[:, k, :], v.rearrange("i (c p) -> p (i c)", p=128),
                             allow_slow_non_contiguous=True).then_inc(small, 16)
            sp.wait_ge(normed, TILES)
            sp.dma_start(kept.rearrange("(t p) d -> p t d", p=TILE), fx.nodes[0:TILE]).then_inc(stored, 16)
            sp.wait_ge(small, 48)
            sp.wait_ge(stored, 16)

        @block.gpsimd
        def _(pool):
            pool.memset(fw2[:, :], 0.0).then_inc(zeroed, 1)
            pool.memset(fb2[:, :], 1.0).then_inc(zeroed, 1)
            pool.memset(fx.eps[:, :], EPS).then_inc(zeroed, 1)
            pool.memset(fx.tiny[:, :], 2.0 ** -60).then_inc(zeroed, 1)
            pool.iota(lane_i[:, :], [[0, 1]], base=0, channel_multiplier=1).then_inc(zeroed, 1)

        @block.vector
        def _(dve):
            steps = [0]

            def step(ins):
                steps[0] += 1
                ins.then_inc(own, 1)
                dve.wait_ge(own, steps[0])

            dve.wait_ge(zeroed, 5)
            step(dve.tensor_copy(lane[:, 3:4], lane_i[:, :]))
            rate = 2.0 * PI / 16.0
            dve.tensor_scalar(lane[0:FREQS, 0:1], lane[0:FREQS, 3:4], 1.0, rate, ALU.add, ALU.mult)
            dve.tensor_scalar(lane[FREQS:, 0:1], lane[FREQS:, 3:4], 1.0 - FREQS, rate, ALU.add, ALU.mult)
            dve.memset(lane[0:FREQS, 1:2], 0.0)
            dve.memset(lane[FREQS:, 1:2], 0.25)
            dve.memset(lane[0:FREQS, 2:3], 0.0)
            step(dve.memset(lane[FREQS:, 2:3], PI / 2))
            dve.wait_ge(n_loaded, 144)
            step(dve.tensor_scalar(phase[:, :], phase[:, :], lane[:, 0:1], None, ALU.mult))
            step(dve.tensor_scalar(turns[:, :], phase[:, :], 0.5 / PI, lane[:, 1:2], ALU.mult, ALU.add))
            step(dve.tensor_scalar(turns[:, :], turns[:, :], 12582912.0, None, ALU.add))
            step(dve.tensor_scalar(turns[:, :], turns[:, :], -12582912.0, None, ALU.add))
            step(dve.scalar_tensor_tensor(phase[:, :], turns[:, :], -6.28125, phase[:, :], ALU.mult, ALU.add))
            step(dve.scalar_tensor_tensor(phase[:, :], turns[:, :], -(2 * PI - 6.28125), phase[:, :], ALU.mult, ALU.add))
            step(dve.tensor_scalar(phase[:, :], phase[:, :], lane[:, 2:3], 3.1415925, ALU.add, ALU.min))
            dve.tensor_scalar(phase[:, :], phase[:, :], -3.1415925, None, ALU.max).then_inc(emb_ready, 1)
            dve.wait_ge(cond_ready, 1)
            step(dve.tensor_copy(fx.cond[:, :], plain[:, :]))
            step(dve.tensor_tensor(fx.cond[64:96, :], plain[64:96, :], fx.cond[64:96, :].bitcast(F32), ALU.subtract))
            for t in range(TILES):
                counts = fx.count_src[0:TILE, t, 0:NODES]
                dve.wait_ge(log_plain, t + 1)
                log_counts(dve, counts, logs[0:TILE, t % 2, :], HDIM1 ** 0.5, log_ready, own, steps)

            dve.wait_ge(loaded, 16)
            for i in range(TILES + 1):
                if i < TILES:
                    row = fx.nodes[0:TILE, i, :]
                    dve.wait_ge(prod, i + 1)
                    dve.scalar_tensor_tensor(row, psum[0:TILE, (6 + i % 2) * BANK:(7 + i % 2) * BANK], 0.0, row,
                                             ALU.max, ALU.add).then_inc(added, 1)
                    dve.wait_ge(added, i + 1)
                    norm_stats(dve, fx, i % 2, row, stat_own, i + 1, var_ready)
                if i >= 1:
                    row = fx.nodes[0:TILE, i - 1, :]
                    dve.wait_ge(std_ready, i)
                    norm_rows(dve, fx, (i - 1) % 2, row, row, rstd_own, i).then_inc(normed, 1)

        @block.scalar
        def _(act):
            act.wait_ge(emb_ready, 1)
            nc.scalar.activation(turns[:, :], phase[:, :], ACT.Sin).then_inc(emb_ready, 1)
            act.wait_ge(inner_prod, 1)
            nc.scalar.activation(inner[:, :], psum[0:COND, 3 * BANK:3 * BANK + NODES], ACT.Silu,
                                 bias=fb1[:, :]).then_inc(inner_ready, 1)
            act.wait_ge(cond_prod, 1)
            nc.scalar.activation(plain[:, :], psum[0:96, 0:NODES], ACT.Identity, bias=fb2[:, :]).then_inc(cond_ready, 1)
            for t in range(TILES):
                if t >= 2:
                    act.wait_ge(log_ready, t - 1)
                nc.scalar.activation(logs[0:TILE, t % 2, :], fx.count_src[0:TILE, t, 0:NODES], ACT.Ln,
                                     bias=fx.tiny[0:TILE, :]).then_inc(log_plain, 1)
            for c in range(CHUNKS):
                act.wait_ge(sums, c + 1)
                nc.scalar.activation(sum_t[:, c, :], psum[:, (c % 2) * 3 * BANK:(c % 2) * 3 * BANK + NODES],
                                     ACT.Copy).then_inc(sums_ready, 1)
            for t in range(TILES):
                act.wait_ge(var_ready, t + 1)
                norm_std(nc, fx, t % 2, std_ready)

        @block.tensor
        def _(pe):
            pe.wait_ge(n_loaded, 144)
            pe.wait_ge(emb_ready, 2)
            for a, z in CUTS:
                mm = pe.matmul(psum[0:COND, 3 * BANK + a:3 * BANK + z], fw1[:, :], turns[:, a:z], start=True, stop=True)
            mm.then_inc(inner_prod, 1)
            pe.wait_ge(inner_ready, 1)
            for a, z in CUTS:
                mm = pe.matmul(psum[0:96, a:z], fw2[:, :], inner[:, a:z], start=True, stop=True)
            mm.then_inc(cond_prod, 1)
            pe.wait_ge(loaded, 16)
            pe.wait_ge(cond_ready, 1)
            for c in range(CHUNKS):
                if c >= 2:
                    pe.wait_ge(sums_ready, c - 1)
                for k in range(TILES):
                    for a, z in CUTS:
                        mm = pe.matmul(psum[:, (c % 2) * 3 * BANK + a:(c % 2) * 3 * BANK + z],
                                       fx.nodes[0:TILE, k, c * 128:(c + 1) * 128], fx.weight_src[0:TILE, k, a:z],
                                       start=(k == 0), stop=(k == TILES - 1))
                mm.then_inc(sums, 1)
            pe.wait_ge(w_loaded, 16)
            pe.wait_ge(sums_ready, CHUNKS)
            for t in range(TILES):
                if t >= 2:
                    pe.wait_ge(added, t - 1)
                for c in range(CHUNKS):
                    mm = pe.matmul(psum[0:TILE, (6 + t % 2) * BANK:(7 + t % 2) * BANK],
                                   sum_t[:, c, t * TILE:(t + 1) * TILE], w_sb[:, c, :], start=(c == 0), stop=(c == CHUNKS - 1))
                mm.then_inc(prod, 1)




def three(pe, out, left, right, first, last):
    (lh, ll), (rh, rl) = left, right
    pe.matmul(out, lh, rh, start=first, stop=False, skip_group_check=True)
    pe.matmul(out, lh, rl, start=False, stop=False, skip_group_check=True)
    return pe.matmul(out, ll, rh, start=False, stop=last, skip_group_check=True)


def second_layer(nc, fx, psum, spill, wq, wk, wv, wo, m1, m2, bv, bo, b2, s1, sb1, t1, tb1, s2, sb2, t2, tb2):
    with ExitStack() as ctx:
        def sem(name):
            return ctx.enter_context(nc.semaphore(name))

        place = packer(nc, TURNED_AT)
        y_h = place("turned_high", [128, CHUNKS, NODES], F32R)
        y_l = place("turned_low", [128, CHUNKS, NODES], F32R)
        place = packer(nc, SLOT_A_AT)
        wa = [place(f"slot_a_{p}", [128, CHUNKS, DIM], F32R) for p in ("high", "low")]
        row_a = place("slot_a_bias_row", [128, DIM], F32)
        attended = packer(nc, SLOT_A_AT)("attended_turned", [128, HEADS1, NODES], F32)
        place = packer(nc, SLOT_B_AT)
        wb = [place(f"slot_b_{p}", [128, CHUNKS, DIM], F32R) for p in ("high", "low")]
        row_b = place("slot_b_bias_row", [128, DIM], F32)
        place = packer(nc, SLOT_B_AT)
        qk = [[place(f"{w}_{p}", [128, NODES], F32R) for p in ("high", "low")] for w in ("queries", "keys")]
        place = packer(nc, VALUES_AT)
        v_h = place("values_high", [128, TILES, DIM], BF16)
        v_l = place("values_low", [128, TILES, DIM], BF16)
        hidden = packer(nc, VALUES_AT)("hidden_rows", [128, 2, CHUNKS, 250], F32)
        place = packer(nc, WORK_AT + TILES * DIM * 4)
        xn = place("normed_rows", [128, 2, DIM], F32)
        yr = place("conditioned_rows", [128, 2, DIM], F32)
        vf = place("value_rows", [128, 2, DIM], F32)
        place = packer(nc, WORK_AT)
        prob = place("probabilities", [128, 2, NODES], F32)
        pt_h = place("turned_probabilities_high", [128, 2, TILES, 250], BF16)
        pt_l = place("turned_probabilities_low", [128, 2, TILES, 250], BF16)
        mass_rows = place("inverse_mass_rows", [128, 2, 250], F32)
        mass_diag = place("inverse_mass_diagonal", [128, 2, TILE], F32)
        hw = packer(nc, HEADW_AT)("head_weights", [128, 2, 2, CHUNKS, HDIM1], F32R)
        place = packer(nc, CONDS_AT + 5024)
        sw = place("condition_weight_parts", [96, 2, DIM], F32R)
        raw = place("condition_weights", [32, 2, DIM], F32)
        stage = place("weight_stage", [128, 2, DIM], F32)
        pair_y = (y_h, y_l)

        def sem(name):
            return ctx.enter_context(nc.semaphore("L1_" + name))

        raw_loaded = sem("raw_loaded")
        conds_ready = sem("conds_ready")
        cond_own = sem("cond_own")
        stage_w0 = sem("stage_w0")
        stage_w1 = sem("stage_w1")
        split_high = sem("split_high")
        w_ready = sem("w_ready")
        bv_loaded = sem("bv_loaded")
        bo_loaded = sem("bo_loaded")
        b2_loaded = sem("b2_loaded")
        x_spilled = sem("x_spilled")
        x_back = sem("x_back")
        mod_ready = sem("mod_ready")
        stats_own = sem("stats_own")
        var_ready = sem("var_ready")
        std_ready = sem("std_ready")
        finish_own = sem("finish_own")
        y_ready = sem("y_ready")
        y_turned = sem("y_turned")
        y_high = sem("y_high")
        y_low = sem("y_low")
        v_prod = sem("v_prod")
        v_sum = sem("v_sum")
        v_high = sem("v_high")
        v_low = sem("v_low")
        proj_prod = sem("proj_prod")
        proj_high = sem("proj_high")
        proj_low = sem("proj_low")
        qk_done = sem("qk_done")
        scored = sem("scored")
        peaked = sem("peaked")
        exped = sem("exped")
        mass_own = sem("mass_own")
        inverted = sem("inverted")
        diagonal = sem("diagonal")
        rows_prod = sem("rows_prod")
        rows_copied = sem("rows_copied")
        turned = sem("turned")
        pt_high = sem("pt_high")
        pt_low = sem("pt_low")
        pv_done = sem("pv_done")
        o_done = sem("o_done")
        att_high = sem("att_high")
        att_low = sem("att_low")
        o_prod = sem("o_prod")
        x_biased = sem("x_biased")
        residual = sem("residual")
        h_prod = sem("h_prod")
        h_rows = sem("h_rows")
        h_high = sem("h_high")
        h_low = sem("h_low")
        m_prod = sem("m_prod")
        x_done = sem("x_done")
        x2_biased = sem("x2_biased")
        stage_loaded = [stage_w0, stage_w1]
        GROUPS = TILES // 2
        LAG_STEPS = TILES + 3

        def bank(n):
            return psum[:, n * BANK:(n + 1) * BANK]

        def cols(t):
            return slice(t * TILE, (t + 1) * TILE)

        def unit_views(source, pt, u, j):
            n = min(4, TILES - 4 * u)
            return (source[0:TILE, 0:n * TILE].rearrange("p (d n) -> p d n", d=n),
                    pt[0:TILE, (j // 2) % 2, 4 * u:4 * u + n, cols(j % 2)])

        def row_scores(dve, scores, i, T, scale):
            p = fx.peak[0:TILE, i % 2]
            dve.tensor_tensor_reduce(prob[0:TILE, i % 2, :], scores, fx.count_src[0:TILE, i, 0:NODES], scale, MASKED,
                                     ALU.add, ALU.max, p[:, 0:1]).then_inc(scored, 1)
            dve.wait_ge(scored, T + 1)
            dve.tensor_scalar(p[:, 1:2], p[:, 0:1], MASKED * 1e-5, -1.0, ALU.max, ALU.mult).then_inc(peaked, 1)

        def row_mass(dve, i, T):
            m = fx.mass[0:TILE, i]
            dve.wait_ge(exped, T + 1)
            dve.tensor_scalar(m[:, 1:2], m[:, 0:1], 1e-30, None, ALU.max).then_inc(mass_own, 1)
            dve.wait_ge(mass_own, T + 1)
            dve.reciprocal(m[:, 2:3], m[:, 1:2]).then_inc(inverted, 1)

        block = ctx.enter_context(nc.Block())

        @block.sync
        def _(sp):
            def weight(b, i, src):
                sp.wait_ge(w_ready, 24 * b + i + 1)
                sp.dma_start(stage[:, i % 2, :] if len(src.shape) == 2 else
                             stage[:, i % 2, :].rearrange("p (c n) -> p c n", c=CHUNKS), src).then_inc(stage_loaded[i % 2], 16)

            def rows_of(w, b, c):
                return w[bass.ds(b, 1), c * 128:(c + 1) * 128, :].rearrange("a p n -> (a p) n")

            def head_of(w, b, h):
                return w[bass.ds(b, 1), :, h * HDIM1:(h + 1) * HDIM1].rearrange("a (c p) n -> p (a c) n", p=128)

            def condition(b, mats, ph):
                if ph == 1:
                    sp.wait_ge(conds_ready, 2 * b + 1)
                for k, (w, bias) in enumerate(mats):
                    sp.dma_start(raw[0:COND, k, :], w[bass.ds(b, 1)].rearrange("a c n -> (a c) n")).then_inc(raw_loaded, 16)
                    sp.dma_start(raw[COND:COND + 1, k, :], bias[bass.ds(b, 1), :]).then_inc(raw_loaded, 16)

            def bias_row(out, v, b, done):
                sp.dma_start(out[:, :], v[bass.ds(b, 1), :].broadcast_to([128, DIM])).then_inc(done, 16)

            sp.wait_ge(w_ready, 2)
            with sp.Fori(0, LAYERS1) as b:
                condition(b, ((s1, sb1), (t1, tb1)), 0)
                for i in range(4):
                    weight(b, i, rows_of(wv, b, i))
                bias_row(row_b, bv, b, bv_loaded)
                for i in (0, 1):
                    weight(b, 4 + i, head_of((wq, wk)[i], b, 0))
                sp.wait_ge(y_ready, 20 * b + 10)
                sp.dma_start(spill.rearrange("(t p) d -> p t d", p=TILE), fx.nodes[0:TILE]).then_inc(x_spilled, 16)
                for i in range(2, 8):
                    weight(b, 4 + i, head_of((wq, wk)[i % 2], b, i // 2))
                    if i == 3:
                        condition(b, ((s2, sb2), (t2, tb2)), 1)
                for i in (0, 1):
                    weight(b, 12 + i, rows_of(wo, b, i))
                sp.wait_ge(qk_done, 40 * b + 40)
                bias_row(row_b, bo, b, bo_loaded)
                sp.wait_ge(o_done, 20 * b + 20)
                sp.wait_ge(x_spilled, 16 * b + 16)
                sp.dma_start(fx.nodes[0:TILE], spill.rearrange("(t p) d -> p t d", p=TILE)).then_inc(x_back, 16)
                for i in (2, 3):
                    weight(b, 12 + i, rows_of(wo, b, i))
                for i in (0, 1):
                    weight(b, 16 + i, rows_of(m1, b, i))
                sp.wait_ge(att_low, 4 * b + 4)
                bias_row(row_a, b2, b, b2_loaded)
                for i in (2, 3):
                    weight(b, 16 + i, rows_of(m1, b, i))
                for i in range(4):
                    weight(b, 20 + i, rows_of(m2, b, i))

        @block.gpsimd
        def _(pool):
            def split(b, i, high, low):
                st = stage[:, i % 2, :]
                wait_apart(pool, fx, stage_loaded[i % 2], 16 * (12 * b + i // 2 + 1))
                if len(high.shape) == 3:
                    st = st.rearrange("p (c n) -> p c n", c=CHUNKS)
                nc.gpsimd.tensor_copy(high, st).then_inc(split_high, 1)
                pool.wait_ge(split_high, 24 * b + i + 1)
                nc.gpsimd.tensor_tensor(low, st, high.bitcast(F32), ALU.subtract).then_inc(w_ready, 1)

            def condition(b, ph):
                wait_apart(pool, fx, raw_loaded, 64 * (2 * b + ph + 1))
                nc.gpsimd.tensor_copy(sw[64:96], raw[:, :, :]).then_inc(cond_own, 1)
                wait_apart(pool, fx, cond_own, 4 * b + 2 * ph + 1)
                nc.gpsimd.tensor_copy(sw[0:32], raw[:, :, :]).then_inc(cond_own, 1)
                pool.wait_ge(cond_own, 4 * b + 2 * ph + 2)
                nc.gpsimd.tensor_tensor(sw[32:64], raw[:, :, :], sw[0:32].bitcast(F32), ALU.subtract).then_inc(conds_ready, 1)
                pool.wait_ge(conds_ready, 2 * b + ph + 1)

            pool.memset(raw[:, :, :], 0.0).then_inc(w_ready, 1)
            pool.memset(mass_diag[0:1, 0, 0:1], 0.0).then_inc(w_ready, 1)
            pool.wait_ge(w_ready, 2)
            with pool.Fori(0, LAYERS1) as b:
                condition(b, 0)
                for i in range(4):
                    split(b, i, wa[0][:, i, :], wa[1][:, i, :])
                for i in (0, 1):
                    split(b, 4 + i, hw[:, 0, i], hw[:, 1, i])
                for t in range(TILES):
                    pool.wait_ge(v_high, 10 * b + t + 1)
                    nc.gpsimd.tensor_tensor(v_l[0:TILE, t, :], vf[0:TILE, t % 2, :], v_h[0:TILE, t, :],
                                            ALU.subtract).then_inc(v_low, 1)
                for h in range(HEADS1):
                    for j in range(TILES):
                        T = 40 * b + 10 * h + j
                        if h > 0 or j >= 2:
                            pool.wait_ge(rows_prod, T - 1)
                        wait_apart(pool, fx, inverted, T + 1)
                        nc.gpsimd.tensor_scalar(mass_diag[0:TILE, j % 2, :], fx.ident[0:TILE, 0:TILE],
                                                fx.mass[0:TILE, j, 2:3], None, ALU.mult).then_inc(diagonal, 1)
                        if h < HEADS1 - 1 and j in (3, 6):
                            i = 6 + 2 * h + (j == 6)
                            pool.wait_ge(proj_prod, 24 * b + 6 * h + 6)
                            split(b, i, hw[:, 0, i % 2], hw[:, 1, i % 2])
                    if h == 1:
                        pool.wait_ge(mod_ready, 20 * b + 10)
                        pool.wait_ge(diagonal, 40 * b + 20)
                        condition(b, 1)
                pool.wait_ge(qk_done, 40 * b + 40)
                for i in range(4):
                    split(b, 12 + i, wb[0][:, i, :], wb[1][:, i, :])
                pool.wait_ge(bo_loaded, 16 * b + 16)
                pool.wait_ge(x_back, 16 * b + 16)
                for t in range(TILES):
                    nc.gpsimd.tensor_tensor(fx.nodes[0:TILE, t, :], fx.nodes[0:TILE, t, :], row_b[0:TILE, :],
                                            ALU.add).then_inc(x_biased, 1)
                pool.wait_ge(att_low, 4 * b + 4)
                for i in range(4):
                    split(b, 16 + i, wa[0][:, i, :], wa[1][:, i, :])
                pool.wait_ge(o_prod, 10 * b + 10)
                for i in range(4):
                    split(b, 20 + i, wb[0][:, i, :], wb[1][:, i, :])
                pool.wait_ge(b2_loaded, 16 * b + 16)
                for t in range(TILES):
                    pool.wait_ge(y_ready, 20 * b + 10 + t + 1)
                    nc.gpsimd.tensor_tensor(fx.nodes[0:TILE, t, :], fx.nodes[0:TILE, t, :], row_a[0:TILE, :],
                                            ALU.add).then_inc(x2_biased, 1)
                pool.wait_ge(x2_biased, 10 * b + 10)
                pool.wait_ge(h_prod, 20 * b + 20)

        @block.tensor
        def _(pe):
            def modulation(b, ph, t):
                pe.wait_ge(conds_ready, 2 * b + ph + 1)
                if t >= 2:
                    pe.wait_ge(y_ready, 20 * b + 10 * ph + t - 1)
                for k in range(2):
                    mm = pe.matmul(bank(4 * (t % 2) + k)[0:TILE], fx.cond[:, cols(t)], sw[:, k, :], start=True, stop=True)
                mm.then_inc(mod_ready, 1)

            def turn_rows(b, ph, t):
                pe.wait_ge(y_ready, 20 * b + 10 * ph + t + 1)
                if t >= 2:
                    pe.wait_ge(y_low, 20 * b + 10 * ph + t - 1)
                for c in range(CHUNKS):
                    mm = pe.transpose(bank(4 * (t % 2) + 2)[:, c * TILE:(c + 1) * TILE], yr[0:TILE, t % 2, c * 128:(c + 1) * 128],
                                      fx.ident[0:TILE, 0:TILE])
                mm.then_inc(y_turned, 1)

            def rows_product(t, n, weights):
                for c in range(CHUNKS):
                    mm = three(pe, bank(n)[0:TILE], [p[:, c, cols(t)] for p in pair_y], [p[:, c, :] for p in weights],
                               c == 0, c == CHUNKS - 1)
                return mm

            with pe.Fori(0, LAYERS1) as b:
                pe.wait_ge(x_done, 10 * b + 10)
                for i in range(TILES + 2):
                    if i < TILES:
                        modulation(b, 0, i)
                    if 1 <= i <= TILES:
                        turn_rows(b, 0, i - 1)
                    if i >= 2:
                        t = i - 2
                        pe.wait_ge(w_ready, 24 * b + 4 + 2)
                        pe.wait_ge(y_low, 20 * b + t + 1)
                        if t >= 2:
                            pe.wait_ge(v_sum, 10 * b + t - 1)
                        rows_product(t, 4 * (t % 2) + 3, wa).then_inc(v_prod, 1)

                for h in range(HEADS1):
                    pe.wait_ge(w_ready, 24 * b + 6 + 2 * h + 2)
                    if h == 0:
                        pe.wait_ge(v_sum, 10 * b + 10)
                    else:
                        pe.wait_ge(pt_low, 120 * b + 30 * h)
                        pe.wait_ge(rows_copied, 20 * b + 5 * h)
                    for c in range(6):
                        w, (a, z) = c // 3, ((0, 500), (500, 1000), (1000, NODES))[c % 3]
                        if c >= 2:
                            pe.wait_ge(proj_low, 24 * b + 6 * h + c - 1)
                        for k in range(CHUNKS):
                            mm = three(pe, bank(6 + c % 2)[:, 0:z - a], [hw[:, p, w, k, :] for p in range(2)],
                                       [p[:, k, a:z] for p in pair_y], k == 0, k == CHUNKS - 1)
                        mm.then_inc(proj_prod, 1)
                    pe.wait_ge(proj_low, 24 * b + 6 * h + 6)
                    for i in range(LAG_STEPS):
                        T = 40 * b + 10 * h + i
                        if i < TILES:
                            if h > 0 or i > 0:
                                pe.wait_ge(scored, T)
                            for a, z in CUTS:
                                mm = three(pe, psum[0:TILE, a:z], [p[:, cols(i)] for p in qk[0]],
                                           [p[:, a:z] for p in qk[1]], True, True)
                            mm.then_inc(qk_done, 1)
                        if 3 <= i:
                            g, half = (i - 3) // 2, (i - 3) % 2
                            G = 20 * b + 5 * h + g
                            if half == 0:
                                pe.wait_ge(pt_low, 120 * b + 30 * h + 6 * g + 6)
                                if h > 0 or g > 0:
                                    pe.wait_ge(o_done, G)
                            for d in range(5 * half, 5 * half + 5):
                                out = bank(5)[:, 0:250]
                                mm = three(pe, out, [p[0:TILE, d, h * HDIM1:(h + 1) * HDIM1] for p in (v_h, v_l)],
                                           [p[0:TILE, g % 2, d, :] for p in (pt_h, pt_l)], d == 0, d == TILES - 1)
                            if half == 1:
                                mm.then_inc(pv_done, 1)
                        if 1 <= i <= TILES:
                            j = i - 1
                            pe.wait_ge(exped, T)
                            for u in range(3):
                                U = 3 * j + u
                                if U >= 3:
                                    pe.wait_ge(pt_low, 120 * b + 30 * h + U - 2)
                                out = bank((3, 4, 7)[u])
                                for d in range(4 * u, min(4 * u + 4, TILES)):
                                    mm = pe.transpose(out[0:TILE, cols(d - 4 * u)], prob[0:TILE, j % 2, cols(d)],
                                                      fx.ident[0:TILE, 0:TILE])
                                mm.then_inc(turned, 1)
                        if 2 <= i <= TILES + 1:
                            j = i - 2
                            g = j // 2
                            pe.wait_ge(diagonal, T - 1)
                            if j % 2 == 0 and g > 0:
                                pe.wait_ge(rows_copied, 20 * b + 5 * h + g)
                            pe.matmul(bank(6)[:, cols(j % 2)],
                                      fx.ones[0:TILE, :], mass_diag[0:TILE, j % 2, :], start=True, stop=True,
                                      skip_group_check=True).then_inc(rows_prod, 1)

                pe.wait_ge(att_low, 4 * b + 4)
                pe.wait_ge(pt_low, 120 * b + 120)
                pe.wait_ge(o_done, 20 * b + 20)
                pe.wait_ge(w_ready, 24 * b + 16 + 2)
                for i in range(TILES + 1):
                    if i < TILES:
                        if i >= 2:
                            pe.wait_ge(residual, 10 * b + i - 1)
                        rows_product(i, 4 * (i % 2) + 3, wb).then_inc(o_prod, 1)
                        modulation(b, 1, i)
                    if i >= 1:
                        turn_rows(b, 1, i - 1)
                pe.wait_ge(w_ready, 24 * b + 20 + 2)
                pe.wait_ge(y_low, 20 * b + 20)
                for n in range(GROUPS):
                    if n >= 2:
                        pe.wait_ge(h_rows, 20 * b + 4 * n - 4)
                    for j in range(CHUNKS):
                        for c in range(CHUNKS):
                            mm = three(pe, bank(4 * (n % 2) + j)[:, 0:250], [p[:, c, j * 128:(j + 1) * 128] for p in wa],
                                       [p[:, c, 250 * n:250 * n + 250] for p in pair_y], c == 0, c == CHUNKS - 1)
                        mm.then_inc(h_prod, 1)
                pe.wait_ge(w_ready, 24 * b + 24 + 2)
                for t in range(TILES):
                    pe.wait_ge(h_low, 5 * b + t // 2 + 1)
                    if t == 0:
                        pe.wait_ge(h_rows, 20 * b + 16)
                    if t >= 4:
                        pe.wait_ge(x_done, 10 * b + 10 + t - 3)
                    rows_product(t, 4 + t % 4, wb).then_inc(m_prod, 1)

        @block.scalar
        def _(act):
            def turned_high(b, ph, t):
                act.wait_ge(y_turned, 20 * b + 10 * ph + t + 1)
                nc.scalar.activation(y_h[:, :, cols(t)], bank(4 * (t % 2) + 2)[:, 0:4 * TILE].rearrange("p (c n) -> p c n", c=4),
                                     ACT.Copy).then_inc(y_high, 1)

            def std(b, ph, t):
                act.wait_ge(var_ready, 20 * b + 10 * ph + t + 1)
                norm_std(nc, fx, t % 2, std_ready)

            with act.Fori(0, LAYERS1) as b:
                for i in range(TILES + 3):
                    if i < TILES:
                        std(b, 0, i)
                    if 1 <= i <= TILES:
                        turned_high(b, 0, i - 1)
                    if i >= 3:
                        t = i - 3
                        act.wait_ge(v_sum, 10 * b + t + 1)
                        nc.scalar.activation(v_h[0:TILE, t, :], vf[0:TILE, t % 2, :], ACT.Copy).then_inc(v_high, 1)
                act.wait_ge(v_low, 10 * b + 10)
                act.wait_ge(x_spilled, 16 * b + 16)
                for h in range(HEADS1):
                    for c in range(6):
                        w, (a, z) = c // 3, ((0, 500), (500, 1000), (1000, NODES))[c % 3]
                        wait_apart(act, fx, proj_prod, 24 * b + 6 * h + c + 1)
                        nc.scalar.activation(qk[w][0][:, a:z], bank(6 + c % 2)[:, 0:z - a], ACT.Identity,
                                             bias=fx.qkb[:, w, bass.ds(HEADS1 * b + h, 1)]).then_inc(proj_high, 1)
                    for i in range(LAG_STEPS):
                        T = 40 * b + 10 * h + i
                        if i < TILES:
                            act.wait_ge(peaked, T + 1)
                            nc.scalar.activation(prob[0:TILE, i % 2, :], prob[0:TILE, i % 2, :], ACT.Exp,
                                                 bias=fx.peak[0:TILE, i % 2, 1:2],
                                                 accum_out=fx.mass[0:TILE, i, 0:1]).then_inc(exped, 1)
                        if 1 <= i <= TILES:
                            j = i - 1
                            for u in range(3):
                                U = 3 * j + u
                                act.wait_ge(turned, 120 * b + 30 * h + U + 1)
                                src, dst = unit_views(bank((3, 4, 7)[u]), pt_h, u, j)
                                nc.scalar.activation(dst, src, ACT.Copy).then_inc(pt_high, 1)
                        if i >= 3 and i % 2 == 1:
                            g = (i - 3) // 2
                            act.wait_ge(rows_prod, 40 * b + 10 * h + 2 * g + 2)
                            if h > 0 or g >= 2:
                                act.wait_ge(o_done, 20 * b + 5 * h + g - 1)
                            nc.scalar.activation(mass_rows[:, g % 2, :], bank(6)[:, 0:250],
                                                 ACT.Copy).then_inc(rows_copied, 1)
                for i in range(TILES + 1):
                    if i < TILES:
                        std(b, 1, i)
                    if i >= 1:
                        turned_high(b, 1, i - 1)
                for n in range(GROUPS):
                    if n >= 2:
                        act.wait_ge(h_low, 5 * b + n - 1)
                    for j in range(CHUNKS):
                        wait_apart(act, fx, h_prod, 20 * b + 4 * n + j + 1)
                        nc.scalar.activation(hidden[:, n % 2, j, :], bank(4 * (n % 2) + j)[:, 0:250], ACT.Relu,
                                             bias=fx.qkb[:, 2, bass.ds(CHUNKS * b + j, 1)]).then_inc(h_rows, 1)

        @block.vector
        def _(dve):
            def stats(b, ph, t):
                L = 20 * b + 10 * ph + t
                norm_stats(dve, fx, t % 2, fx.nodes[0:TILE, t, :], stats_own, L + 1, var_ready)

            def finish(b, ph, t):
                L = 20 * b + 10 * ph + t
                dve.wait_ge(std_ready, L + 1)
                if t >= 2:
                    dve.wait_ge(y_turned, L - 1)
                norm_rows(dve, fx, t % 2, xn[0:TILE, t % 2, :], fx.nodes[0:TILE, t, :], finish_own, 3 * L + 1)\
                    .then_inc(finish_own, 1)
                dve.wait_ge(mod_ready, L + 1)
                dve.wait_ge(finish_own, 3 * L + 2)
                dve.scalar_tensor_tensor(yr[0:TILE, t % 2, :], bank(4 * (t % 2))[0:TILE], 1.0, xn[0:TILE, t % 2, :],
                                         ALU.add, ALU.mult).then_inc(finish_own, 1)
                dve.wait_ge(finish_own, 3 * L + 3)
                dve.tensor_tensor(yr[0:TILE, t % 2, :], yr[0:TILE, t % 2, :], bank(4 * (t % 2) + 1)[0:TILE],
                                  ALU.add).then_inc(y_ready, 1)

            def turned_low(b, ph, t):
                dve.wait_ge(y_high, 20 * b + 10 * ph + t + 1)
                dve.tensor_tensor(y_l[:, :, cols(t)], bank(4 * (t % 2) + 2)[:, 0:4 * TILE].rearrange("p (c n) -> p c n", c=4),
                                  y_h[:, :, cols(t)].bitcast(F32), ALU.subtract).then_inc(y_low, 1)

            dve.memset(fx.peak[0:1, 0, 0:1], 0.0).then_inc(x_done, TILES)
            with dve.Fori(0, LAYERS1) as b:
                dve.wait_ge(x_done, 10 * b + 10)
                for i in range(TILES + 3):
                    if 2 <= i <= TILES + 1:
                        turned_low(b, 0, i - 2)
                    if i < TILES:
                        stats(b, 0, i)
                    if 1 <= i <= TILES:
                        finish(b, 0, i - 1)
                    if i >= 3:
                        t = i - 3
                        dve.wait_ge(v_prod, 10 * b + t + 1)
                        if t == 0:
                            dve.wait_ge(bv_loaded, 16 * b + 16)
                        if t >= 2:
                            dve.wait_ge(v_low, 10 * b + t - 1)
                        dve.tensor_tensor(vf[0:TILE, t % 2, :], bank(4 * (t % 2) + 3)[0:TILE], row_b[0:TILE, :],
                                          ALU.add).then_inc(v_sum, 1)
                dve.wait_ge(x_spilled, 16 * b + 16)
                for h in range(HEADS1):
                    for c in range(6):
                        w, (a, z) = c // 3, ((0, 500), (500, 1000), (1000, NODES))[c % 3]
                        dve.wait_ge(proj_high, 24 * b + 6 * h + c + 1)
                        dve.scalar_tensor_tensor(qk[w][1][:, a:z], bank(6 + c % 2)[:, 0:z - a],
                                                 fx.qkb[:, w, bass.ds(HEADS1 * b + h, 1)], qk[w][0][:, a:z].bitcast(F32),
                                                 ALU.add, ALU.subtract).then_inc(proj_low, 1)
                    for i in range(LAG_STEPS):
                        T = 40 * b + 10 * h + i
                        if i < TILES:
                            if i >= 2:
                                dve.wait_ge(turned, 120 * b + 30 * h + 3 * (i - 1))
                            wait_apart(dve, fx, qk_done, T + 1)
                            row_scores(dve, psum[0:TILE, 0:NODES], i, T, HDIM1 ** -0.5)
                        if 1 <= i <= TILES:
                            row_mass(dve, i - 1, T - 1)
                            j = i - 1
                            for u in range(3):
                                U = 3 * j + u
                                dve.wait_ge(pt_high, 120 * b + 30 * h + U + 1)
                                src, dst = unit_views(bank((3, 4, 7)[u]), pt_l, u, j)
                                _, high = unit_views(bank((3, 4, 7)[u]), pt_h, u, j)
                                dve.tensor_tensor(dst, src, high, ALU.subtract).then_inc(pt_low, 1)
                        if i >= 4 and i % 2 == 0:
                            g = (i - 4) // 2
                            dve.wait_ge(pv_done, 20 * b + 5 * h + g + 1)
                            dve.wait_ge(rows_copied, 20 * b + 5 * h + g + 1)
                            dve.tensor_tensor(attended[:, h, 250 * g:250 * g + 250],
                                              bank(5)[:, 0:250], mass_rows[:, g % 2, :],
                                              ALU.mult).then_inc(o_done, 1)
                dve.wait_ge(o_done, 20 * b + 20)
                for c in range(CHUNKS):
                    dve.tensor_copy(y_h[:, c, :], attended[:, c, :]).then_inc(att_high, 1)
                for c in range(CHUNKS):
                    dve.wait_ge(att_high, 4 * b + c + 1)
                    dve.tensor_tensor(y_l[:, c, :], attended[:, c, :], y_h[:, c, :].bitcast(F32),
                                      ALU.subtract).then_inc(att_low, 1)
                for i in range(TILES + 2):
                    if i < TILES:
                        dve.wait_ge(o_prod, 10 * b + i + 1)
                        dve.wait_ge(x_biased, 10 * b + i + 1)
                        dve.tensor_tensor(fx.nodes[0:TILE, i, :], bank(4 * (i % 2) + 3)[0:TILE], fx.nodes[0:TILE, i, :],
                                          ALU.add).then_inc(residual, 1)
                        dve.wait_ge(residual, 10 * b + i + 1)
                        stats(b, 1, i)
                    if i >= 2:
                        turned_low(b, 1, i - 2)
                    if 1 <= i <= TILES:
                        finish(b, 1, i - 1)
                for n in range(GROUPS):
                    dve.wait_ge(h_rows, 20 * b + 4 * n + 4)
                    at = slice(250 * n, 250 * n + 250)
                    dve.tensor_copy(y_h[:, :, at], hidden[:, n % 2]).then_inc(h_high, 1)
                    dve.wait_ge(h_high, 5 * b + n + 1)
                    dve.tensor_tensor(y_l[:, :, at], hidden[:, n % 2], y_h[:, :, at].bitcast(F32),
                                      ALU.subtract).then_inc(h_low, 1)
                for t in range(TILES):
                    dve.wait_ge(m_prod, 10 * b + t + 1)
                    dve.wait_ge(x2_biased, 10 * b + t + 1)
                    dve.tensor_tensor(fx.nodes[0:TILE, t, :], bank(4 + t % 4)[0:TILE], fx.nodes[0:TILE, t, :],
                                      ALU.add).then_inc(x_done, 1)



def third_layer(nc, fx, psum, kept, count_rows, eps, w1, b1, g1, be1, w2, b2, g2, be2):
    with ExitStack() as ctx:
        def sem(name):
            return ctx.enter_context(nc.semaphore("L2_" + name))

        before = packer(nc, VALUES_AT)("layer_input", [128, TILES, DIM], F32)
        counts = packer(nc, LOGS_AT)("counts_by_target", [128, TILES, WIDE], F32)
        place = packer(nc, TURNED_AT)
        plane = [place(f"batch_plane_{k}", [128, CHUNKS, NODES], F32) for k in range(2)]
        place = packer(nc, SLOT_A_AT)
        w = [place(f"batch_weight_{k}", [128, CHUNKS, DIM], F32) for k in range(2)]
        lanes = place("batch_vectors", [128, 6, CHUNKS], F32)
        factor = place("diagonal_factor", [128, 2], F32)
        diagonal = place("diagonal", [128, TILE], F32)
        stats = place("batch_stats", [128, 2, 3, 6], F32)
        moments = place("batch_moments", [128, 2, 2], F32)
        affine = place("batch_affine", [128, 2, 4], F32)

        loaded, in_loaded, w_loaded = sem("counts_loaded"), sem("input_loaded"), sem("weights_loaded")
        joined, stat_own, var_ready = sem("inputs_joined"), sem("stats_step"), sem("variance_ready")
        std_ready, rstd_own, normed = sem("std_ready"), sem("rstd_step"), sem("nodes_normed")
        own, diag_ready = sem("diagonal_step"), sem("diagonal_ready")
        prod, copied = sem("products"), sem("products_copied")
        b_own, b_var, b_std, b_aff = sem("batch_step"), sem("batch_variance"), sem("batch_std"), sem("batch_affine_ready")
        applied, turned, added = sem("batch_applied"), sem("turned_back"), sem("output_added")

        def region(c):
            return psum[:, (c % 2) * 3 * BANK:(c % 2) * 3 * BANK + NODES]

        def bank(n):
            return psum[:, n * BANK:(n + 1) * BANK]

        block = ctx.enter_context(nc.Block())

        @block.sync
        def _(sp):
            sp.dma_start(before[0:TILE], kept.rearrange("(t p) d -> p t d", p=TILE)).then_inc(in_loaded, 16)
            sp.dma_start(counts[0:TILE, :, 0:NODES],
                         count_rows[0:NODES, :].rearrange("(t p) s -> p t s", p=TILE)).then_inc(loaded, 16)
            sp.dma_start(factor[:, 0:1], eps.rearrange("(a b) -> a b", a=1).broadcast_to([128, 1])).then_inc(w_loaded, 16)
            for k, v in enumerate((w1, w2)):
                sp.dma_start(w[k][:, :, :], v.rearrange("(c p) n -> p c n", p=128)).then_inc(w_loaded, 16)
            for k, v in enumerate((b1, g1, be1, b2, g2, be2)):
                sp.dma_start(lanes[:, k, :], v.rearrange("(c p) -> p c", p=128),
                             allow_slow_non_contiguous=True).then_inc(w_loaded, 16)

        @block.vector
        def _(dve):
            dve.wait_ge(in_loaded, 16)
            for i in range(TILES + 1):
                if i < TILES:
                    row = fx.nodes[0:TILE, i, :]
                    dve.tensor_tensor(row, row, before[0:TILE, i, :], ALU.add).then_inc(joined, 1)
                    dve.wait_ge(joined, i + 1)
                    norm_stats(dve, fx, i % 2, row, stat_own, i + 1, var_ready)
                if i >= 1:
                    row = fx.nodes[0:TILE, i - 1, :]
                    dve.wait_ge(std_ready, i)
                    norm_rows(dve, fx, (i - 1) % 2, row, row, rstd_own, i).then_inc(normed, 1)
            dve.wait_ge(w_loaded, 144)
            dve.wait_ge(loaded, 16)
            dve.tensor_scalar(factor[:, 1:2], factor[:, 0:1], 1.0, None, ALU.add).then_inc(own, 1)
            dve.wait_ge(own, 1)
            dve.tensor_scalar(diagonal[:, :], fx.ident[:, 0:TILE], factor[:, 1:2], None, ALU.mult).then_inc(own, 1)
            dve.wait_ge(own, 2)
            for t in range(TILES):
                at = counts[0:TILE, t, t * TILE:(t + 1) * TILE]
                dve.tensor_tensor(at, at, diagonal[0:TILE, :], ALU.add).then_inc(diag_ready, 1)

            for n in range(2 * CHUNKS):
                k, j = n // CHUNKS, n % CHUNKS
                u = plane[1 - k][:, j, :]
                at = n % 2
                dve.wait_ge(copied, CHUNKS + n + 1)
                for q, (a, z) in enumerate(((0, 500), (500, 1000), (1000, NODES))):
                    dve.bn_stats(stats[:, at, q, :], u[:, a:z]).then_inc(b_own, 1)
                wait_apart(dve, fx, b_own, 6 * n + 3)
                dve.bn_aggr(moments[:, at, :], stats[:, at].rearrange("p q s -> p (q s)")).then_inc(b_var, 1)
                dve.wait_ge(b_std, n + 1)
                f = affine[:, at]
                dve.reciprocal(f[:, 1:2], f[:, 0:1]).then_inc(b_own, 1)
                dve.wait_ge(b_own, 6 * n + 4)
                dve.tensor_tensor(f[:, 2:3], f[:, 1:2], lanes[:, 3 * k + 1, j:j + 1], ALU.mult).then_inc(b_own, 1)
                dve.wait_ge(b_own, 6 * n + 5)
                dve.tensor_tensor(f[:, 3:4], f[:, 2:3], moments[:, at, 0:1], ALU.mult).then_inc(b_own, 1)
                dve.wait_ge(b_own, 6 * n + 6)
                dve.tensor_tensor(f[:, 3:4], lanes[:, 3 * k + 2, j:j + 1], f[:, 3:4], ALU.subtract).then_inc(b_aff, 1)

            for i in range(TILES + 1):
                if i < TILES:
                    row = fx.nodes[0:TILE, i, :]
                    dve.wait_ge(turned, i + 1)
                    dve.tensor_tensor(row, bank(6 + i % 2)[0:TILE], row, ALU.add).then_inc(added, 1)
                    dve.wait_ge(added, i + 1)
                    norm_stats(dve, fx, i % 2, row, stat_own, TILES + i + 1, var_ready)
                if i >= 1:
                    row = fx.nodes[0:TILE, i - 1, :]
                    dve.wait_ge(std_ready, TILES + i)
                    norm_rows(dve, fx, (i - 1) % 2, row, row, rstd_own, TILES + i).then_inc(normed, 1)

        @block.scalar
        def _(act):
            for t in range(TILES):
                act.wait_ge(var_ready, t + 1)
                norm_std(nc, fx, t % 2, std_ready)
            for c in range(CHUNKS):
                act.wait_ge(prod, c + 1)
                nc.scalar.activation(plane[0][:, c, :], region(c), ACT.Copy).then_inc(copied, 1)
            act.wait_ge(w_loaded, 144)

            def apply(n):
                k, j = n // CHUNKS, n % CHUNKS
                u = plane[1 - k][:, j, :]
                act.wait_ge(b_var, n + 1)
                nc.scalar.activation(affine[:, n % 2, 0:1], moments[:, n % 2, 1:2], ACT.Sqrt, bias=fx.eps[:, :]).then_inc(b_std, 1)
                act.wait_ge(b_aff, n + 1)
                nc.scalar.activation(u, u, (ACT.Relu, ACT.Identity)[k], bias=affine[:, n % 2, 3:4],
                                     scale=affine[:, n % 2, 2:3]).then_inc(applied, 1)

            for n in range(2 * CHUNKS):
                k, j = n // CHUNKS, n % CHUNKS
                act.wait_ge(prod, CHUNKS + n + 1)
                nc.scalar.activation(plane[1 - k][:, j, :], region(n), ACT.Identity,
                                     bias=lanes[:, 3 * k, j:j + 1]).then_inc(copied, 1)
                apply(n)
            for t in range(TILES):
                act.wait_ge(var_ready, TILES + t + 1)
                norm_std(nc, fx, t % 2, std_ready)

        @block.tensor
        def _(pe):
            pe.wait_ge(normed, TILES)
            pe.wait_ge(diag_ready, TILES)
            for c in range(CHUNKS):
                if c >= 2:
                    pe.wait_ge(copied, c - 1)
                for k in range(TILES):
                    for a, z in CUTS:
                        mm = pe.matmul(region(c)[:, a:z], fx.nodes[0:TILE, k, c * 128:(c + 1) * 128],
                                       counts[0:TILE, k, a:z], start=(k == 0), stop=(k == TILES - 1))
                mm.then_inc(prod, 1)
            for n in range(2 * CHUNKS):
                k, j = n // CHUNKS, n % CHUNKS
                if j == 0:
                    if k == 0:
                        pe.wait_ge(w_loaded, 144)
                        pe.wait_ge(copied, CHUNKS)
                    else:
                        pe.wait_ge(applied, CHUNKS)
                if n >= 2:
                    pe.wait_ge(copied, CHUNKS + n - 1)
                for c in range(CHUNKS):
                    for a, z in CUTS:
                        mm = pe.matmul(region(n)[:, a:z], w[k][:, c, j * 128:(j + 1) * 128], plane[k][:, c, a:z],
                                       start=(c == 0), stop=(c == CHUNKS - 1))
                mm.then_inc(prod, 1)
            pe.wait_ge(applied, 2 * CHUNKS)
            for t in range(TILES):
                if t >= 2:
                    pe.wait_ge(added, t - 1)
                for c in range(CHUNKS):
                    mm = pe.transpose(bank(6 + t % 2)[0:TILE, c * 128:(c + 1) * 128], plane[0][:, c, t * TILE:(t + 1) * TILE],
                                      fx.ident[:, :])
                mm.then_inc(turned, 1)


def fourth_layer(nc, fx, psum, count_rows, ws, wb, a_w, a_b, out):
    with ExitStack() as ctx:
        def sem(name):
            return ctx.enter_context(nc.semaphore("L3_" + name))

        logs = packer(nc, LOGS_AT)("log_counts_by_target", [128, TILES, WIDE], F32)
        place = packer(nc, TURNED_AT)
        x_t = place("nodes_turned", [128, CHUNKS, NODES], F32)
        wx_t = place("projected_turned", [128, CHUNKS, NODES], F32)
        spread = place("source_scores_spread", [128, HEADS3, NODES], F32)
        values = packer(nc, VALUES_AT)("projected_parts", [128, TILES, HEADS3, 2, HDIM3], BF16)
        after = WORK_AT + TILES * DIM * 4
        place = packer(nc, after)
        target = place("target_scores", [128, TILES, HEADS3], F32)
        bias_a = place("score_bias_row", [128, HEADS3], F32)
        col_b = place("projection_bias_columns", [128, CHUNKS], F32)
        a_src = place("source_vectors", [128, HEADS3], F32)
        a_tgt = place("target_vectors", [128, CHUNKS, HEADS3], F32)
        after += 640
        place = packer(nc, after)
        prob = place("row_probabilities", [128, 2, NODES], F32)
        pt = [place(f"turned_{p}", [128, 2, TILES, TILE], BF16) for p in ("high", "low")]
        fifth = place("fifth_of_source_scores", [128, 2, NODES], F32)
        part = place("output_part", [128, TILES, HDIM3], F32)
        place = packer(nc, after)
        w_sb = place("projection_weights", [128, CHUNKS, DIM], F32)
        row_b = place("projection_bias_row", [128, DIM], F32)
        wf = place("projected_rows", [128, 2, DIM], F32)
        wide = place("source_vectors_spread", [128, HEADS3, 128], F32)
        plain = packer(nc, after + 18432)("plain_logs_by_target", [128, 2, NODES], F32)

        counted, set_zero, loaded, stored = sem("counts_loaded"), sem("vectors_zeroed"), sem("weights_loaded"), sem("stored")
        log_plain, log_ready, own = sem("logs_plain"), sem("logs_ready"), sem("log_step")
        turned, x_copied, spread_ready = sem("nodes_turned"), sem("turned_copied"), sem("vectors_spread")
        prod, copied, v_prod, v_sum = sem("products"), sem("products_copied"), sem("value_products"), sem("values_summed")
        v_high, v_low, r_prod, r_sum, r_ready = (sem("values_high"), sem("values_low"), sem("target_products"),
                                                 sem("targets_summed"), sem("targets_ready"))
        fifth_ready, leaky, scored, peaked = sem("fifth_ready"), sem("leaky"), sem("scored"), sem("peaked")
        exped, mass_own, inverted = sem("exped"), sem("mass_step"), sem("inverted")
        p_turned, p_high, p_low, pv = sem("p_turned"), sem("p_high"), sem("p_low"), sem("weighted")
        half, summed, joined = sem("half_scaled"), sem("halves_joined"), sem("nodes_joined")
        stat_own, var_ready, std_ready = sem("stats_step"), sem("variance_ready"), sem("std_ready")
        rstd_own, normed = sem("rstd_step"), sem("normed")

        def region(c):
            return psum[:, (c % 2) * 3 * BANK:(c % 2) * 3 * BANK + NODES]

        def bank(n):
            return psum[:, n * BANK:(n + 1) * BANK]

        def cols(t):
            return slice(t * TILE, (t + 1) * TILE)

        def unit_views(source, place_, u, j):
            n = min(4, TILES - 4 * u)
            return (source[0:TILE, 0:n * TILE].rearrange("p (d n) -> p d n", d=n), place_[0:TILE, j % 2, 4 * u:4 * u + n, :])

        LAG = TILES + 3

        block = ctx.enter_context(nc.Block())

        @block.sync
        def _(sp):
            sp.dma_start(logs[0:TILE, :, 0:NODES],
                         count_rows[0:NODES, :].rearrange("(t p) s -> p t s", p=TILE)).then_inc(counted, 16)
            for c in range(CHUNKS):
                sp.dma_start(w_sb[:, c, :].rearrange("p (h d) -> p h d", h=HEADS3),
                             ws[:, c * 128:(c + 1) * 128, :].rearrange("h p d -> p h d")).then_inc(loaded, 16)
            sp.dma_start(row_b[:, :], wb.rearrange("(a h) d -> a (h d)", a=1).broadcast_to([128, DIM])).then_inc(loaded, 16)
            sp.dma_start(col_b[:, :], wb.rearrange("(c e) d -> (e d) c", e=2), allow_slow_non_contiguous=True).then_inc(loaded, 16)
            sp.dma_start(bias_a[:, :], a_b.rearrange("(a h) -> a h", a=1).broadcast_to([128, HEADS3])).then_inc(loaded, 16)
            sp.wait_ge(set_zero, 2)
            for h in range(HEADS3):
                lo = HDIM3 * (h % 2)
                sp.dma_start(a_src[lo:lo + HDIM3, h:h + 1], a_w[h, HDIM3:2 * HDIM3].rearrange("(p a) -> p a", a=1),
                             allow_slow_non_contiguous=True).then_inc(loaded, 16)
                sp.dma_start(a_tgt[lo:lo + HDIM3, h // 2, h:h + 1], a_w[h, 0:HDIM3].rearrange("(p a) -> p a", a=1),
                             allow_slow_non_contiguous=True).then_inc(loaded, 16)
            sp.wait_ge(normed, TILES)
            sp.dma_start(out.rearrange("(t p) d -> p t d", p=TILE), fx.nodes[0:TILE]).then_inc(stored, 16)
            sp.wait_ge(stored, 16)

        ALL = 16 * (4 + 3 + 2 * HEADS3)

        @block.gpsimd
        def _(pool):
            pool.memset(a_src[:, :], 0.0).then_inc(set_zero, 1)
            pool.memset(a_tgt[:, :, :], 0.0).then_inc(set_zero, 1)
            for t in range(TILES):
                pool.wait_ge(v_high, t + 1)
                nc.gpsimd.tensor_tensor(values[0:TILE, t, :, 1, :], wf[0:TILE, t % 2, :].rearrange("p (h d) -> p h d", d=HDIM3),
                                        values[0:TILE, t, :, 0, :], ALU.subtract).then_inc(v_low, 1)
            with pool.Fori(0, HEADS3) as h:
                for j in range(TILES):
                    pool.wait_ge(summed, 10 * h + j + 1)
                    at = fx.nodes[0:TILE, j, bass.ds(h * HDIM3, HDIM3)]
                    nc.gpsimd.tensor_tensor(at, at, part[0:TILE, j, :], ALU.add).then_inc(joined, 1)

        @block.vector
        def _(dve):
            steps = [0]
            dve.wait_ge(loaded, ALL)
            for h in range(HEADS3):
                dve.tensor_scalar(wide[:, h, :], fx.ones[:, :], a_src[:, h:h + 1], None, ALU.mult).then_inc(spread_ready, 1)
            for t in range(TILES):
                dve.wait_ge(log_plain, t + 1)
                log_counts(dve, logs[0:TILE, t, 0:NODES], plain[0:TILE, t % 2, :], 1.0, log_ready, own, steps)
                dve.wait_ge(v_prod, t + 1)
                if t >= 2:
                    dve.wait_ge(v_low, t - 1)
                dve.tensor_tensor(wf[0:TILE, t % 2, :], bank(6 + t % 2)[0:TILE], row_b[0:TILE, :], ALU.add).then_inc(v_sum, 1)
            dve.wait_ge(r_prod, TILES)
            r = target[0:TILE].rearrange("p t h -> p (t h)")
            dve.tensor_tensor(target[0:TILE], bank(6)[0:TILE, 0:TILES * HEADS3].rearrange("p (t h) -> p t h", h=HEADS3),
                              bias_a[0:TILE, :].unsqueeze(1).broadcast_to([TILE, TILES, HEADS3]), ALU.add).then_inc(r_sum, 1)
            dve.wait_ge(r_sum, 1)
            dve.tensor_scalar(r, r, -0.8, None, ALU.mult).then_inc(r_ready, 1)
            dve.wait_ge(r_ready, 1)
            dve.wait_ge(v_low, TILES)
            dve.wait_ge(copied, CHUNKS + HEADS3)
            with dve.Fori(0, HEADS3) as h:
                for i in range(LAG):
                    T = 10 * h + i
                    if i < TILES:
                        if i == 0:
                            dve.wait_ge(fifth_ready, h + 1)
                        if i >= 2:
                            dve.wait_ge(p_turned, 30 * h + 3 * (i - 1))
                        dve.scalar_tensor_tensor(prob[0:TILE, i % 2, :], fifth[0:TILE, bass.ds(h % 2, 1), :].rearrange("p a n -> p (a n)"),
                                                 target[0:TILE, i, bass.ds(h, 1)], spread[0:TILE, bass.ds(h, 1), :].rearrange("p a n -> p (a n)"),
                                                 ALU.add, ALU.max).then_inc(leaky, 1)
                        wait_apart(dve, fx, leaky, T + 1)
                        p = fx.peak[0:TILE, i % 2]
                        dve.tensor_tensor_reduce(prob[0:TILE, i % 2, :], prob[0:TILE, i % 2, :], logs[0:TILE, i, 0:NODES], 1.0,
                                                 MASKED, ALU.add, ALU.max, p[:, 0:1]).then_inc(scored, 1)
                        dve.wait_ge(scored, T + 1)
                        dve.tensor_scalar(p[:, 1:2], p[:, 0:1], MASKED * 1e-5, -1.0, ALU.max, ALU.mult).then_inc(peaked, 1)
                    if 1 <= i <= TILES:
                        j = i - 1
                        m = fx.mass[0:TILE, j]
                        dve.wait_ge(exped, T)
                        dve.tensor_scalar(m[:, 1:2], m[:, 0:1], 1e-30, None, ALU.max).then_inc(mass_own, 1)
                        dve.wait_ge(mass_own, T)
                        dve.reciprocal(m[:, 2:3], m[:, 1:2]).then_inc(inverted, 1)
                        for u in range(3):
                            dve.wait_ge(p_high, 30 * h + 3 * j + u + 1)
                            src, dst = unit_views(bank((3, 4, 7)[u]), pt[1], u, j)
                            high = unit_views(bank((3, 4, 7)[u]), pt[0], u, j)[1]
                            dve.tensor_tensor(dst, src, high, ALU.subtract).then_inc(p_low, 1)
                    if i >= 3:
                        j = i - 3
                        dve.wait_ge(half, 10 * h + j + 1)
                        dve.scalar_tensor_tensor(part[0:TILE, j, :], bank(j % 2)[0:TILE, 0:HDIM3], fx.mass[0:TILE, j, 2:3],
                                                 part[0:TILE, j, :], ALU.mult, ALU.add).then_inc(summed, 1)
            dve.wait_ge(joined, TILES * HEADS3)
            for i in range(TILES + 1):
                if i < TILES:
                    norm_stats(dve, fx, i % 2, fx.nodes[0:TILE, i, :], stat_own, i + 1, var_ready)
                if i >= 1:
                    row = fx.nodes[0:TILE, i - 1, :]
                    dve.wait_ge(std_ready, i)
                    norm_rows(dve, fx, (i - 1) % 2, row, row, rstd_own, i).then_inc(normed, 1)

        @block.scalar
        def _(act):
            act.wait_ge(counted, 16)
            act.wait_ge(loaded, ALL)

            def log(t):
                if t >= 2:
                    act.wait_ge(log_ready, t - 1)
                nc.scalar.activation(plain[0:TILE, t % 2, :], logs[0:TILE, t, 0:NODES], ACT.Ln,
                                     bias=fx.tiny[0:TILE, :]).then_inc(log_plain, 1)

            for t in range(TILES):
                act.wait_ge(turned, t + 1)
                nc.scalar.activation(x_t[:, :, cols(t)], bank(6 + t % 2)[:, 0:4 * TILE].rearrange("p (c n) -> p c n", c=4),
                                     ACT.Copy).then_inc(x_copied, 1)
            for t in range(TILES):
                log(t)
                act.wait_ge(v_sum, t + 1)
                nc.scalar.activation(values[0:TILE, t, :, 0, :], wf[0:TILE, t % 2, :].rearrange("p (h d) -> p h d", d=HDIM3),
                                     ACT.Copy).then_inc(v_high, 1)
            for j in range(CHUNKS):
                act.wait_ge(prod, j + 1)
                nc.scalar.activation(wx_t[:, j, :], region(j), ACT.Identity, bias=col_b[:, j:j + 1]).then_inc(copied, 1)
            for h in range(HEADS3):
                act.wait_ge(prod, CHUNKS + h + 1)
                nc.scalar.activation(spread[:, h, :], region(h), ACT.Copy).then_inc(copied, 1)
            act.wait_ge(copied, CHUNKS + HEADS3)
            act.wait_ge(v_low, TILES)
            nc.scalar.activation(fifth[0:TILE, 0, :], spread[0:TILE, 0, :], ACT.Copy, scale=0.2).then_inc(fifth_ready, 1)
            with act.Fori(0, HEADS3) as h:
                for i in range(LAG):
                    T = 10 * h + i
                    if i < TILES:
                        act.wait_ge(peaked, T + 1)
                        nc.scalar.activation(prob[0:TILE, i % 2, :], prob[0:TILE, i % 2, :], ACT.Exp,
                                             bias=fx.peak[0:TILE, i % 2, 1:2], accum_out=fx.mass[0:TILE, i, 0:1]).then_inc(exped, 1)
                    if 1 <= i <= TILES:
                        j = i - 1
                        for u in range(3):
                            act.wait_ge(p_turned, 30 * h + 3 * j + u + 1)
                            src, dst = unit_views(bank((3, 4, 7)[u]), pt[0], u, j)
                            nc.scalar.activation(dst, src, ACT.Copy).then_inc(p_high, 1)
                    if i == 5:
                        nxt = (h + 1) % HEADS3
                        nc.scalar.activation(fifth[0:TILE, bass.ds((h + 1) % 2, 1), :], spread[0:TILE, bass.ds(nxt, 1), :],
                                             ACT.Copy, scale=0.2).then_inc(fifth_ready, 1)
                    if i >= 3:
                        j = i - 3
                        act.wait_ge(pv, 10 * h + j + 1)
                        act.wait_ge(inverted, 10 * h + j + 1)
                        if j == 4:
                            act.wait_ge(joined, 10 * h + 1)
                        nc.scalar.activation(part[0:TILE, j, :], bank(j % 2)[0:TILE, HDIM3:2 * HDIM3], ACT.Copy,
                                             scale=fx.mass[0:TILE, j, 2:3]).then_inc(half, 1)
                act.wait_ge(joined, 10 * h + 4)
            for t in range(TILES):
                act.wait_ge(var_ready, t + 1)
                norm_std(nc, fx, t % 2, std_ready)

        @block.tensor
        def _(pe):
            for t in range(TILES):
                if t >= 2:
                    pe.wait_ge(x_copied, t - 1)
                for c in range(CHUNKS):
                    mm = pe.transpose(bank(6 + t % 2)[:, cols(c)], fx.nodes[0:TILE, t, c * 128:(c + 1) * 128],
                                      fx.ident[0:TILE, 0:TILE])
                mm.then_inc(turned, 1)
            pe.wait_ge(x_copied, TILES)
            pe.wait_ge(loaded, ALL)
            for t in range(TILES):
                if t >= 2:
                    pe.wait_ge(v_sum, t - 1)
                for c in range(CHUNKS):
                    mm = pe.matmul(bank(6 + t % 2)[0:TILE], x_t[:, c, cols(t)], w_sb[:, c, :], start=(c == 0),
                                   stop=(c == CHUNKS - 1))
                mm.then_inc(v_prod, 1)
            for j in range(CHUNKS):
                if j >= 2:
                    pe.wait_ge(copied, j - 1)
                for c in range(CHUNKS):
                    for a, z in CUTS:
                        mm = pe.matmul(region(j)[:, a:z], w_sb[:, c, j * 128:(j + 1) * 128], x_t[:, c, a:z],
                                       start=(c == 0), stop=(c == CHUNKS - 1))
                mm.then_inc(prod, 1)
            pe.wait_ge(copied, CHUNKS)
            pe.wait_ge(spread_ready, HEADS3)
            for h in range(HEADS3):
                if h >= 2:
                    pe.wait_ge(copied, CHUNKS + h - 1)
                for a, z in CUTS:
                    mm = pe.matmul(region(h)[:, a:z], wide[:, h, :], wx_t[:, h // 2, a:z], start=True, stop=True)
                mm.then_inc(prod, 1)
            pe.wait_ge(v_sum, TILES)
            for t in range(TILES):
                for c in range(CHUNKS):
                    mm = pe.matmul(bank(6)[0:TILE, t * HEADS3:(t + 1) * HEADS3], wx_t[:, c, cols(t)], a_tgt[:, c, :],
                                   start=(c == 0), stop=(c == CHUNKS - 1))
                mm.then_inc(r_prod, 1)
            pe.wait_ge(copied, CHUNKS + HEADS3)
            pe.wait_ge(r_ready, 1)
            with pe.Fori(0, HEADS3) as h:
                for i in range(LAG):
                    T = 10 * h + i
                    if 1 <= i <= TILES:
                        j = i - 1
                        pe.wait_ge(exped, T)
                        for u in range(3):
                            if j > 0:
                                pe.wait_ge(p_low, 30 * h + 3 * j + u - 2)
                            for d in range(4 * u, min(4 * u + 4, TILES)):
                                mm = pe.transpose(bank((3, 4, 7)[u])[0:TILE, cols(d - 4 * u)], prob[0:TILE, j % 2, cols(d)],
                                                  fx.ident[0:TILE, 0:TILE])
                            mm.then_inc(p_turned, 1)
                    if 2 <= i <= TILES + 1:
                        j = i - 2
                        pe.wait_ge(p_low, 30 * h + 3 * j + 3)
                        if j >= 2:
                            pe.wait_ge(summed, 10 * h + j - 1)
                        for d in range(TILES):
                            both = values[0:TILE, d, bass.ds(h, 1), :, :].rearrange("p a k n -> p (a k n)")
                            for k in range(2):
                                mm = pe.matmul(bank(j % 2)[0:TILE, 0:2 * HDIM3], pt[k][0:TILE, j % 2, d, :], both,
                                               start=(d == 0 and k == 0), stop=(d == TILES - 1 and k == 1))
                        mm.then_inc(pv, 1)
                pe.wait_ge(summed, 10 * h + 10)
                pe.wait_ge(p_low, 30 * h + 30)


_INS = ("x", "src", "dst", "edge_weight", "node_vec1", "L0_gnn_W", "L1_gnn_f_w1", "L1_gnn_f_b1", "L1_gnn_f_w2",
        "L1_gnn_f_b2", "L1_gnn_s1_w", "L1_gnn_s1_b", "L1_gnn_b1_w", "L1_gnn_b1_b", "L1_gnn_wq", "L1_gnn_bq", "L1_gnn_wk",
        "L1_gnn_bk", "L1_gnn_wv", "L1_gnn_bv", "L1_gnn_wo", "L1_gnn_bo", "L1_gnn_s2_w", "L1_gnn_s2_b", "L1_gnn_b2_w",
        "L1_gnn_b2_b", "L1_gnn_m_w1", "L1_gnn_m_b1", "L1_gnn_m_w2", "L1_gnn_m_b2", "L2_gnn_eps", "L2_gnn_W1", "L2_gnn_b1",
        "L2_gnn_gamma1", "L2_gnn_beta1", "L2_gnn_W2", "L2_gnn_b2", "L2_gnn_gamma2", "L2_gnn_beta2", "L3_gnn_Ws", "L3_gnn_Wb",
        "L3_gnn_a_w", "L3_gnn_a_b")


def graph_network(nc, t, out):
    fx = Fixed(nc)
    psum = nc.alloc_psum_tensor("psum", [128, 8 * BANK], F32)
    kept = nc.dram_tensor("layer_input_kept", [NODES, DIM], F32, kind="Internal").ap()
    spill = nc.dram_tensor("nodes_kept", [NODES, DIM], F32, kind="Internal").ap()
    count_rows = nc.dram_tensor("counts_kept", [WIDE, NODES], F32, kind="Internal").ap()

    def l1(name):
        return t["L1_gnn_" + name]

    def l2(name):
        return t["L2_gnn_" + name]

    edge_bands(nc, fx, psum, t["src"], t["dst"], t["edge_weight"], count_rows)
    first_layer(nc, fx, psum, t["x"], t["L0_gnn_W"], t["node_vec1"], l1("f_w1"), l1("f_b1"), l1("f_w2"), l1("f_b2"),
                l1("bq"), l1("bk"), l1("m_b1"), kept)
    second_layer(nc, fx, psum, spill, l1("wq"), l1("wk"), l1("wv"), l1("wo"), l1("m_w1"), l1("m_w2"), l1("bv"), l1("bo"),
                 l1("m_b2"), l1("s1_w"), l1("s1_b"), l1("b1_w"), l1("b1_b"), l1("s2_w"), l1("s2_b"), l1("b2_w"), l1("b2_b"))
    third_layer(nc, fx, psum, kept, count_rows, l2("eps"), l2("W1"), l2("b1"), l2("gamma1"), l2("beta1"), l2("W2"),
                l2("b2"), l2("gamma2"), l2("beta2"))
    fourth_layer(nc, fx, psum, count_rows, t["L3_gnn_Ws"], t["L3_gnn_Wb"], t["L3_gnn_a_w"], t["L3_gnn_a_b"], out)


def kernel(**inputs):
    import numpy as _np
    import concourse.bacc as _bacc
    from concourse import mybir as _mybir
    from concourse.bass_utils import run_bass_kernel_spmd as _run

    nc = _bacc.Bacc("TRN2", target_bir_lowering=False, num_devices=1)
    arrays, handles = {}, {}
    for name in _INS:
        a = _np.ascontiguousarray(inputs[name])
        arrays[f"in_{name}"] = a
        handles[name] = nc.dram_tensor(f"in_{name}", a.shape, _mybir.dt.from_np(a.dtype), kind="ExternalInput").ap()
    out = nc.dram_tensor("out_nodes", (NODES, DIM), _mybir.dt.float32, kind="ExternalOutput").ap()
    graph_network(nc, handles, out)
    r = _run(nc, [arrays], core_ids=[0])
    return r.results[0]["out_nodes"]
```

```python
from contextlib import ExitStack

import numpy as np

import concourse.bass as bass
from concourse import mybir

ALU = mybir.AluOpType
ACT = mybir.ActivationFunctionType
AX = mybir.AxisListType
F32 = mybir.dt.float32
F32R = mybir.dt.float32r
BF16 = mybir.dt.bfloat16
F16 = mybir.dt.float16
I32 = mybir.dt.int32

NODES, DIM, EDGES = 1250, 512, 20000
TILE = 125
TILES = NODES // TILE
ETILES = EDGES // TILE
PAIRS = ETILES // 2
SETS = 2
BAND = 32
BANDS = -(-NODES // BAND)
WIDE = BANDS * BAND
CHUNKS = DIM // 128
BANK = 512
CUTS = [(0, 512), (512, 1024), (1024, NODES)]
MASKED = -1.0e30
EPS = 1e-5
LAYERS1, HEADS1, HDIM1 = 4, 4, 128
COND, FREQS = 16, 32
HEADS3, HDIM3 = 8, 64
SBUF_BASE = 16512


WORK1 = 2 * TILES * WIDE * 4


def packer(nc, start):
    at = [start]

    def place(name, shape, dtype):
        size = int(np.prod(shape[1:])) * (2 if dtype in (BF16, F16) else 4)
        t = nc.alloc_sbuf_tensor_at(name, shape, dtype, offset=SBUF_BASE + at[0])
        at[0] += -(-size // 32) * 32
        return t

    return place


def edge_bands(nc, fx, psum, src, dst, weight, count_rows):
    with ExitStack() as ctx:
        def sem(name):
            return ctx.enter_context(nc.semaphore(name))

        place = packer(nc, WORK1)
        rows_i = place("edge_rows_int", [128, 2, 2, TILE], I32)
        rows_w = place("edge_rows_weight", [128, 2, TILE], F32)
        rows_f = place("edge_rows_float", [128, 3, 2, TILE], F32)
        cols = place("edge_columns", [128, 3, ETILES], F32)
        parts = place("weight_parts", [128, ETILES, 3], BF16)
        rest = place("weight_rest", [128, 2, ETILES], F32)
        ids_i = place("node_ids_int", [128, WIDE], I32)
        ids = place("node_ids", [128, WIDE], F16)
        onehot = place("onehot_source", [128, SETS, 2, NODES], BF16)
        station = place("onehot_band", [128, SETS, 2, 4, BAND], BF16)
        bands = place("band_products", [128, 2, NODES], F32)
        split = place("band_weight_parts", [128, 2, TILES, 3, BAND], F32)
        pair = place("band_weight_pair", [128, 2, TILES, BAND], F32)
        ext = place("tile_extremes", [128, 2, 2], F32)
        ext_b = place("tile_extremes_spread", [128, 2, 2, BANDS], F32)
        hit = place("band_meets_tile", [128, 3, ETILES], F32)
        band_at = place("band_start", [128, 2], F32)
        band_at_i = place("band_start_int", [128, 1], I32)
        up = place("pair_number_up", [128, 2, ETILES], F32)
        up_i = place("pair_number_int", [128, ETILES], I32)
        span = place("band_span_columns", [128, 4], F32)
        row = place("band_span_rows", [1, 6, BANDS], F32)
        row_i = place("band_span_registers", [1, 3, BANDS], I32)
        count_src, weight_src, ident, ones = fx.count_src, fx.weight_src, fx.ident, fx.ones

        loaded = sem("edges_loaded")
        consts = sem("constants_ready")
        floats = sem("edge_floats_ready")
        turned = sem("edges_turned")
        spread = sem("extremes_spread")
        colsok = sem("edge_columns_ready")
        own = sem("vector_setup_step")
        spanned = sem("spans_turned")
        ready = sem("spans_ready")
        band_half = sem("onehot_band_plain")
        oh_ready = sem("onehots_ready")
        oh_free = sem("onehots_used")
        band_copied = sem("band_copied")
        turn = sem("band_turned")
        unturn = sem("turned_copied")
        summed = sem("weights_summed")
        stored = [sem(f"counts_stored_{s}") for s in range(2)]

        def region(s):
            return psum[:, s * 3 * BANK:s * 3 * BANK + NODES]

        def unit(v):
            return psum[:, (6 + v % 2) * BANK:(7 + v % 2) * BANK]

        def load(eng, what, b):
            return eng.value_load(row_i[0:1, what, bass.ds(b, 1)], min_val=(0, 1, 0)[what],
                                  max_val=(BANDS + 1) * PAIRS)

        block = ctx.enter_context(nc.Block())

        @block.sync
        def _(sp):
            for a, v in enumerate((src, dst)):
                r = v.rearrange("(t e) -> t e", e=TILE)
                sp.dma_start(rows_i[:, a, 0, :], r[0:128, :]).then_inc(loaded, 16)
                sp.dma_start(rows_i[0:32, a, 1, :], r[128:ETILES, :]).then_inc(loaded, 16)
            r = weight.rearrange("(t e) -> t e", e=TILE)
            sp.dma_start(rows_w[:, 0, :], r[0:128, :]).then_inc(loaded, 16)
            sp.dma_start(rows_w[0:32, 1, :], r[128:ETILES, :]).then_inc(loaded, 16)

            def store(i):
                for s in range(2):
                    b = 2 * i + s
                    sp.wait_ge(band_copied, b + 1)
                    sp.dma_start(count_rows[bass.ds(b * BAND, BAND), :], bands[0:BAND, s, :]).then_inc(stored[s], 16)

            with sp.Fori(0, BANDS // 2) as i:
                store(i)
            for s in range(2):
                sp.wait_ge(stored[s], 16 * (BANDS // 2))

        @block.gpsimd
        def _(pool):
            pool.memset(ident[:, :], 0.0).then_inc(consts, 1)
            pool.wait_ge(consts, 1)
            pool.affine_select(out=ident[:, :], in_=ident[:, :], compare_op=ALU.not_equal, fill=1.0,
                               base=0, pattern=[[-1, 128]], channel_multiplier=1).then_inc(consts, 1)
            pool.memset(ones[:, :], 1.0).then_inc(consts, 1)
            pool.iota(ids_i[:, :], [[1, WIDE]], base=0, channel_multiplier=0).then_inc(consts, 1)
            pool.iota(band_at_i[:, :], [[0, 1]], base=0, channel_multiplier=BAND).then_inc(consts, 1)
            pool.iota(up_i[:, :], [[1, PAIRS], [0, 2]], base=0, channel_multiplier=0).then_inc(consts, 1)

            pool.memset(pair[0:1, 0, 0, 0:1], 0.0).then_inc(summed, 2)
            pool.wait_ge(summed, 2)
            with pool.Fori(0, BANDS // 2) as i:
                for s in range(2):
                    b = 2 * i + s
                    pool.wait_ge(unturn, 3 * b + 3)
                    nc.gpsimd.tensor_tensor(pair[0:TILE, s], split[0:TILE, s, :, 0, :], split[0:TILE, s, :, 1, :],
                                            ALU.add).then_inc(summed, 1)
                    pool.wait_ge(summed, 2 * b + 3)
                    nc.gpsimd.tensor_tensor(weight_src[0:TILE, :, bass.ds(b * BAND, BAND)], pair[0:TILE, s],
                                            split[0:TILE, s, :, 2, :], ALU.add).then_inc(summed, 1)

        @block.vector
        def _(dve):
            steps = [0]

            def step(ins):
                steps[0] += 1
                ins.then_inc(own, 1)
                dve.wait_ge(own, steps[0])

            v = nc.vector
            dve.wait_ge(loaded, 96)
            for a in range(3):
                for c, n in ((0, 128), (1, 32)):
                    src_rows = rows_i[0:n, a, c, :] if a < 2 else rows_w[0:n, c, :]
                    v.tensor_copy(rows_f[0:n, a, c, :], src_rows).then_inc(floats, 1)
            dve.wait_ge(floats, 6)
            for c, n in ((0, 128), (1, 32)):
                for e, op in ((0, ALU.min), (1, ALU.max)):
                    step(v.tensor_reduce(ext[0:n, e, c:c + 1], rows_f[0:n, 1, c, :], AX.X, op))
            dve.wait_ge(consts, 6)
            for c, n in ((0, 128), (1, 32)):
                for e in range(2):
                    v.tensor_scalar(ext_b[0:n, e, c, :], ones[0:n, 0:BANDS], ext[0:n, e, c:c + 1], None,
                                    ALU.mult).then_inc(spread, 1)
            v.tensor_copy(ids[:, :], ids_i[:, :])
            step(v.tensor_copy(band_at[:, 0:1], band_at_i[:, :]))
            v.tensor_scalar(band_at[:, 1:2], band_at[:, 0:1], float(BAND - 1), None, ALU.add)
            v.tensor_scalar(up[:, 0, :], up_i[:, :], 1.0, None, ALU.add)
            step(v.tensor_scalar(up[:, 1, :], up_i[:, :], -1.0, float(PAIRS), ALU.mult, ALU.add))
            dve.wait_ge(turned, 6)
            for a in range(3):
                step(v.tensor_copy(cols[0:TILE, a, :], psum[0:TILE, a * BANK:a * BANK + ETILES]))
            w, r = cols[0:TILE, 2, :], rest[0:TILE]
            step(v.tensor_copy(parts[0:TILE, :, 0], w))
            step(v.tensor_tensor(r[:, 0, :], w, parts[0:TILE, :, 0], ALU.subtract))
            step(v.tensor_copy(parts[0:TILE, :, 1], r[:, 0, :]))
            step(v.tensor_tensor(r[:, 1, :], r[:, 0, :], parts[0:TILE, :, 1], ALU.subtract))
            step(v.tensor_copy(parts[0:TILE, :, 2], r[:, 1, :]))
            dve.wait_ge(spread, 8)
            low = psum[0:BANDS, 3 * BANK:3 * BANK + ETILES]
            high = psum[0:BANDS, 4 * BANK:4 * BANK + ETILES]
            h = hit[0:BANDS]
            step(v.tensor_scalar(h[:, 0, :], high, band_at[0:BANDS, 0:1], None, ALU.is_ge))
            step(v.scalar_tensor_tensor(h[:, 1, :], low, band_at[0:BANDS, 1:2], h[:, 0, :], ALU.is_le, ALU.mult))
            step(v.tensor_tensor(h[:, 0, :], h[:, 1, :], up[0:BANDS, 1, :], ALU.mult))
            step(v.tensor_tensor(h[:, 2, :], h[:, 1, :], up[0:BANDS, 0, :], ALU.mult))
            step(v.tensor_reduce(span[0:BANDS, 2:3], h[:, 0, :], AX.X, ALU.max))
            step(v.tensor_reduce(span[0:BANDS, 3:4], h[:, 2, :], AX.X, ALU.max))
            step(v.tensor_scalar(span[0:BANDS, 2:3], span[0:BANDS, 2:3], -1.0, float(PAIRS), ALU.mult, ALU.add))
            step(v.tensor_scalar(span[0:BANDS, 0:1], span[0:BANDS, 2:3], float(PAIRS - 2), None, ALU.min))
            step(v.tensor_scalar(span[0:BANDS, 2:3], span[0:BANDS, 0:1], 2.0, None, ALU.add))
            v.tensor_tensor(span[0:BANDS, 1:2], span[0:BANDS, 2:3], span[0:BANDS, 3:4], ALU.max).then_inc(spanned, 1)
            dve.wait_ge(spanned, 3)
            for k in range(2):
                step(v.tensor_copy(row[0:1, k, :], psum[0:1, 5 * BANK + 64 * k:5 * BANK + 64 * k + BANDS]))
            step(v.tensor_tensor(row[0:1, 2, :], row[0:1, 1, :], row[0:1, 0, :], ALU.subtract))
            step(v.memset(row[0:1, 3, :], 1.0))
            step(v.tensor_tensor_scan(row[0:1, 4, :], row[0:1, 3, :], row[0:1, 2, :], 0.0, ALU.mult, ALU.add))
            step(v.tensor_tensor(row[0:1, 5, :], row[0:1, 4, :], row[0:1, 2, :], ALU.subtract))
            step(v.tensor_tensor(row[0:1, 2, :], row[0:1, 5, :], row[0:1, 0, :], ALU.subtract))
            step(v.tensor_scalar(row[0:1, 2, :], row[0:1, 2, :], float(PAIRS), None, ALU.add))
            step(v.tensor_copy(row_i[0:1, 0, :], row[0:1, 5, :]))
            step(v.tensor_copy(row_i[0:1, 1, :], row[0:1, 4, :]))
            step(v.tensor_copy(row_i[0:1, 2, :], row[0:1, 2, :]))
            v.memset(row[0:1, 3, :], 1.0).then_inc(ready, 1)

            with dve.Fori(0, BANDS // 2) as i:
                begin = load(dve, 0, 2 * i)
                for s in range(2):
                    b = 2 * i + s
                    end, skew = load(dve, 1, b), load(dve, 2, b)
                    with dve.Fori(begin, end) as n:
                        at = n % SETS
                        t = 2 * nc.s_assert_within(n + PAIRS - skew, 0, PAIRS - 1,
                                                   skip_runtime_bounds_check_because="n runs over the pairs of the band")
                        plain = station[0:TILE, bass.ds(at, 1), :, 0, :].rearrange("p a q j -> p (a q) j")
                        dve.wait_ge(oh_free, n + 1)
                        v.tensor_tensor(plain, ids[0:TILE, bass.ds(b * BAND, BAND)].unsqueeze(1).broadcast_to([TILE, 2, BAND]),
                                        cols[0:TILE, 1, bass.ds(t, 2)].unsqueeze(2).broadcast_to([TILE, 2, BAND]),
                                        ALU.is_equal).then_inc(band_half, 1)
                        v.tensor_scalar(onehot[0:TILE, bass.ds(at, 1), 0, :], ids[0:TILE, 0:NODES],
                                        cols[0:TILE, 0, bass.ds(t, 1)], None, ALU.is_equal).then_inc(oh_ready, 1)
                        dve.wait_ge(band_half, n + 1)
                        v.tensor_tensor(
                            station[0:TILE, bass.ds(at, 1), :, 1:4, :].rearrange("p a q k j -> p (a q) k j"),
                            plain.unsqueeze(2).broadcast_to([TILE, 2, 3, BAND]),
                            parts[0:TILE, bass.ds(t, 2), :].unsqueeze(3).broadcast_to([TILE, 2, 3, BAND]),
                            ALU.mult).then_inc(oh_ready, 1)
                        v.tensor_scalar(onehot[0:TILE, bass.ds(at, 1), 1, :], ids[0:TILE, 0:NODES],
                                        cols[0:TILE, 0, bass.ds(t + 1, 1)], None, ALU.is_equal).then_inc(oh_ready, 1)
                    begin = end

        @block.tensor
        def _(pe):
            pe.wait_ge(consts, 3)
            pe.wait_ge(floats, 6)
            for a in range(3):
                pe.transpose(psum[0:TILE, a * BANK:a * BANK + 128], rows_f[:, a, 0, :], ident[:, :]).then_inc(turned, 1)
                pe.transpose(psum[0:TILE, a * BANK + 128:a * BANK + ETILES], rows_f[0:32, a, 1, :],
                             ident[0:32, 0:32]).then_inc(turned, 1)
            pe.wait_ge(spread, 4)
            for e in range(2):
                for c, n in ((0, 128), (1, 32)):
                    pe.matmul(psum[0:BANDS, (3 + e) * BANK + 128 * c:(3 + e) * BANK + 128 * c + n], ext_b[0:n, e, c, :],
                              ident[0:n, 0:n], start=True, stop=True).then_inc(spread, 1)
            pe.wait_ge(spanned, 1)
            for k in range(2):
                mm = pe.matmul(psum[0:1, 5 * BANK + 64 * k:5 * BANK + 64 * k + BANDS], span[0:BANDS, k:k + 1],
                               ident[0:BANDS, 0:BANDS], start=True, stop=True)
                mm.then_inc(spanned, 1)
            pe.wait_ge(ready, 1)
            pe.wait_ge(oh_free, SETS)

            def product(s, n, start):
                at = n % SETS
                for q in range(2):
                    pe.wait_ge(oh_ready, 3 * n + 2 + q)
                    for a, z in CUTS:
                        mm = pe.matmul(region(s)[:, a:z], station[0:TILE, bass.ds(at, 1), q, :, :].rearrange("p a k j -> p (a k j)"),
                                       onehot[0:TILE, bass.ds(at, 1), q, a:z], start=start and q == 0, stop=True,
                                       skip_group_check=True)
                mm.then_inc(oh_free, 1)

            def turn_band(b, s, first):
                pe.wait_ge(band_copied, b + 1)
                for u in range(3):
                    if u >= 2 or not first:
                        pe.wait_ge(unturn, 3 * b + u - 1)
                    for j in range(4 * u, min(4 * u + 4, TILES)):
                        mm = pe.transpose(unit(s + u)[0:TILE, (j % 4) * 128:(j % 4) * 128 + 128],
                                          bands[:, s, j * TILE:(j + 1) * TILE], ident[:, :])
                    mm.then_inc(turn, 1)

            def pair_of(i, first_pair):
                begin = load(pe, 0, 2 * i)
                for s in range(2):
                    end = load(pe, 1, 2 * i + s)
                    product(s, begin, True)
                    if s == 1 or not first_pair:
                        turn_band(2 * i + s - 1, 1 - s, first_pair)
                    with pe.Fori(begin + 1, end) as n:
                        product(s, n, False)
                    begin = end

            pair_of(0, True)
            with pe.Fori(1, BANDS // 2) as i:
                pair_of(i, False)
            turn_band(BANDS - 1, 1, False)

        @block.scalar
        def _(act):
            act.wait_ge(consts, 3)
            for k in range(SETS):
                nc.scalar.activation(bands[0:1, 0, k:k + 1], ones[0:1, 0:1], ACT.Copy).then_inc(oh_free, 1)
            act.wait_ge(ready, 1)

            def copy_units(b, s, wait_sums):
                if wait_sums:
                    act.wait_ge(summed, 2 * b)
                for u in range(3):
                    act.wait_ge(turn, 3 * b + u + 1)
                    n = min(4, TILES - 4 * u)
                    view = unit(s + u)[0:TILE, 0:n * 128].rearrange("p (j k d) -> p j k d", k=4, d=BAND)
                    nc.scalar.activation(count_src[0:TILE, 4 * u:4 * u + n, bass.ds(b * BAND, BAND)], view[:, :, 0, :],
                                         ACT.Copy)
                    nc.scalar.activation(split[0:TILE, s, 4 * u:4 * u + n, :, :], view[:, :, 1:4, :],
                                         ACT.Copy).then_inc(unturn, 1)

            def pair_of(i, first_pair):
                for s in range(2):
                    b = 2 * i + s
                    end = load(act, 1, b)
                    if s == 1 or not first_pair:
                        copy_units(b - 1, 1 - s, not first_pair)
                    if not first_pair:
                        act.wait_ge(stored[s], 16 * i)
                        act.wait_ge(turn, 3 * b - 3)
                    act.wait_ge(oh_free, end + SETS)
                    nc.scalar.activation(bands[:, s, :], region(s), ACT.Copy).then_inc(band_copied, 1)

            pair_of(0, True)
            with act.Fori(1, BANDS // 2) as i:
                pair_of(i, False)
            copy_units(BANDS - 1, 1, True)


PLANE = CHUNKS * NODES * 4
LOGS_AT = 0
TURNED_AT = LOGS_AT + TILES * WIDE * 4
SLOT_A_AT = TURNED_AT + 2 * PLANE
SLOT_B_AT = SLOT_A_AT + PLANE
VALUES_AT = SLOT_B_AT + 4 * 5024
WORK_AT = VALUES_AT + TILES * DIM * 4
WORK_SIZE = 33280
HEADW_AT = WORK_AT + WORK_SIZE
CONDS_AT = HEADW_AT + 8192
FIXED_AT = CONDS_AT + 5024 + 4096 + 4096 + 4096
ROW_TAIL = 2 * CHUNKS * DIM * 4
PI = float(np.pi)


class Fixed:

    def __init__(self, nc):
        place = packer(nc, FIXED_AT)
        self.passed = nc.alloc_semaphore("waits_passed")
        self.ident = place("identity", [128, 128], F32)
        self.ones = place("all_ones", [128, 128], F32)
        self.eps = place("norm_eps", [128, 1], F32)
        self.tiny = place("log_floor", [128, 1], F32)
        self.stats = place("norm_stats", [128, 2, 6], F32)
        self.moments = place("norm_moments", [128, 2, 2], F32)
        self.std = place("norm_std", [128, 2], F32)
        self.rstd = place("norm_rstd", [128, 2], F32)
        self.shift = place("norm_shift", [128, 2], F32)
        self.qkb = place("head_biases", [128, 3, LAYERS1 * HEADS1], F32)
        self.peak = place("row_peaks", [128, 2, 2], F32)
        self.mass = place("row_masses", [128, TILES, 3], F32)
        self.nodes = packer(nc, WORK_AT)("nodes", [128, TILES, DIM], F32)
        self.count_src = packer(nc, LOGS_AT)("counts", [128, TILES, WIDE], F32)
        self.count_dst = packer(nc, LOGS_AT)("counts_by_target", [128, TILES, WIDE], F32)
        self.weight_src = packer(nc, TURNED_AT)("weights", [128, TILES, WIDE], F32)
        self.cond = packer(nc, CONDS_AT)("condition_parts", [96, NODES], F32R)


def wait_apart(eng, fx, sem, value):
    eng.wait_ge(sem, value)
    eng.sem_inc(fx.passed, 1)


def norm_stats(dve, fx, at, rows, own, own_value, var_ready):
    dve.bn_stats(fx.stats[0:TILE, at, :], rows).then_inc(own, 1)
    wait_apart(dve, fx, own, own_value)
    dve.bn_aggr(fx.moments[0:TILE, at, :], fx.stats[0:TILE, at, :]).then_inc(var_ready, 1)


def norm_std(nc, fx, at, std_ready):
    nc.scalar.activation(fx.std[0:TILE, at:at + 1], fx.moments[0:TILE, at, 1:2], ACT.Sqrt,
                         bias=fx.eps[0:TILE, :]).then_inc(std_ready, 1)


def norm_rows(dve, fx, at, out, rows, own, own_value):
    dve.reciprocal(fx.rstd[0:TILE, at:at + 1], fx.std[0:TILE, at:at + 1]).then_inc(own, 1)
    dve.wait_ge(own, own_value)
    return dve.tensor_scalar(out, rows, fx.moments[0:TILE, at, 0:1], fx.rstd[0:TILE, at:at + 1],
                             ALU.subtract, ALU.mult)


def log_counts(dve, counts, logs, scale, ready, own, steps):
    steps[0] += 1
    dve.tensor_scalar(logs, logs, scale, None, ALU.mult).then_inc(own, 1)
    dve.wait_ge(own, steps[0])
    steps[0] += 1
    dve.tensor_scalar(counts, counts, 0.0, MASKED, ALU.is_equal, ALU.mult).then_inc(own, 1)
    dve.wait_ge(own, steps[0])
    dve.tensor_tensor(counts, counts, logs, ALU.add).then_inc(ready, 1)


def first_layer(nc, fx, psum, x, w0, noise, f_w1, f_b1, f_w2, f_b2, bq, bk, b1, kept):
    with ExitStack() as ctx:
        def sem(name):
            return ctx.enter_context(nc.semaphore(name))

        place = packer(nc, TURNED_AT + TILES * WIDE * 4)
        sum_t = place("edge_sums_turned", [128, CHUNKS, NODES], F32)
        w_sb = place("first_weight", [128, CHUNKS, DIM], F32)
        place = packer(nc, VALUES_AT)
        phase = place("noise_phase", [2 * FREQS, NODES], F32)
        turns = place("noise_turns", [2 * FREQS, NODES], F32)
        inner = place("condition_inner", [COND, NODES], F32)
        plain = place("condition_plain", [96, NODES], F32)
        logs = packer(nc, WORK_AT + TILES * DIM * 4)("plain_logs", [128, 2, NODES], F32)
        place = packer(nc, HEADW_AT)
        fw1 = place("noise_weight_1", [2 * FREQS, COND], F32)
        fw2 = place("noise_weight_2", [COND, 96], F32)
        fb1 = place("noise_bias_1", [COND, 1], F32)
        fb2 = place("noise_bias_2", [96, 1], F32)
        lane_i = place("lane_number_int", [2 * FREQS, 1], I32)
        lane = place("lane_number", [2 * FREQS, 4], F32)

        loaded = sem("x_loaded")
        w_loaded = sem("first_weight_loaded")
        n_loaded = sem("noise_loaded")
        zeroed = sem("noise_buffers_set")
        small = sem("biases_loaded")
        own = sem("noise_step")
        emb_ready = sem("embedding_ready")
        inner_prod = sem("inner_product")
        inner_ready = sem("inner_ready")
        cond_prod = sem("condition_product")
        cond_ready = sem("condition_plain_ready")
        log_plain = sem("logs_plain")
        log_ready = sem("logs_ready")
        sums = sem("edge_sums")
        sums_ready = sem("edge_sums_copied")
        prod = sem("first_products")
        added = sem("relu_added")
        stat_own = sem("stats_step")
        var_ready = sem("variance_ready")
        std_ready = sem("std_ready")
        rstd_own = sem("rstd_step")
        normed = sem("nodes_normed")
        stored = sem("nodes_kept")

        block = ctx.enter_context(nc.Block())

        @block.sync
        def _(sp):
            xr = x.rearrange("(t p) d -> p t d", p=TILE)
            sp.dma_start(fx.nodes[0:TILE], xr).then_inc(loaded, 16)
            sp.wait_ge(zeroed, 2)
            sp.dma_start(phase[:, :], noise.rearrange("n a -> a n").broadcast_to([2 * FREQS, NODES])).then_inc(n_loaded, 16)
            sp.dma_start(fw1[:, :], f_w1).then_inc(n_loaded, 16)
            sp.dma_start(fb1[:, :], f_b1.rearrange("(p a) -> p a", a=1)).then_inc(n_loaded, 16)
            for g in range(3):
                sp.dma_start(fw2[:, 32 * g:32 * g + COND], f_w2).then_inc(n_loaded, 16)
                sp.dma_start(fb2[32 * g:32 * g + COND, :], f_b2.rearrange("(p a) -> p a", a=1)).then_inc(n_loaded, 16)
            sp.dma_start(w_sb[:, :, :], w0.rearrange("(c p) n -> p c n", p=128)).then_inc(w_loaded, 16)
            for k, v in enumerate((bq, bk, b1)):
                sp.dma_start(fx.qkb[:, k, :], v.rearrange("i (c p) -> p (i c)", p=128),
                             allow_slow_non_contiguous=True).then_inc(small, 16)
            sp.wait_ge(normed, TILES)
            sp.dma_start(kept.rearrange("(t p) d -> p t d", p=TILE), fx.nodes[0:TILE]).then_inc(stored, 16)
            sp.wait_ge(small, 48)
            sp.wait_ge(stored, 16)

        @block.gpsimd
        def _(pool):
            pool.memset(fw2[:, :], 0.0).then_inc(zeroed, 1)
            pool.memset(fb2[:, :], 1.0).then_inc(zeroed, 1)
            pool.memset(fx.eps[:, :], EPS).then_inc(zeroed, 1)
            pool.memset(fx.tiny[:, :], 2.0 ** -60).then_inc(zeroed, 1)
            pool.iota(lane_i[:, :], [[0, 1]], base=0, channel_multiplier=1).then_inc(zeroed, 1)

        @block.vector
        def _(dve):
            steps = [0]

            def step(ins):
                steps[0] += 1
                ins.then_inc(own, 1)
                dve.wait_ge(own, steps[0])

            dve.wait_ge(zeroed, 5)
            step(dve.tensor_copy(lane[:, 3:4], lane_i[:, :]))
            rate = 2.0 * PI / 16.0
            dve.tensor_scalar(lane[0:FREQS, 0:1], lane[0:FREQS, 3:4], 1.0, rate, ALU.add, ALU.mult)
            dve.tensor_scalar(lane[FREQS:, 0:1], lane[FREQS:, 3:4], 1.0 - FREQS, rate, ALU.add, ALU.mult)
            dve.memset(lane[0:FREQS, 1:2], 0.0)
            dve.memset(lane[FREQS:, 1:2], 0.25)
            dve.memset(lane[0:FREQS, 2:3], 0.0)
            step(dve.memset(lane[FREQS:, 2:3], PI / 2))
            dve.wait_ge(n_loaded, 144)
            step(dve.tensor_scalar(phase[:, :], phase[:, :], lane[:, 0:1], None, ALU.mult))
            step(dve.tensor_scalar(turns[:, :], phase[:, :], 0.5 / PI, lane[:, 1:2], ALU.mult, ALU.add))
            step(dve.tensor_scalar(turns[:, :], turns[:, :], 12582912.0, None, ALU.add))
            step(dve.tensor_scalar(turns[:, :], turns[:, :], -12582912.0, None, ALU.add))
            step(dve.scalar_tensor_tensor(phase[:, :], turns[:, :], -6.28125, phase[:, :], ALU.mult, ALU.add))
            step(dve.scalar_tensor_tensor(phase[:, :], turns[:, :], -(2 * PI - 6.28125), phase[:, :], ALU.mult, ALU.add))
            step(dve.tensor_scalar(phase[:, :], phase[:, :], lane[:, 2:3], 3.1415925, ALU.add, ALU.min))
            dve.tensor_scalar(phase[:, :], phase[:, :], -3.1415925, None, ALU.max).then_inc(emb_ready, 1)
            dve.wait_ge(cond_ready, 1)
            step(dve.tensor_copy(fx.cond[:, :], plain[:, :]))
            step(dve.tensor_tensor(fx.cond[64:96, :], plain[64:96, :], fx.cond[64:96, :].bitcast(F32), ALU.subtract))
            for t in range(TILES):
                counts = fx.count_src[0:TILE, t, 0:NODES]
                dve.wait_ge(log_plain, t + 1)
                log_counts(dve, counts, logs[0:TILE, t % 2, :], HDIM1 ** 0.5, log_ready, own, steps)

            dve.wait_ge(loaded, 16)
            for i in range(TILES + 1):
                if i < TILES:
                    row = fx.nodes[0:TILE, i, :]
                    dve.wait_ge(prod, i + 1)
                    dve.scalar_tensor_tensor(row, psum[0:TILE, (6 + i % 2) * BANK:(7 + i % 2) * BANK], 0.0, row,
                                             ALU.max, ALU.add).then_inc(added, 1)
                    dve.wait_ge(added, i + 1)
                    norm_stats(dve, fx, i % 2, row, stat_own, i + 1, var_ready)
                if i >= 1:
                    row = fx.nodes[0:TILE, i - 1, :]
                    dve.wait_ge(std_ready, i)
                    norm_rows(dve, fx, (i - 1) % 2, row, row, rstd_own, i).then_inc(normed, 1)

        @block.scalar
        def _(act):
            act.wait_ge(emb_ready, 1)
            nc.scalar.activation(turns[:, :], phase[:, :], ACT.Sin).then_inc(emb_ready, 1)
            act.wait_ge(inner_prod, 1)
            nc.scalar.activation(inner[:, :], psum[0:COND, 3 * BANK:3 * BANK + NODES], ACT.Silu,
                                 bias=fb1[:, :]).then_inc(inner_ready, 1)
            act.wait_ge(cond_prod, 1)
            nc.scalar.activation(plain[:, :], psum[0:96, 0:NODES], ACT.Identity, bias=fb2[:, :]).then_inc(cond_ready, 1)
            for t in range(TILES):
                if t >= 2:
                    act.wait_ge(log_ready, t - 1)
                nc.scalar.activation(logs[0:TILE, t % 2, :], fx.count_src[0:TILE, t, 0:NODES], ACT.Ln,
                                     bias=fx.tiny[0:TILE, :]).then_inc(log_plain, 1)
            for c in range(CHUNKS):
                act.wait_ge(sums, c + 1)
                nc.scalar.activation(sum_t[:, c, :], psum[:, (c % 2) * 3 * BANK:(c % 2) * 3 * BANK + NODES],
                                     ACT.Copy).then_inc(sums_ready, 1)
            for t in range(TILES):
                act.wait_ge(var_ready, t + 1)
                norm_std(nc, fx, t % 2, std_ready)

        @block.tensor
        def _(pe):
            pe.wait_ge(n_loaded, 144)
            pe.wait_ge(emb_ready, 2)
            for a, z in CUTS:
                mm = pe.matmul(psum[0:COND, 3 * BANK + a:3 * BANK + z], fw1[:, :], turns[:, a:z], start=True, stop=True)
            mm.then_inc(inner_prod, 1)
            pe.wait_ge(inner_ready, 1)
            for a, z in CUTS:
                mm = pe.matmul(psum[0:96, a:z], fw2[:, :], inner[:, a:z], start=True, stop=True)
            mm.then_inc(cond_prod, 1)
            pe.wait_ge(loaded, 16)
            pe.wait_ge(cond_ready, 1)
            for c in range(CHUNKS):
                if c >= 2:
                    pe.wait_ge(sums_ready, c - 1)
                for k in range(TILES):
                    for a, z in CUTS:
                        mm = pe.matmul(psum[:, (c % 2) * 3 * BANK + a:(c % 2) * 3 * BANK + z],
                                       fx.nodes[0:TILE, k, c * 128:(c + 1) * 128], fx.weight_src[0:TILE, k, a:z],
                                       start=(k == 0), stop=(k == TILES - 1))
                mm.then_inc(sums, 1)
            pe.wait_ge(w_loaded, 16)
            pe.wait_ge(sums_ready, CHUNKS)
            for t in range(TILES):
                if t >= 2:
                    pe.wait_ge(added, t - 1)
                for c in range(CHUNKS):
                    mm = pe.matmul(psum[0:TILE, (6 + t % 2) * BANK:(7 + t % 2) * BANK],
                                   sum_t[:, c, t * TILE:(t + 1) * TILE], w_sb[:, c, :], start=(c == 0), stop=(c == CHUNKS - 1))
                mm.then_inc(prod, 1)




def three(pe, out, left, right, first, last):
    (lh, ll), (rh, rl) = left, right
    pe.matmul(out, lh, rh, start=first, stop=False, skip_group_check=True)
    pe.matmul(out, lh, rl, start=False, stop=False, skip_group_check=True)
    return pe.matmul(out, ll, rh, start=False, stop=last, skip_group_check=True)


def second_layer(nc, fx, psum, spill, wq, wk, wv, wo, m1, m2, bv, bo, b2, s1, sb1, t1, tb1, s2, sb2, t2, tb2):
    with ExitStack() as ctx:
        def sem(name):
            return ctx.enter_context(nc.semaphore(name))

        place = packer(nc, TURNED_AT)
        y_h = place("turned_high", [128, CHUNKS, NODES], F32R)
        y_l = place("turned_low", [128, CHUNKS, NODES], F32R)
        place = packer(nc, SLOT_A_AT)
        wa = [place(f"slot_a_{p}", [128, CHUNKS, DIM], F32R) for p in ("high", "low")]
        row_a = place("slot_a_bias_row", [128, DIM], F32)
        attended = packer(nc, SLOT_A_AT)("attended_turned", [128, HEADS1, NODES], F32)
        place = packer(nc, SLOT_B_AT)
        wb = [place(f"slot_b_{p}", [128, CHUNKS, DIM], F32R) for p in ("high", "low")]
        row_b = place("slot_b_bias_row", [128, DIM], F32)
        place = packer(nc, SLOT_B_AT)
        qk = [[place(f"{w}_{p}", [128, NODES], F32R) for p in ("high", "low")] for w in ("queries", "keys")]
        place = packer(nc, VALUES_AT)
        v_h = place("values_high", [128, TILES, DIM], BF16)
        v_l = place("values_low", [128, TILES, DIM], BF16)
        hidden = packer(nc, VALUES_AT)("hidden_rows", [128, 2, CHUNKS, 250], F32)
        place = packer(nc, WORK_AT + TILES * DIM * 4)
        xn = place("normed_rows", [128, 2, DIM], F32)
        yr = place("conditioned_rows", [128, 2, DIM], F32)
        vf = place("value_rows", [128, 2, DIM], F32)
        place = packer(nc, WORK_AT)
        prob = place("probabilities", [128, 2, NODES], F32)
        pt_h = place("turned_probabilities_high", [128, 2, TILES, 250], BF16)
        pt_l = place("turned_probabilities_low", [128, 2, TILES, 250], BF16)
        mass_rows = place("inverse_mass_rows", [128, 2, 250], F32)
        mass_diag = place("inverse_mass_diagonal", [128, 2, TILE], F32)
        hw = packer(nc, HEADW_AT)("head_weights", [128, 2, 2, CHUNKS, HDIM1], F32R)
        place = packer(nc, CONDS_AT + 5024)
        sw = place("condition_weight_parts", [96, 2, DIM], F32R)
        raw = place("condition_weights", [32, 2, DIM], F32)
        stage = place("weight_stage", [128, 2, DIM], F32)
        pair_y = (y_h, y_l)

        def sem(name):
            return ctx.enter_context(nc.semaphore("L1_" + name))

        raw_loaded = sem("raw_loaded")
        conds_ready = sem("conds_ready")
        cond_own = sem("cond_own")
        stage_w0 = sem("stage_w0")
        stage_w1 = sem("stage_w1")
        split_high = sem("split_high")
        w_ready = sem("w_ready")
        bias_loaded = sem("bias_row_loaded")
        x_spilled = sem("x_spilled")
        x_back = sem("x_back")
        mod_ready = sem("mod_ready")
        stats_own = sem("stats_own")
        var_ready = sem("var_ready")
        std_ready = sem("std_ready")
        finish_own = sem("finish_own")
        rstd_own = sem("rstd_own")
        shift_ready = sem("norm_shift_ready")
        xn_ready = sem("normed_rows_ready")
        y_ready = sem("y_ready")
        y_turned = sem("y_turned")
        y_high = sem("y_high")
        y_low = sem("y_low")
        v_prod = sem("v_prod")
        v_copied = sem("v_copied")
        v_sum = sem("v_sum")
        v_high = sem("v_high")
        v_low = sem("v_low")
        proj_prod = sem("proj_prod")
        proj_high = sem("proj_high")
        proj_low = sem("proj_low")
        qk_done = sem("qk_done")
        scored = sem("scored")
        peaked = sem("peaked")
        exped = sem("exped")
        mass_own = sem("mass_own")
        inverted = sem("inverted")
        diagonal = sem("diagonal")
        rows_prod = sem("rows_prod")
        rows_copied = sem("rows_copied")
        turned = sem("turned")
        pt_high = sem("pt_high")
        pt_low = sem("pt_low")
        pv_done = sem("pv_done")
        o_done = sem("o_done")
        att_high = sem("att_high")
        att_low = sem("att_low")
        o_prod = sem("o_prod")
        x_biased = sem("x_biased")
        residual = sem("residual")
        h_prod = sem("h_prod")
        h_rows = sem("h_rows")
        h_high = sem("h_high")
        h_low = sem("h_low")
        m_prod = sem("m_prod")
        x_done = sem("x_done")
        x2_biased = sem("x2_biased")
        stage_loaded = [stage_w0, stage_w1]
        GROUPS = TILES // 2
        LAG_STEPS = TILES + 3

        def bank(n):
            return psum[:, n * BANK:(n + 1) * BANK]

        def cols(t):
            return slice(t * TILE, (t + 1) * TILE)

        def unit_views(source, pt, u, j):
            n = min(4, TILES - 4 * u)
            return (source[0:TILE, 0:n * TILE].rearrange("p (d n) -> p d n", d=n),
                    pt[0:TILE, (j // 2) % 2, 4 * u:4 * u + n, cols(j % 2)])

        def row_scores(dve, scores, i, T, scale):
            p = fx.peak[0:TILE, i % 2]
            dve.tensor_tensor_reduce(prob[0:TILE, i % 2, :], scores, fx.count_src[0:TILE, i, 0:NODES], scale, MASKED,
                                     ALU.add, ALU.max, p[:, 0:1]).then_inc(scored, 1)
            dve.wait_ge(scored, T + 1)
            dve.tensor_scalar(p[:, 1:2], p[:, 0:1], MASKED * 1e-5, -1.0, ALU.max, ALU.mult).then_inc(peaked, 1)

        def row_mass(dve, i, T):
            m = fx.mass[0:TILE, i]
            dve.wait_ge(exped, T + 1)
            dve.tensor_scalar(m[:, 1:2], m[:, 0:1], 1e-30, None, ALU.max).then_inc(mass_own, 1)
            dve.wait_ge(mass_own, T + 1)
            dve.reciprocal(m[:, 2:3], m[:, 1:2]).then_inc(inverted, 1)

        block = ctx.enter_context(nc.Block())

        @block.sync
        def _(sp):
            def weight(b, i, src):
                sp.wait_ge(w_ready, 24 * b + i + 1)
                sp.dma_start(stage[:, i % 2, :] if len(src.shape) == 2 else
                             stage[:, i % 2, :].rearrange("p (c n) -> p c n", c=CHUNKS), src).then_inc(stage_loaded[i % 2], 16)

            def rows_of(w, b, c):
                return w[bass.ds(b, 1), c * 128:(c + 1) * 128, :].rearrange("a p n -> (a p) n")

            def head_of(w, b, h):
                return w[bass.ds(b, 1), :, h * HDIM1:(h + 1) * HDIM1].rearrange("a (c p) n -> p (a c) n", p=128)

            def condition(b, mats, ph):
                if ph == 1:
                    sp.wait_ge(conds_ready, 2 * b + 1)
                for k, (w, bias) in enumerate(mats):
                    sp.dma_start(raw[0:COND, k, :], w[bass.ds(b, 1)].rearrange("a c n -> (a c) n")).then_inc(raw_loaded, 16)
                    sp.dma_start(raw[COND:COND + 1, k, :], bias[bass.ds(b, 1), :]).then_inc(raw_loaded, 16)

            def bias_row(out, v, b):
                sp.dma_start(out[:, :], v[bass.ds(b, 1), :].broadcast_to([128, DIM])).then_inc(bias_loaded, 16)

            sp.wait_ge(w_ready, 2)
            with sp.Fori(0, LAYERS1) as b:
                condition(b, ((s1, sb1), (t1, tb1)), 0)
                for i in range(4):
                    weight(b, i, rows_of(wv, b, i))
                bias_row(row_b, bv, b)
                for i in (0, 1):
                    weight(b, 4 + i, head_of((wq, wk)[i], b, 0))
                sp.wait_ge(y_ready, 20 * b + 10)
                sp.dma_start(spill.rearrange("(t p) d -> p t d", p=TILE), fx.nodes[0:TILE]).then_inc(x_spilled, 16)
                for i in range(2, 8):
                    weight(b, 4 + i, head_of((wq, wk)[i % 2], b, i // 2))
                    if i == 3:
                        condition(b, ((s2, sb2), (t2, tb2)), 1)
                for i in (0, 1):
                    weight(b, 12 + i, rows_of(wo, b, i))
                sp.wait_ge(qk_done, 40 * b + 40)
                bias_row(row_b, bo, b)
                sp.wait_ge(o_done, 20 * b + 20)
                sp.wait_ge(x_spilled, 16 * b + 16)
                sp.dma_start(fx.nodes[0:TILE], spill.rearrange("(t p) d -> p t d", p=TILE)).then_inc(x_back, 16)
                for i in (2, 3):
                    weight(b, 12 + i, rows_of(wo, b, i))
                for i in (0, 1):
                    weight(b, 16 + i, rows_of(m1, b, i))
                sp.wait_ge(att_low, 4 * b + 4)
                sp.wait_ge(bias_loaded, 48 * b + 32)
                bias_row(row_a, b2, b)
                for i in (2, 3):
                    weight(b, 16 + i, rows_of(m1, b, i))
                for i in range(4):
                    weight(b, 20 + i, rows_of(m2, b, i))

        @block.gpsimd
        def _(pool):
            def split(b, i, high, low):
                st = stage[:, i % 2, :]
                wait_apart(pool, fx, stage_loaded[i % 2], 16 * (12 * b + i // 2 + 1))
                if len(high.shape) == 3:
                    st = st.rearrange("p (c n) -> p c n", c=CHUNKS)
                nc.gpsimd.tensor_copy(high, st).then_inc(split_high, 1)
                pool.wait_ge(split_high, 24 * b + i + 1)
                nc.gpsimd.tensor_tensor(low, st, high.bitcast(F32), ALU.subtract).then_inc(w_ready, 1)

            def condition(b, ph):
                wait_apart(pool, fx, raw_loaded, 64 * (2 * b + ph + 1))
                nc.gpsimd.tensor_copy(sw[64:96], raw[:, :, :]).then_inc(cond_own, 1)
                wait_apart(pool, fx, cond_own, 4 * b + 2 * ph + 1)
                nc.gpsimd.tensor_copy(sw[0:32], raw[:, :, :]).then_inc(cond_own, 1)
                pool.wait_ge(cond_own, 4 * b + 2 * ph + 2)
                nc.gpsimd.tensor_tensor(sw[32:64], raw[:, :, :], sw[0:32].bitcast(F32), ALU.subtract).then_inc(conds_ready, 1)
                pool.wait_ge(conds_ready, 2 * b + ph + 1)

            pool.memset(raw[:, :, :], 0.0).then_inc(w_ready, 1)
            pool.memset(mass_diag[0:1, 0, 0:1], 0.0).then_inc(w_ready, 1)
            pool.wait_ge(w_ready, 2)
            with pool.Fori(0, LAYERS1) as b:
                condition(b, 0)
                for i in range(4):
                    split(b, i, wa[0][:, i, :], wa[1][:, i, :])
                for i in (0, 1):
                    split(b, 4 + i, hw[:, 0, i], hw[:, 1, i])
                pool.wait_ge(bias_loaded, 48 * b + 16)
                for i in range(TILES + 1):
                    if i < TILES:
                        pool.wait_ge(v_copied, 10 * b + i + 1)
                        nc.gpsimd.tensor_tensor(vf[0:TILE, i % 2, :], vf[0:TILE, i % 2, :], row_b[0:TILE, :],
                                                ALU.add).then_inc(v_sum, 1)
                    if i >= 1:
                        t = i - 1
                        pool.wait_ge(v_high, 10 * b + t + 1)
                        nc.gpsimd.tensor_tensor(v_l[0:TILE, t, :], vf[0:TILE, t % 2, :], v_h[0:TILE, t, :],
                                                ALU.subtract).then_inc(v_low, 1)
                for h in range(HEADS1):
                    for j in range(TILES):
                        T = 40 * b + 10 * h + j
                        if h > 0 or j >= 2:
                            pool.wait_ge(rows_prod, T - 1)
                        wait_apart(pool, fx, inverted, T + 1)
                        nc.gpsimd.tensor_scalar(mass_diag[0:TILE, j % 2, :], fx.ident[0:TILE, 0:TILE],
                                                fx.mass[0:TILE, j, 2:3], None, ALU.mult).then_inc(diagonal, 1)
                        if h < HEADS1 - 1 and j in (3, 6):
                            i = 6 + 2 * h + (j == 6)
                            pool.wait_ge(proj_prod, 24 * b + 6 * h + 6)
                            split(b, i, hw[:, 0, i % 2], hw[:, 1, i % 2])
                    if h == 1:
                        pool.wait_ge(mod_ready, 20 * b + 10)
                        pool.wait_ge(diagonal, 40 * b + 20)
                        condition(b, 1)
                pool.wait_ge(qk_done, 40 * b + 40)
                for i in range(4):
                    split(b, 12 + i, wb[0][:, i, :], wb[1][:, i, :])
                pool.wait_ge(bias_loaded, 48 * b + 32)
                pool.wait_ge(x_back, 16 * b + 16)
                for t in range(TILES):
                    nc.gpsimd.tensor_tensor(fx.nodes[0:TILE, t, :], fx.nodes[0:TILE, t, :], row_b[0:TILE, :],
                                            ALU.add).then_inc(x_biased, 1)
                pool.wait_ge(att_low, 4 * b + 4)
                for i in range(4):
                    split(b, 16 + i, wa[0][:, i, :], wa[1][:, i, :])
                pool.wait_ge(o_prod, 10 * b + 10)
                for i in range(4):
                    split(b, 20 + i, wb[0][:, i, :], wb[1][:, i, :])
                pool.wait_ge(bias_loaded, 48 * b + 48)
                for t in range(TILES):
                    pool.wait_ge(y_ready, 20 * b + 10 + t + 1)
                    nc.gpsimd.tensor_tensor(fx.nodes[0:TILE, t, :], fx.nodes[0:TILE, t, :], row_a[0:TILE, :],
                                            ALU.add).then_inc(x2_biased, 1)
                pool.wait_ge(x2_biased, 10 * b + 10)
                pool.wait_ge(h_prod, 20 * b + 20)

        @block.tensor
        def _(pe):
            def modulation(b, ph, t):
                pe.wait_ge(conds_ready, 2 * b + ph + 1)
                if t >= 2:
                    pe.wait_ge(y_ready, 20 * b + 10 * ph + t - 1)
                for k in range(2):
                    mm = pe.matmul(bank(4 * (t % 2) + k)[0:TILE], fx.cond[:, cols(t)], sw[:, k, :], start=True, stop=True)
                mm.then_inc(mod_ready, 1)

            def turn_rows(b, ph, t):
                pe.wait_ge(y_ready, 20 * b + 10 * ph + t + 1)
                if t >= 2:
                    pe.wait_ge(y_low, 20 * b + 10 * ph + t - 1)
                for c in range(CHUNKS):
                    mm = pe.transpose(bank(4 * (t % 2) + 2)[:, c * TILE:(c + 1) * TILE], yr[0:TILE, t % 2, c * 128:(c + 1) * 128],
                                      fx.ident[0:TILE, 0:TILE])
                mm.then_inc(y_turned, 1)

            def rows_product(t, n, weights):
                for c in range(CHUNKS):
                    mm = three(pe, bank(n)[0:TILE], [p[:, c, cols(t)] for p in pair_y], [p[:, c, :] for p in weights],
                               c == 0, c == CHUNKS - 1)
                return mm

            with pe.Fori(0, LAYERS1) as b:
                pe.wait_ge(x_done, 10 * b + 10)
                for i in range(1, TILES + 4):
                    if i >= 4:
                        t = i - 4
                        pe.wait_ge(w_ready, 24 * b + 4 + 2)
                        pe.wait_ge(y_low, 20 * b + t + 1)
                        if t >= 2:
                            pe.wait_ge(v_copied, 10 * b + t - 1)
                        rows_product(t, 4 * (t % 2) + 3, wa).then_inc(v_prod, 1)
                    if 2 <= i <= TILES + 1:
                        turn_rows(b, 0, i - 2)
                    if i <= TILES:
                        modulation(b, 0, i - 1)

                for h in range(HEADS1):
                    pe.wait_ge(w_ready, 24 * b + 6 + 2 * h + 2)
                    if h == 0:
                        pe.wait_ge(v_copied, 10 * b + 10)
                    else:
                        pe.wait_ge(pt_low, 120 * b + 30 * h)
                        pe.wait_ge(rows_copied, 20 * b + 5 * h)
                    for c in range(6):
                        w, (a, z) = c // 3, ((0, 500), (500, 1000), (1000, NODES))[c % 3]
                        if c >= 2:
                            pe.wait_ge(proj_low, 24 * b + 6 * h + c - 1)
                        for k in range(CHUNKS):
                            mm = three(pe, bank(6 + c % 2)[:, 0:z - a], [hw[:, p, w, k, :] for p in range(2)],
                                       [p[:, k, a:z] for p in pair_y], k == 0, k == CHUNKS - 1)
                        mm.then_inc(proj_prod, 1)
                    pe.wait_ge(proj_low, 24 * b + 6 * h + 6)
                    for i in range(LAG_STEPS):
                        T = 40 * b + 10 * h + i
                        if i < TILES:
                            if h > 0 or i > 0:
                                pe.wait_ge(scored, T)
                            for a, z in CUTS:
                                mm = three(pe, psum[0:TILE, a:z], [p[:, cols(i)] for p in qk[0]],
                                           [p[:, a:z] for p in qk[1]], True, True)
                            mm.then_inc(qk_done, 1)
                        if 3 <= i:
                            g, half = (i - 3) // 2, (i - 3) % 2
                            G = 20 * b + 5 * h + g
                            if half == 0:
                                pe.wait_ge(pt_low, 120 * b + 30 * h + 6 * g + 6)
                                if h > 0 or g > 0:
                                    pe.wait_ge(o_done, G)
                            for d in range(5 * half, 5 * half + 5):
                                out = bank(5)[:, 0:250]
                                mm = three(pe, out, [p[0:TILE, d, h * HDIM1:(h + 1) * HDIM1] for p in (v_h, v_l)],
                                           [p[0:TILE, g % 2, d, :] for p in (pt_h, pt_l)], d == 0, d == TILES - 1)
                            if half == 1:
                                mm.then_inc(pv_done, 1)
                        if 1 <= i <= TILES:
                            j = i - 1
                            pe.wait_ge(exped, T)
                            for u in range(3):
                                U = 3 * j + u
                                if U >= 3:
                                    pe.wait_ge(pt_low, 120 * b + 30 * h + U - 2)
                                out = bank((3, 4, 7)[u])
                                for d in range(4 * u, min(4 * u + 4, TILES)):
                                    mm = pe.transpose(out[0:TILE, cols(d - 4 * u)], prob[0:TILE, j % 2, cols(d)],
                                                      fx.ident[0:TILE, 0:TILE])
                                mm.then_inc(turned, 1)
                        if 2 <= i <= TILES + 1:
                            j = i - 2
                            g = j // 2
                            pe.wait_ge(diagonal, T - 1)
                            if j % 2 == 0 and g > 0:
                                pe.wait_ge(rows_copied, 20 * b + 5 * h + g)
                            pe.matmul(bank(6)[:, cols(j % 2)],
                                      fx.ones[0:TILE, :], mass_diag[0:TILE, j % 2, :], start=True, stop=True,
                                      skip_group_check=True).then_inc(rows_prod, 1)

                pe.wait_ge(att_low, 4 * b + 4)
                pe.wait_ge(pt_low, 120 * b + 120)
                pe.wait_ge(o_done, 20 * b + 20)
                pe.wait_ge(w_ready, 24 * b + 16 + 2)
                for i in range(TILES + 2):
                    if i < TILES:
                        if i >= 2:
                            pe.wait_ge(residual, 10 * b + i - 1)
                        rows_product(i, 4 * (i % 2) + 3, wb).then_inc(o_prod, 1)
                    if i >= 2:
                        turn_rows(b, 1, i - 2)
                    if 1 <= i <= TILES:
                        modulation(b, 1, i - 1)
                pe.wait_ge(w_ready, 24 * b + 20 + 2)
                pe.wait_ge(y_low, 20 * b + 20)
                for n in range(GROUPS):
                    if n >= 2:
                        pe.wait_ge(h_rows, 20 * b + 4 * n - 4)
                    for j in range(CHUNKS):
                        for c in range(CHUNKS):
                            mm = three(pe, bank(4 * (n % 2) + j)[:, 0:250], [p[:, c, j * 128:(j + 1) * 128] for p in wa],
                                       [p[:, c, 250 * n:250 * n + 250] for p in pair_y], c == 0, c == CHUNKS - 1)
                        mm.then_inc(h_prod, 1)
                pe.wait_ge(w_ready, 24 * b + 24 + 2)
                for t in range(TILES):
                    pe.wait_ge(h_low, 5 * b + t // 2 + 1)
                    if t == 0:
                        pe.wait_ge(h_rows, 20 * b + 16)
                    if t >= 4:
                        pe.wait_ge(x_done, 10 * b + 10 + t - 3)
                    rows_product(t, 4 + t % 4, wb).then_inc(m_prod, 1)

        @block.scalar
        def _(act):
            def turned_high(b, ph, t):
                act.wait_ge(y_turned, 20 * b + 10 * ph + t + 1)
                nc.scalar.activation(y_h[:, :, cols(t)], bank(4 * (t % 2) + 2)[:, 0:4 * TILE].rearrange("p (c n) -> p c n", c=4),
                                     ACT.Copy).then_inc(y_high, 1)

            def std(b, ph, t):
                act.wait_ge(var_ready, 20 * b + 10 * ph + t + 1)
                norm_std(nc, fx, t % 2, std_ready)

            def normed(b, ph, t):
                act.wait_ge(shift_ready, 20 * b + 10 * ph + t + 1)
                nc.scalar.activation(xn[0:TILE, t % 2, :], fx.nodes[0:TILE, t, :], ACT.Identity,
                                     bias=fx.shift[0:TILE, t % 2:t % 2 + 1],
                                     scale=fx.rstd[0:TILE, t % 2:t % 2 + 1]).then_inc(xn_ready, 1)

            with act.Fori(0, LAYERS1) as b:
                for i in range(TILES + 5):
                    if i < TILES:
                        std(b, 0, i)
                    if 1 <= i <= TILES:
                        normed(b, 0, i - 1)
                    if 2 <= i <= TILES + 1:
                        turned_high(b, 0, i - 2)
                    if 4 <= i <= TILES + 3:
                        t = i - 4
                        act.wait_ge(v_prod, 10 * b + t + 1)
                        if t >= 2:
                            act.wait_ge(v_low, 10 * b + t - 1)
                        nc.scalar.activation(vf[0:TILE, t % 2, :], bank(4 * (t % 2) + 3)[0:TILE], ACT.Copy).then_inc(v_copied, 1)
                    if i >= 5:
                        t = i - 5
                        act.wait_ge(v_sum, 10 * b + t + 1)
                        nc.scalar.activation(v_h[0:TILE, t, :], vf[0:TILE, t % 2, :], ACT.Copy).then_inc(v_high, 1)
                act.wait_ge(v_low, 10 * b + 10)
                act.wait_ge(x_spilled, 16 * b + 16)
                for h in range(HEADS1):
                    for c in range(6):
                        w, (a, z) = c // 3, ((0, 500), (500, 1000), (1000, NODES))[c % 3]
                        wait_apart(act, fx, proj_prod, 24 * b + 6 * h + c + 1)
                        nc.scalar.activation(qk[w][0][:, a:z], bank(6 + c % 2)[:, 0:z - a], ACT.Identity,
                                             bias=fx.qkb[:, w, bass.ds(HEADS1 * b + h, 1)]).then_inc(proj_high, 1)
                    for i in range(LAG_STEPS):
                        T = 40 * b + 10 * h + i
                        if 1 <= i <= TILES:
                            j = i - 1
                            for u in range(3):
                                U = 3 * j + u
                                act.wait_ge(turned, 120 * b + 30 * h + U + 1)
                                src, dst = unit_views(bank((3, 4, 7)[u]), pt_h, u, j)
                                nc.scalar.activation(dst, src, ACT.Copy).then_inc(pt_high, 1)
                        if i < TILES:
                            act.wait_ge(peaked, T + 1)
                            nc.scalar.activation(prob[0:TILE, i % 2, :], prob[0:TILE, i % 2, :], ACT.Exp,
                                                 bias=fx.peak[0:TILE, i % 2, 1:2],
                                                 accum_out=fx.mass[0:TILE, i, 0:1]).then_inc(exped, 1)
                        if i >= 3 and i % 2 == 1:
                            g = (i - 3) // 2
                            act.wait_ge(rows_prod, 40 * b + 10 * h + 2 * g + 2)
                            if h > 0 or g >= 2:
                                act.wait_ge(o_done, 20 * b + 5 * h + g - 1)
                            nc.scalar.activation(mass_rows[:, g % 2, :], bank(6)[:, 0:250],
                                                 ACT.Copy).then_inc(rows_copied, 1)
                for i in range(TILES + 2):
                    if i < TILES:
                        std(b, 1, i)
                    if 1 <= i <= TILES:
                        normed(b, 1, i - 1)
                    if i >= 2:
                        turned_high(b, 1, i - 2)
                for n in range(GROUPS):
                    if n >= 2:
                        act.wait_ge(h_low, 5 * b + n - 1)
                    for j in range(CHUNKS):
                        wait_apart(act, fx, h_prod, 20 * b + 4 * n + j + 1)
                        nc.scalar.activation(hidden[:, n % 2, j, :], bank(4 * (n % 2) + j)[:, 0:250], ACT.Relu,
                                             bias=fx.qkb[:, 2, bass.ds(CHUNKS * b + j, 1)]).then_inc(h_rows, 1)

        @block.vector
        def _(dve):
            def stats(b, ph, t):
                L = 20 * b + 10 * ph + t
                norm_stats(dve, fx, t % 2, fx.nodes[0:TILE, t, :], stats_own, L + 1, var_ready)

            def scale(b, ph, t):
                L = 20 * b + 10 * ph + t
                k = slice(t % 2, t % 2 + 1)
                dve.wait_ge(std_ready, L + 1)
                dve.reciprocal(fx.rstd[0:TILE, k], fx.std[0:TILE, k]).then_inc(rstd_own, 1)
                dve.wait_ge(rstd_own, L + 1)
                dve.scalar_tensor_tensor(fx.shift[0:TILE, k], fx.moments[0:TILE, t % 2, 0:1], -1.0, fx.rstd[0:TILE, k],
                                         ALU.mult, ALU.mult).then_inc(shift_ready, 1)

            def finish(b, ph, t):
                L = 20 * b + 10 * ph + t
                dve.wait_ge(xn_ready, L + 1)
                if t >= 2:
                    dve.wait_ge(y_turned, L - 1)
                dve.wait_ge(mod_ready, L + 1)
                dve.scalar_tensor_tensor(yr[0:TILE, t % 2, :], bank(4 * (t % 2))[0:TILE], 1.0, xn[0:TILE, t % 2, :],
                                         ALU.add, ALU.mult).then_inc(finish_own, 1)
                dve.wait_ge(finish_own, L + 1)
                dve.tensor_tensor(yr[0:TILE, t % 2, :], yr[0:TILE, t % 2, :], bank(4 * (t % 2) + 1)[0:TILE],
                                  ALU.add).then_inc(y_ready, 1)

            def turned_low(b, ph, t):
                dve.wait_ge(y_high, 20 * b + 10 * ph + t + 1)
                dve.tensor_tensor(y_l[:, :, cols(t)], bank(4 * (t % 2) + 2)[:, 0:4 * TILE].rearrange("p (c n) -> p c n", c=4),
                                  y_h[:, :, cols(t)].bitcast(F32), ALU.subtract).then_inc(y_low, 1)

            dve.memset(fx.peak[0:1, 0, 0:1], 0.0).then_inc(x_done, TILES)
            with dve.Fori(0, LAYERS1) as b:
                dve.wait_ge(x_done, 10 * b + 10)
                for i in range(TILES + 3):
                    if 2 <= i <= TILES + 1:
                        finish(b, 0, i - 2)
                    if i < TILES:
                        stats(b, 0, i)
                    if 1 <= i <= TILES:
                        scale(b, 0, i - 1)
                    if i >= 3:
                        turned_low(b, 0, i - 3)
                dve.wait_ge(x_spilled, 16 * b + 16)
                for h in range(HEADS1):
                    for c in range(6):
                        w, (a, z) = c // 3, ((0, 500), (500, 1000), (1000, NODES))[c % 3]
                        dve.wait_ge(proj_high, 24 * b + 6 * h + c + 1)
                        dve.scalar_tensor_tensor(qk[w][1][:, a:z], bank(6 + c % 2)[:, 0:z - a],
                                                 fx.qkb[:, w, bass.ds(HEADS1 * b + h, 1)], qk[w][0][:, a:z].bitcast(F32),
                                                 ALU.add, ALU.subtract).then_inc(proj_low, 1)
                    for i in range(LAG_STEPS):
                        T = 40 * b + 10 * h + i
                        if i < TILES:
                            if i >= 2:
                                dve.wait_ge(turned, 120 * b + 30 * h + 3 * (i - 1))
                            wait_apart(dve, fx, qk_done, T + 1)
                            row_scores(dve, psum[0:TILE, 0:NODES], i, T, HDIM1 ** -0.5)
                        if 1 <= i <= TILES:
                            row_mass(dve, i - 1, T - 1)
                            j = i - 1
                            for u in range(3):
                                U = 3 * j + u
                                dve.wait_ge(pt_high, 120 * b + 30 * h + U + 1)
                                src, dst = unit_views(bank((3, 4, 7)[u]), pt_l, u, j)
                                _, high = unit_views(bank((3, 4, 7)[u]), pt_h, u, j)
                                dve.tensor_tensor(dst, src, high, ALU.subtract).then_inc(pt_low, 1)
                        if i >= 4 and i % 2 == 0:
                            g = (i - 4) // 2
                            dve.wait_ge(pv_done, 20 * b + 5 * h + g + 1)
                            dve.wait_ge(rows_copied, 20 * b + 5 * h + g + 1)
                            dve.tensor_tensor(attended[:, h, 250 * g:250 * g + 250],
                                              bank(5)[:, 0:250], mass_rows[:, g % 2, :],
                                              ALU.mult).then_inc(o_done, 1)
                dve.wait_ge(o_done, 20 * b + 20)
                for c in range(CHUNKS):
                    dve.tensor_copy(y_h[:, c, :], attended[:, c, :]).then_inc(att_high, 1)
                for c in range(CHUNKS):
                    dve.wait_ge(att_high, 4 * b + c + 1)
                    dve.tensor_tensor(y_l[:, c, :], attended[:, c, :], y_h[:, c, :].bitcast(F32),
                                      ALU.subtract).then_inc(att_low, 1)
                for i in range(TILES + 3):
                    if 2 <= i <= TILES + 1:
                        finish(b, 1, i - 2)
                    if i < TILES:
                        dve.wait_ge(o_prod, 10 * b + i + 1)
                        dve.wait_ge(x_biased, 10 * b + i + 1)
                        dve.tensor_tensor(fx.nodes[0:TILE, i, :], bank(4 * (i % 2) + 3)[0:TILE], fx.nodes[0:TILE, i, :],
                                          ALU.add).then_inc(residual, 1)
                        dve.wait_ge(residual, 10 * b + i + 1)
                        stats(b, 1, i)
                    if 1 <= i <= TILES:
                        scale(b, 1, i - 1)
                    if i >= 3:
                        turned_low(b, 1, i - 3)
                for n in range(GROUPS):
                    dve.wait_ge(h_rows, 20 * b + 4 * n + 4)
                    at = slice(250 * n, 250 * n + 250)
                    dve.tensor_copy(y_h[:, :, at], hidden[:, n % 2]).then_inc(h_high, 1)
                    dve.wait_ge(h_high, 5 * b + n + 1)
                    dve.tensor_tensor(y_l[:, :, at], hidden[:, n % 2], y_h[:, :, at].bitcast(F32),
                                      ALU.subtract).then_inc(h_low, 1)
                for t in range(TILES):
                    dve.wait_ge(m_prod, 10 * b + t + 1)
                    dve.wait_ge(x2_biased, 10 * b + t + 1)
                    dve.tensor_tensor(fx.nodes[0:TILE, t, :], bank(4 + t % 4)[0:TILE], fx.nodes[0:TILE, t, :],
                                      ALU.add).then_inc(x_done, 1)



def third_layer(nc, fx, psum, kept, count_rows, eps, w1, b1, g1, be1, w2, b2, g2, be2):
    with ExitStack() as ctx:
        def sem(name):
            return ctx.enter_context(nc.semaphore("L2_" + name))

        before = packer(nc, VALUES_AT)("layer_input", [128, TILES, DIM], F32)
        counts = fx.count_dst
        place = packer(nc, TURNED_AT)
        plane = [place(f"batch_plane_{k}", [128, CHUNKS, NODES], F32) for k in range(2)]
        place = packer(nc, SLOT_A_AT)
        w = [place(f"batch_weight_{k}", [128, CHUNKS, DIM], F32) for k in range(2)]
        lanes = place("batch_vectors", [128, 6, CHUNKS], F32)
        factor = place("diagonal_factor", [128, 2], F32)
        diagonal = place("diagonal", [128, TILE], F32)
        stats = place("batch_stats", [128, 2, 3, 6], F32)
        moments = place("batch_moments", [128, 2, 2], F32)
        affine = place("batch_affine", [128, 2, 4], F32)

        loaded, in_loaded, w_loaded = sem("counts_loaded"), sem("input_loaded"), sem("weights_loaded")
        joined, stat_own, var_ready = sem("inputs_joined"), sem("stats_step"), sem("variance_ready")
        std_ready, rstd_own, normed = sem("std_ready"), sem("rstd_step"), sem("nodes_normed")
        own, diag_ready = sem("diagonal_step"), sem("diagonal_ready")
        prod, copied = sem("products"), sem("products_copied")
        b_own, b_var, b_std, b_aff = sem("batch_step"), sem("batch_variance"), sem("batch_std"), sem("batch_affine_ready")
        applied, turned, added = sem("batch_applied"), sem("turned_back"), sem("output_added")

        def region(c):
            return psum[:, (c % 2) * 3 * BANK:(c % 2) * 3 * BANK + NODES]

        def bank(n):
            return psum[:, n * BANK:(n + 1) * BANK]

        block = ctx.enter_context(nc.Block())

        @block.sync
        def _(sp):
            sp.dma_start(before[0:TILE], kept.rearrange("(t p) d -> p t d", p=TILE)).then_inc(in_loaded, 16)
            sp.dma_start(counts[0:TILE, :, 0:NODES],
                         count_rows[0:NODES, :].rearrange("(t p) s -> p t s", p=TILE)).then_inc(loaded, 16)
            sp.dma_start(factor[:, 0:1], eps.rearrange("(a b) -> a b", a=1).broadcast_to([128, 1])).then_inc(w_loaded, 16)
            for k, v in enumerate((w1, w2)):
                sp.dma_start(w[k][:, :, :], v.rearrange("(c p) n -> p c n", p=128)).then_inc(w_loaded, 16)
            for k, v in enumerate((b1, g1, be1, b2, g2, be2)):
                sp.dma_start(lanes[:, k, :], v.rearrange("(c p) -> p c", p=128),
                             allow_slow_non_contiguous=True).then_inc(w_loaded, 16)

        @block.vector
        def _(dve):
            dve.wait_ge(in_loaded, 16)
            for i in range(TILES + 1):
                if i < TILES:
                    row = fx.nodes[0:TILE, i, :]
                    dve.tensor_tensor(row, row, before[0:TILE, i, :], ALU.add).then_inc(joined, 1)
                    dve.wait_ge(joined, i + 1)
                    norm_stats(dve, fx, i % 2, row, stat_own, i + 1, var_ready)
                if i >= 1:
                    row = fx.nodes[0:TILE, i - 1, :]
                    dve.wait_ge(std_ready, i)
                    norm_rows(dve, fx, (i - 1) % 2, row, row, rstd_own, i).then_inc(normed, 1)
            dve.wait_ge(w_loaded, 144)
            dve.wait_ge(loaded, 16)
            dve.tensor_scalar(factor[:, 1:2], factor[:, 0:1], 1.0, None, ALU.add).then_inc(own, 1)
            dve.wait_ge(own, 1)
            dve.tensor_scalar(diagonal[:, :], fx.ident[:, 0:TILE], factor[:, 1:2], None, ALU.mult).then_inc(own, 1)
            dve.wait_ge(own, 2)
            for t in range(TILES):
                at = counts[0:TILE, t, t * TILE:(t + 1) * TILE]
                dve.tensor_tensor(at, at, diagonal[0:TILE, :], ALU.add).then_inc(diag_ready, 1)

            for n in range(2 * CHUNKS):
                k, j = n // CHUNKS, n % CHUNKS
                u = plane[1 - k][:, j, :]
                at = n % 2
                dve.wait_ge(copied, CHUNKS + n + 1)
                for q, (a, z) in enumerate(((0, 500), (500, 1000), (1000, NODES))):
                    dve.bn_stats(stats[:, at, q, :], u[:, a:z]).then_inc(b_own, 1)
                wait_apart(dve, fx, b_own, 6 * n + 3)
                dve.bn_aggr(moments[:, at, :], stats[:, at].rearrange("p q s -> p (q s)")).then_inc(b_var, 1)
                dve.wait_ge(b_std, n + 1)
                f = affine[:, at]
                dve.reciprocal(f[:, 1:2], f[:, 0:1]).then_inc(b_own, 1)
                dve.wait_ge(b_own, 6 * n + 4)
                dve.tensor_tensor(f[:, 2:3], f[:, 1:2], lanes[:, 3 * k + 1, j:j + 1], ALU.mult).then_inc(b_own, 1)
                dve.wait_ge(b_own, 6 * n + 5)
                dve.tensor_tensor(f[:, 3:4], f[:, 2:3], moments[:, at, 0:1], ALU.mult).then_inc(b_own, 1)
                dve.wait_ge(b_own, 6 * n + 6)
                dve.tensor_tensor(f[:, 3:4], lanes[:, 3 * k + 2, j:j + 1], f[:, 3:4], ALU.subtract).then_inc(b_aff, 1)

            for i in range(TILES + 1):
                if i < TILES:
                    row = fx.nodes[0:TILE, i, :]
                    dve.wait_ge(turned, i + 1)
                    dve.tensor_tensor(row, bank(6 + i % 2)[0:TILE], row, ALU.add).then_inc(added, 1)
                    dve.wait_ge(added, i + 1)
                    norm_stats(dve, fx, i % 2, row, stat_own, TILES + i + 1, var_ready)
                if i >= 1:
                    row = fx.nodes[0:TILE, i - 1, :]
                    dve.wait_ge(std_ready, TILES + i)
                    norm_rows(dve, fx, (i - 1) % 2, row, row, rstd_own, TILES + i).then_inc(normed, 1)

        @block.scalar
        def _(act):
            for t in range(TILES):
                act.wait_ge(var_ready, t + 1)
                norm_std(nc, fx, t % 2, std_ready)
            for c in range(CHUNKS):
                act.wait_ge(prod, c + 1)
                nc.scalar.activation(plane[0][:, c, :], region(c), ACT.Copy).then_inc(copied, 1)
            act.wait_ge(w_loaded, 144)

            def apply(n):
                k, j = n // CHUNKS, n % CHUNKS
                u = plane[1 - k][:, j, :]
                act.wait_ge(b_var, n + 1)
                nc.scalar.activation(affine[:, n % 2, 0:1], moments[:, n % 2, 1:2], ACT.Sqrt, bias=fx.eps[:, :]).then_inc(b_std, 1)
                act.wait_ge(b_aff, n + 1)
                nc.scalar.activation(u, u, (ACT.Relu, ACT.Identity)[k], bias=affine[:, n % 2, 3:4],
                                     scale=affine[:, n % 2, 2:3]).then_inc(applied, 1)

            for n in range(2 * CHUNKS):
                k, j = n // CHUNKS, n % CHUNKS
                act.wait_ge(prod, CHUNKS + n + 1)
                nc.scalar.activation(plane[1 - k][:, j, :], region(n), ACT.Identity,
                                     bias=lanes[:, 3 * k, j:j + 1]).then_inc(copied, 1)
                apply(n)
            for t in range(TILES):
                act.wait_ge(var_ready, TILES + t + 1)
                norm_std(nc, fx, t % 2, std_ready)

        @block.tensor
        def _(pe):
            pe.wait_ge(normed, TILES)
            pe.wait_ge(diag_ready, TILES)
            for c in range(CHUNKS):
                if c >= 2:
                    pe.wait_ge(copied, c - 1)
                for k in range(TILES):
                    for a, z in CUTS:
                        mm = pe.matmul(region(c)[:, a:z], fx.nodes[0:TILE, k, c * 128:(c + 1) * 128],
                                       counts[0:TILE, k, a:z], start=(k == 0), stop=(k == TILES - 1))
                mm.then_inc(prod, 1)
            for n in range(2 * CHUNKS):
                k, j = n // CHUNKS, n % CHUNKS
                if j == 0:
                    if k == 0:
                        pe.wait_ge(w_loaded, 144)
                        pe.wait_ge(copied, CHUNKS)
                    else:
                        pe.wait_ge(applied, CHUNKS)
                if n >= 2:
                    pe.wait_ge(copied, CHUNKS + n - 1)
                for c in range(CHUNKS):
                    for a, z in CUTS:
                        mm = pe.matmul(region(n)[:, a:z], w[k][:, c, j * 128:(j + 1) * 128], plane[k][:, c, a:z],
                                       start=(c == 0), stop=(c == CHUNKS - 1))
                mm.then_inc(prod, 1)
            pe.wait_ge(applied, 2 * CHUNKS)
            for t in range(TILES):
                if t >= 2:
                    pe.wait_ge(added, t - 1)
                for c in range(CHUNKS):
                    mm = pe.transpose(bank(6 + t % 2)[0:TILE, c * 128:(c + 1) * 128], plane[0][:, c, t * TILE:(t + 1) * TILE],
                                      fx.ident[:, :])
                mm.then_inc(turned, 1)


def fourth_layer(nc, fx, psum, count_rows, ws, wb, a_w, a_b, out):
    with ExitStack() as ctx:
        def sem(name):
            return ctx.enter_context(nc.semaphore("L3_" + name))

        logs = fx.count_dst
        place = packer(nc, TURNED_AT)
        x_t = place("nodes_turned", [128, CHUNKS, NODES], F32)
        wx_t = place("projected_turned", [128, CHUNKS, NODES], F32)
        spread = place("source_scores_spread", [128, HEADS3, NODES], F32)
        values = packer(nc, VALUES_AT)("projected_parts", [128, TILES, HEADS3, 2, HDIM3], BF16)
        after = WORK_AT + TILES * DIM * 4
        place = packer(nc, after)
        target = place("target_scores", [128, TILES, HEADS3], F32)
        bias_a = place("score_bias_row", [128, HEADS3], F32)
        col_b = place("projection_bias_columns", [128, CHUNKS], F32)
        a_src = place("source_vectors", [128, HEADS3], F32)
        a_tgt = place("target_vectors", [128, CHUNKS, HEADS3], F32)
        after += 640
        place = packer(nc, after)
        prob = place("row_probabilities", [128, 2, NODES], F32)
        pt = [place(f"turned_{p}", [128, 2, TILES, TILE], BF16) for p in ("high", "low")]
        slope = place("source_slopes_spread", [128, 2, NODES], F32)
        part = place("output_part", [128, TILES, HDIM3], F32)
        offset = packer(nc, TURNED_AT)("logs_and_source_scores", [128, 2, NODES], F32)
        place = packer(nc, after)
        w_sb = place("projection_weights", [128, CHUNKS, DIM], F32)
        row_b = place("projection_bias_row", [128, DIM], F32)
        wf = place("projected_rows", [128, 2, DIM], F32)
        wide = place("source_vectors_spread", [128, HEADS3, 128], F32)
        plain = packer(nc, after + 18432)("plain_logs_by_target", [128, 2, NODES], F32)

        set_zero, loaded, stored = sem("vectors_zeroed"), sem("weights_loaded"), sem("stored")
        log_plain, log_ready, own = sem("logs_plain"), sem("logs_ready"), sem("log_step")
        turned, x_copied, spread_ready = sem("nodes_turned"), sem("turned_copied"), sem("vectors_spread")
        prod, copied, v_prod, v_sum = sem("products"), sem("products_copied"), sem("value_products"), sem("values_summed")
        v_high, v_low, r_prod, r_ready = sem("values_high"), sem("values_low"), sem("target_products"), sem("targets_ready")
        slope_ready, bent, offset_ready = sem("slopes_ready"), sem("relu_of_slopes"), sem("offsets_ready")
        scored, peaked = sem("scored"), sem("peaked")
        exped, mass_own, inverted = sem("exped"), sem("mass_step"), sem("inverted")
        p_turned, p_high, p_low, pv = sem("p_turned"), sem("p_high"), sem("p_low"), sem("weighted")
        half, summed, joined = sem("half_scaled"), sem("halves_joined"), sem("nodes_joined")
        stat_own, var_ready, std_ready = sem("stats_step"), sem("variance_ready"), sem("std_ready")
        rstd_own, normed = sem("rstd_step"), sem("normed")

        def region(c):
            return psum[:, (c % 2) * 3 * BANK:(c % 2) * 3 * BANK + NODES]

        def bank(n):
            return psum[:, n * BANK:(n + 1) * BANK]

        def cols(t):
            return slice(t * TILE, (t + 1) * TILE)

        def unit_views(source, place_, u, j):
            n = min(4, TILES - 4 * u)
            return (source[0:TILE, 0:n * TILE].rearrange("p (d n) -> p d n", d=n), place_[0:TILE, j % 2, 4 * u:4 * u + n, :])

        BANKS = ((3, 4, 7), (2, 5, 6))

        def behind(h, i, k, first, last):
            if i >= k:
                return None if last else (h, i - k)
            return None if first else (h - 1, TILES + i - k)

        def run_heads(eng, step):
            for i in range(TILES):
                step(0, i, True, False)
            with eng.Fori(1, HEADS3) as h:
                for i in range(TILES):
                    step(h, i, False, False)
            for i in range(5):
                step(HEADS3, i, False, True)

        block = ctx.enter_context(nc.Block())

        @block.sync
        def _(sp):
            for t in range(TILES):
                at = slice(t * TILE, (t + 1) * TILE)
                sp.dma_start(logs[0:TILE, t, at], count_rows[at, at]).then_inc(loaded, 16)
            for c in range(CHUNKS):
                sp.dma_start(w_sb[:, c, :].rearrange("p (h d) -> p h d", h=HEADS3),
                             ws[:, c * 128:(c + 1) * 128, :].rearrange("h p d -> p h d")).then_inc(loaded, 16)
            sp.dma_start(row_b[:, :], wb.rearrange("(a h) d -> a (h d)", a=1).broadcast_to([128, DIM])).then_inc(loaded, 16)
            sp.dma_start(col_b[:, :], wb.rearrange("(c e) d -> (e d) c", e=2), allow_slow_non_contiguous=True).then_inc(loaded, 16)
            sp.dma_start(bias_a[:, :], a_b.rearrange("(a h) -> a h", a=1).broadcast_to([128, HEADS3])).then_inc(loaded, 16)
            sp.wait_ge(set_zero, 2)
            for h in range(HEADS3):
                lo = HDIM3 * (h % 2)
                sp.dma_start(a_src[lo:lo + HDIM3, h:h + 1], a_w[h, HDIM3:2 * HDIM3].rearrange("(p a) -> p a", a=1),
                             allow_slow_non_contiguous=True).then_inc(loaded, 16)
                sp.dma_start(a_tgt[lo:lo + HDIM3, h // 2, h:h + 1], a_w[h, 0:HDIM3].rearrange("(p a) -> p a", a=1),
                             allow_slow_non_contiguous=True).then_inc(loaded, 16)
            sp.wait_ge(normed, TILES)
            sp.dma_start(out.rearrange("(t p) d -> p t d", p=TILE), fx.nodes[0:TILE]).then_inc(stored, 16)
            sp.wait_ge(stored, 16)

        ALL = 16 * (TILES + 4 + 3 + 2 * HEADS3)

        @block.gpsimd
        def _(pool):
            pool.memset(a_src[:, :], 0.0).then_inc(set_zero, 1)
            pool.memset(a_tgt[:, :, :], 0.0).then_inc(set_zero, 1)
            for t in range(TILES):
                pool.wait_ge(v_high, t + 1)
                nc.gpsimd.tensor_tensor(values[0:TILE, t, :, 1, :], wf[0:TILE, t % 2, :].rearrange("p (h d) -> p h d", d=HDIM3),
                                        values[0:TILE, t, :, 0, :], ALU.subtract).then_inc(v_low, 1)
            pool.wait_ge(copied, CHUNKS + HEADS3)
            pool.wait_ge(r_prod, TILES)
            pool.wait_ge(log_ready, TILES)

            def step(h, i, first, last):
                T = 10 * h + i
                five_back = behind(h, i, 5, first, last)
                if not last:
                    if not first or i >= 2:
                        wait_apart(pool, fx, scored, T - 1)
                    nc.gpsimd.tensor_tensor(offset[0:TILE, i % 2, :], logs[0:TILE, i, 0:NODES],
                                            spread[0:TILE, bass.ds(h, 1), :].rearrange("p a n -> p (a n)"),
                                            ALU.add).then_inc(offset_ready, 1)
                if five_back:
                    hh, j = five_back
                    wait_apart(pool, fx, summed, T - 4)
                    at = fx.nodes[0:TILE, j, bass.ds(hh * HDIM3, HDIM3)]
                    nc.gpsimd.tensor_tensor(at, at, part[0:TILE, j, :], ALU.add).then_inc(joined, 1)

            run_heads(pool, step)

        @block.vector
        def _(dve):
            steps = [0]
            dve.wait_ge(loaded, ALL)
            for h in range(HEADS3):
                dve.tensor_scalar(wide[:, h, :], fx.ones[:, :], a_src[:, h:h + 1], None, ALU.mult).then_inc(spread_ready, 1)
            for t in range(TILES):
                dve.wait_ge(log_plain, t + 1)
                log_counts(dve, logs[0:TILE, t, 0:NODES], plain[0:TILE, t % 2, :], 1.0, log_ready, own, steps)
                dve.wait_ge(v_prod, t + 1)
                if t >= 2:
                    dve.wait_ge(v_low, t - 1)
                dve.tensor_tensor(wf[0:TILE, t % 2, :], bank(6 + t % 2)[0:TILE], row_b[0:TILE, :], ALU.add).then_inc(v_sum, 1)
            dve.wait_ge(r_prod, TILES)
            r = target[0:TILE].rearrange("p t h -> p (t h)")
            dve.tensor_tensor(target[0:TILE], bank(6)[0:TILE, 0:TILES * HEADS3].rearrange("p (t h) -> p t h", h=HEADS3),
                              bias_a[0:TILE, :].unsqueeze(1).broadcast_to([TILE, TILES, HEADS3]), ALU.add).then_inc(own, 1)
            dve.wait_ge(own, steps[0] + 1)
            dve.tensor_scalar(r, r, -0.8, None, ALU.mult).then_inc(r_ready, 1)
            dve.wait_ge(v_low, TILES)
            dve.wait_ge(copied, CHUNKS + HEADS3)

            def step(h, i, first, last):
                T = 10 * h + i
                one, two_back, four_back = (behind(h, i, k, first, last) for k in (1, 2, 4))
                p = fx.peak[0:TILE, i % 2]
                if not last:
                    dve.wait_ge(offset_ready, T + 1)
                    wait_apart(dve, fx, bent, T + 1)
                    dve.tensor_tensor_reduce(prob[0:TILE, i % 2, :], prob[0:TILE, i % 2, :], offset[0:TILE, i % 2, :], 1.0,
                                             MASKED, ALU.add, ALU.max, p[:, 0:1]).then_inc(scored, 1)
                if one:
                    m = fx.mass[0:TILE, one[1]]
                    dve.wait_ge(exped, T)
                    dve.tensor_scalar(m[:, 1:2], m[:, 0:1], 1e-30, None, ALU.max).then_inc(mass_own, 1)
                if not last:
                    dve.wait_ge(scored, T + 1)
                    dve.tensor_scalar(p[:, 1:2], p[:, 0:1], MASKED * 1e-5, -1.0, ALU.max, ALU.mult).then_inc(peaked, 1)
                if one:
                    dve.wait_ge(mass_own, T)
                    dve.reciprocal(m[:, 2:3], m[:, 1:2]).then_inc(inverted, 1)
                if four_back:
                    j = four_back[1]
                    dve.wait_ge(half, T - 3)
                    dve.scalar_tensor_tensor(part[0:TILE, j, :], bank(j % 2)[0:TILE, 0:HDIM3], fx.mass[0:TILE, j, 2:3],
                                             part[0:TILE, j, :], ALU.mult, ALU.add).then_inc(summed, 1)
                if two_back:
                    j = two_back[1]
                    for u in range(3):
                        dve.wait_ge(p_high, 3 * T - 5 + u)
                        src, dst = unit_views(bank(BANKS[j % 2][u]), pt[1], u, j)
                        high = unit_views(bank(BANKS[j % 2][u]), pt[0], u, j)[1]
                        dve.tensor_tensor(dst, src, high, ALU.subtract).then_inc(p_low, 1)

            run_heads(dve, step)
            dve.wait_ge(joined, TILES * HEADS3)
            for i in range(TILES + 1):
                if i < TILES:
                    norm_stats(dve, fx, i % 2, fx.nodes[0:TILE, i, :], stat_own, i + 1, var_ready)
                if i >= 1:
                    row = fx.nodes[0:TILE, i - 1, :]
                    dve.wait_ge(std_ready, i)
                    norm_rows(dve, fx, (i - 1) % 2, row, row, rstd_own, i).then_inc(normed, 1)

        @block.scalar
        def _(act):
            act.wait_ge(loaded, ALL)

            def log(t):
                if t >= 2:
                    act.wait_ge(log_ready, t - 1)
                nc.scalar.activation(plain[0:TILE, t % 2, :], logs[0:TILE, t, 0:NODES], ACT.Ln,
                                     bias=fx.tiny[0:TILE, :]).then_inc(log_plain, 1)

            for t in range(TILES):
                act.wait_ge(turned, t + 1)
                nc.scalar.activation(x_t[:, :, cols(t)], bank(6 + t % 2)[:, 0:4 * TILE].rearrange("p (c n) -> p c n", c=4),
                                     ACT.Copy).then_inc(x_copied, 1)
            for t in range(TILES):
                log(t)
                act.wait_ge(v_sum, t + 1)
                nc.scalar.activation(values[0:TILE, t, :, 0, :], wf[0:TILE, t % 2, :].rearrange("p (h d) -> p h d", d=HDIM3),
                                     ACT.Copy).then_inc(v_high, 1)
            for j in range(CHUNKS):
                act.wait_ge(prod, j + 1)
                nc.scalar.activation(wx_t[:, j, :], region(j), ACT.Identity, bias=col_b[:, j:j + 1]).then_inc(copied, 1)
            for h in range(HEADS3):
                act.wait_ge(prod, CHUNKS + h + 1)
                nc.scalar.activation(spread[:, h, :], region(h), ACT.Copy).then_inc(copied, 1)
            act.wait_ge(copied, CHUNKS + HEADS3)
            act.wait_ge(v_low, TILES)
            act.wait_ge(r_ready, 1)
            nc.scalar.activation(slope[0:TILE, 0, :], spread[0:TILE, 0, :], ACT.Copy, scale=-0.8).then_inc(slope_ready, 1)

            def step(h, i, first, last):
                T = 10 * h + i
                one, two_back, four_back = (behind(h, i, k, first, last) for k in (1, 2, 4))
                if four_back:
                    j = four_back[1]
                    if not first and not last and i >= 4:
                        act.wait_ge(joined, 10 * h if i == TILES - 1 else T - 13)
                    act.wait_ge(inverted, T - 3)
                    act.wait_ge(pv, T - 3)
                    nc.scalar.activation(part[0:TILE, j, :], bank(j % 2)[0:TILE, HDIM3:2 * HDIM3], ACT.Copy,
                                         scale=fx.mass[0:TILE, j, 2:3]).then_inc(half, 1)
                if two_back:
                    j = two_back[1]
                    for u in range(3):
                        act.wait_ge(p_turned, 3 * T - 5 + u)
                        src, dst = unit_views(bank(BANKS[j % 2][u]), pt[0], u, j)
                        nc.scalar.activation(dst, src, ACT.Copy).then_inc(p_high, 1)
                if not last:
                    if i == 0:
                        wait_apart(act, fx, slope_ready, h + 1)
                    nc.scalar.activation(prob[0:TILE, i % 2, :], slope[0:TILE, bass.ds(h % 2, 1), :].rearrange("p a n -> p (a n)"),
                                         ACT.Relu, bias=target[0:TILE, i, bass.ds(h, 1)]).then_inc(bent, 1)
                if one:
                    j = one[1]
                    act.wait_ge(peaked, T)
                    nc.scalar.activation(prob[0:TILE, j % 2, :], prob[0:TILE, j % 2, :], ACT.Exp,
                                         bias=fx.peak[0:TILE, j % 2, 1:2], accum_out=fx.mass[0:TILE, j, 0:1]).then_inc(exped, 1)
                if not last and i == 5:
                    nxt = (h + 1) % HEADS3
                    nc.scalar.activation(slope[0:TILE, bass.ds((h + 1) % 2, 1), :], spread[0:TILE, bass.ds(nxt, 1), :],
                                         ACT.Copy, scale=-0.8).then_inc(slope_ready, 1)

            run_heads(act, step)
            for t in range(TILES):
                act.wait_ge(var_ready, t + 1)
                norm_std(nc, fx, t % 2, std_ready)

        @block.tensor
        def _(pe):
            for t in range(TILES):
                if t >= 2:
                    pe.wait_ge(x_copied, t - 1)
                for c in range(CHUNKS):
                    mm = pe.transpose(bank(6 + t % 2)[:, cols(c)], fx.nodes[0:TILE, t, c * 128:(c + 1) * 128],
                                      fx.ident[0:TILE, 0:TILE])
                mm.then_inc(turned, 1)
            pe.wait_ge(x_copied, TILES)
            pe.wait_ge(loaded, ALL)
            for t in range(TILES):
                if t >= 2:
                    pe.wait_ge(v_sum, t - 1)
                for c in range(CHUNKS):
                    mm = pe.matmul(bank(6 + t % 2)[0:TILE], x_t[:, c, cols(t)], w_sb[:, c, :], start=(c == 0),
                                   stop=(c == CHUNKS - 1))
                mm.then_inc(v_prod, 1)
            for j in range(CHUNKS):
                if j >= 2:
                    pe.wait_ge(copied, j - 1)
                for c in range(CHUNKS):
                    for a, z in CUTS:
                        mm = pe.matmul(region(j)[:, a:z], w_sb[:, c, j * 128:(j + 1) * 128], x_t[:, c, a:z],
                                       start=(c == 0), stop=(c == CHUNKS - 1))
                mm.then_inc(prod, 1)
            pe.wait_ge(copied, CHUNKS)
            pe.wait_ge(spread_ready, HEADS3)
            for h in range(HEADS3):
                if h >= 2:
                    pe.wait_ge(copied, CHUNKS + h - 1)
                for a, z in CUTS:
                    mm = pe.matmul(region(h)[:, a:z], wide[:, h, :], wx_t[:, h // 2, a:z], start=True, stop=True)
                mm.then_inc(prod, 1)
            pe.wait_ge(v_sum, TILES)
            for t in range(TILES):
                for c in range(CHUNKS):
                    mm = pe.matmul(bank(6)[0:TILE, t * HEADS3:(t + 1) * HEADS3], wx_t[:, c, cols(t)], a_tgt[:, c, :],
                                   start=(c == 0), stop=(c == CHUNKS - 1))
                mm.then_inc(r_prod, 1)
            pe.wait_ge(copied, CHUNKS + HEADS3)
            pe.wait_ge(r_ready, 1)

            def step(h, i, first, last):
                T = 10 * h + i
                one, two_back = behind(h, i, 1, first, last), behind(h, i, 2, first, last)
                if one:
                    j = one[1]
                    pe.wait_ge(exped, T)
                    if not first or j >= 2:
                        pe.wait_ge(p_low, 3 * T - 6)
                    for u in range(3):
                        for d in range(4 * u, min(4 * u + 4, TILES)):
                            mm = pe.transpose(bank(BANKS[j % 2][u])[0:TILE, cols(d - 4 * u)], prob[0:TILE, j % 2, cols(d)],
                                              fx.ident[0:TILE, 0:TILE])
                        mm.then_inc(p_turned, 1)
                if two_back:
                    hh, j = two_back
                    pe.wait_ge(p_low, 3 * T - 3)
                    if not first or j >= 2:
                        pe.wait_ge(summed, T - 3)
                    for d in range(TILES):
                        both = values[0:TILE, d, bass.ds(hh, 1), :, :].rearrange("p a k n -> p (a k n)")
                        for k in range(2):
                            mm = pe.matmul(bank(j % 2)[0:TILE, 0:2 * HDIM3], pt[k][0:TILE, j % 2, d, :], both,
                                           start=(d == 0 and k == 0), stop=(d == TILES - 1 and k == 1))
                    mm.then_inc(pv, 1)

            run_heads(pe, step)


_INS = ("x", "src", "dst", "edge_weight", "node_vec1", "L0_gnn_W", "L1_gnn_f_w1", "L1_gnn_f_b1", "L1_gnn_f_w2",
        "L1_gnn_f_b2", "L1_gnn_s1_w", "L1_gnn_s1_b", "L1_gnn_b1_w", "L1_gnn_b1_b", "L1_gnn_wq", "L1_gnn_bq", "L1_gnn_wk",
        "L1_gnn_bk", "L1_gnn_wv", "L1_gnn_bv", "L1_gnn_wo", "L1_gnn_bo", "L1_gnn_s2_w", "L1_gnn_s2_b", "L1_gnn_b2_w",
        "L1_gnn_b2_b", "L1_gnn_m_w1", "L1_gnn_m_b1", "L1_gnn_m_w2", "L1_gnn_m_b2", "L2_gnn_eps", "L2_gnn_W1", "L2_gnn_b1",
        "L2_gnn_gamma1", "L2_gnn_beta1", "L2_gnn_W2", "L2_gnn_b2", "L2_gnn_gamma2", "L2_gnn_beta2", "L3_gnn_Ws", "L3_gnn_Wb",
        "L3_gnn_a_w", "L3_gnn_a_b")


def graph_network(nc, t, out):
    fx = Fixed(nc)
    psum = nc.alloc_psum_tensor("psum", [128, 8 * BANK], F32)
    kept = nc.dram_tensor("layer_input_kept", [NODES, DIM], F32, kind="Internal").ap()
    spill = nc.dram_tensor("nodes_kept", [NODES, DIM], F32, kind="Internal").ap()
    count_rows = nc.dram_tensor("counts_kept", [WIDE, NODES], F32, kind="Internal").ap()

    def l1(name):
        return t["L1_gnn_" + name]

    def l2(name):
        return t["L2_gnn_" + name]

    edge_bands(nc, fx, psum, t["src"], t["dst"], t["edge_weight"], count_rows)
    first_layer(nc, fx, psum, t["x"], t["L0_gnn_W"], t["node_vec1"], l1("f_w1"), l1("f_b1"), l1("f_w2"), l1("f_b2"),
                l1("bq"), l1("bk"), l1("m_b1"), kept)
    second_layer(nc, fx, psum, spill, l1("wq"), l1("wk"), l1("wv"), l1("wo"), l1("m_w1"), l1("m_w2"), l1("bv"), l1("bo"),
                 l1("m_b2"), l1("s1_w"), l1("s1_b"), l1("b1_w"), l1("b1_b"), l1("s2_w"), l1("s2_b"), l1("b2_w"), l1("b2_b"))
    third_layer(nc, fx, psum, kept, count_rows, l2("eps"), l2("W1"), l2("b1"), l2("gamma1"), l2("beta1"), l2("W2"),
                l2("b2"), l2("gamma2"), l2("beta2"))
    fourth_layer(nc, fx, psum, count_rows, t["L3_gnn_Ws"], t["L3_gnn_Wb"], t["L3_gnn_a_w"], t["L3_gnn_a_b"], out)


def kernel(**inputs):
    import numpy as _np
    import concourse.bacc as _bacc
    from concourse import mybir as _mybir
    from concourse.bass_utils import run_bass_kernel_spmd as _run

    nc = _bacc.Bacc("TRN2", target_bir_lowering=False, num_devices=1)
    arrays, handles = {}, {}
    for name in _INS:
        a = _np.ascontiguousarray(inputs[name])
        arrays[f"in_{name}"] = a
        handles[name] = nc.dram_tensor(f"in_{name}", a.shape, _mybir.dt.from_np(a.dtype), kind="ExternalInput").ap()
    out = nc.dram_tensor("out_nodes", (NODES, DIM), _mybir.dt.float32, kind="ExternalOutput").ap()
    graph_network(nc, handles, out)
    r = _run(nc, [arrays], core_ids=[0])
    return r.results[0]["out_nodes"]
```

```python
from contextlib import ExitStack

import numpy as np

import concourse.bass as bass
from concourse import mybir

ALU = mybir.AluOpType
ACT = mybir.ActivationFunctionType
AX = mybir.AxisListType
F32 = mybir.dt.float32
F32R = mybir.dt.float32r
BF16 = mybir.dt.bfloat16
F16 = mybir.dt.float16
I32 = mybir.dt.int32

NODES, DIM, EDGES = 1250, 512, 20000
TILE = 125
TILES = NODES // TILE
ETILES = EDGES // TILE
PAIRS = ETILES // 2
SETS = 2
BAND = 32
BANDS = -(-NODES // BAND)
WIDE = BANDS * BAND
CHUNKS = DIM // 128
BANK = 512
CUTS = [(0, 512), (512, 1024), (1024, NODES)]
MASKED = -1.0e30
EPS = 1e-5
LAYERS1, HEADS1, HDIM1 = 4, 4, 128
COND, FREQS = 16, 32
HEADS3, HDIM3 = 8, 64
SBUF_BASE = 16512


WORK1 = 2 * TILES * WIDE * 4


def packer(nc, start):
    at = [start]

    def place(name, shape, dtype):
        size = int(np.prod(shape[1:])) * (2 if dtype in (BF16, F16) else 4)
        t = nc.alloc_sbuf_tensor_at(name, shape, dtype, offset=SBUF_BASE + at[0])
        at[0] += -(-size // 32) * 32
        return t

    return place


def edge_bands(nc, fx, psum, src, dst, weight, count_rows, x):
    with ExitStack() as ctx:
        def sem(name):
            return ctx.enter_context(nc.semaphore(name))

        place = packer(nc, WORK1)
        rows_i = place("edge_rows_int", [128, 2, 2, TILE], I32)
        rows_w = place("edge_rows_weight", [128, 2, TILE], F32)
        rows_f = place("edge_rows_float", [128, 3, 2, TILE], F32)
        cols = place("edge_columns", [128, 3, ETILES], F32)
        parts = place("weight_parts", [128, ETILES, 3], BF16)
        rest = place("weight_rest", [128, 2, ETILES], F32)
        tail = packer(nc, HEADW_AT)
        ids_i = tail("node_ids_int", [128, WIDE], I32)
        ids = place("node_ids", [128, WIDE], F16)
        onehot = place("onehot_source", [128, SETS, 2, NODES], BF16)
        station = place("onehot_band", [128, SETS, 2, 4, BAND], BF16)
        bands = place("band_products", [128, 2, NODES], F32)
        split = tail("band_weight_parts", [128, 2, TILES, 3, BAND], F32)
        pair = tail("band_weight_pair", [128, 2, TILES, BAND], F32)
        ext = place("tile_extremes", [128, 2, 2], F32)
        ext_b = place("tile_extremes_spread", [128, 2, 2, BANDS], F32)
        hit = place("band_meets_tile", [128, 3, ETILES], F32)
        band_at = place("band_start", [128, 2], F32)
        band_at_i = place("band_start_int", [128, 1], I32)
        up = place("pair_number_up", [128, 2, ETILES], F32)
        up_i = place("pair_number_int", [128, ETILES], I32)
        span = place("band_span_columns", [128, 4], F32)
        row = place("band_span_rows", [1, 6, BANDS], F32)
        row_i = place("band_span_registers", [1, 3, BANDS], I32)
        count_src, weight_src, ident, ones = fx.count_src, fx.weight_src, fx.ident, fx.ones

        loaded = sem("edges_loaded")
        x_loaded = sem("x_loaded")
        consts = sem("constants_ready")
        floats = sem("edge_floats_ready")
        turned = sem("edges_turned")
        spread = sem("extremes_spread")
        colsok = sem("edge_columns_ready")
        own = sem("vector_setup_step")
        spanned = sem("spans_turned")
        ready = sem("spans_ready")
        band_half = sem("onehot_band_plain")
        oh_ready = sem("onehots_ready")
        oh_free = sem("onehots_used")
        band_copied = sem("band_copied")
        turn = sem("band_turned")
        unturn = sem("turned_copied")
        summed = sem("weights_summed")
        stored = [sem(f"counts_stored_{s}") for s in range(2)]

        def region(s):
            return psum[:, s * 3 * BANK:s * 3 * BANK + NODES]

        def unit(v):
            return psum[:, (6 + v % 2) * BANK:(7 + v % 2) * BANK]

        def load(eng, what, b):
            return eng.value_load(row_i[0:1, what, bass.ds(b, 1)], min_val=(0, 1, 0)[what],
                                  max_val=(BANDS + 1) * PAIRS)

        block = ctx.enter_context(nc.Block())

        @block.sync
        def _(sp):
            for a, v in enumerate((src, dst)):
                r = v.rearrange("(t e) -> t e", e=TILE)
                sp.dma_start(rows_i[:, a, 0, :], r[0:128, :]).then_inc(loaded, 16)
                sp.dma_start(rows_i[0:32, a, 1, :], r[128:ETILES, :]).then_inc(loaded, 16)
            r = weight.rearrange("(t e) -> t e", e=TILE)
            sp.dma_start(rows_w[:, 0, :], r[0:128, :]).then_inc(loaded, 16)
            sp.dma_start(rows_w[0:32, 1, :], r[128:ETILES, :]).then_inc(loaded, 16)

            sp.dma_start(fx.nodes[0:TILE], x.rearrange("(t p) d -> p t d", p=TILE)).then_inc(x_loaded, 16)

            def store(i):
                for s in range(2):
                    b = 2 * i + s
                    sp.wait_ge(band_copied, b + 1)
                    sp.dma_start(count_rows[bass.ds(b * BAND, BAND), :], bands[0:BAND, s, :]).then_inc(stored[s], 16)

            with sp.Fori(0, BANDS // 2) as i:
                store(i)
            sp.wait_ge(x_loaded, 16)
            for s in range(2):
                sp.wait_ge(stored[s], 16 * (BANDS // 2))

        @block.gpsimd
        def _(pool):
            pool.memset(ident[:, :], 0.0).then_inc(consts, 1)
            pool.wait_ge(consts, 1)
            pool.affine_select(out=ident[:, :], in_=ident[:, :], compare_op=ALU.not_equal, fill=1.0,
                               base=0, pattern=[[-1, 128]], channel_multiplier=1).then_inc(consts, 1)
            pool.memset(ones[:, :], 1.0).then_inc(consts, 1)
            pool.iota(ids_i[:, :], [[1, WIDE]], base=0, channel_multiplier=0).then_inc(consts, 1)
            pool.iota(band_at_i[:, :], [[0, 1]], base=0, channel_multiplier=BAND).then_inc(consts, 1)
            pool.iota(up_i[:, :], [[1, PAIRS], [0, 2]], base=0, channel_multiplier=0).then_inc(consts, 1)

            pool.memset(pair[0:1, 0, 0, 0:1], 0.0).then_inc(summed, 2)
            pool.wait_ge(summed, 2)
            with pool.Fori(0, BANDS // 2) as i:
                for s in range(2):
                    b = 2 * i + s
                    pool.wait_ge(unturn, 3 * b + 3)
                    nc.gpsimd.tensor_tensor(pair[0:TILE, s], split[0:TILE, s, :, 0, :], split[0:TILE, s, :, 1, :],
                                            ALU.add).then_inc(summed, 1)
                    pool.wait_ge(summed, 2 * b + 3)
                    nc.gpsimd.tensor_tensor(weight_src[0:TILE, :, bass.ds(b * BAND, BAND)], pair[0:TILE, s],
                                            split[0:TILE, s, :, 2, :], ALU.add).then_inc(summed, 1)

        @block.vector
        def _(dve):
            steps = [0]

            def step(ins):
                steps[0] += 1
                ins.then_inc(own, 1)
                dve.wait_ge(own, steps[0])

            v = nc.vector
            dve.wait_ge(loaded, 96)
            for a in range(3):
                for c, n in ((0, 128), (1, 32)):
                    src_rows = rows_i[0:n, a, c, :] if a < 2 else rows_w[0:n, c, :]
                    v.tensor_copy(rows_f[0:n, a, c, :], src_rows).then_inc(floats, 1)
            dve.wait_ge(floats, 6)
            for c, n in ((0, 128), (1, 32)):
                for e, op in ((0, ALU.min), (1, ALU.max)):
                    step(v.tensor_reduce(ext[0:n, e, c:c + 1], rows_f[0:n, 1, c, :], AX.X, op))
            dve.wait_ge(consts, 6)
            for c, n in ((0, 128), (1, 32)):
                for e in range(2):
                    v.tensor_scalar(ext_b[0:n, e, c, :], ones[0:n, 0:BANDS], ext[0:n, e, c:c + 1], None,
                                    ALU.mult).then_inc(spread, 1)
            v.tensor_copy(ids[:, :], ids_i[:, :])
            step(v.tensor_copy(band_at[:, 0:1], band_at_i[:, :]))
            v.tensor_scalar(band_at[:, 1:2], band_at[:, 0:1], float(BAND - 1), None, ALU.add)
            v.tensor_scalar(up[:, 0, :], up_i[:, :], 1.0, None, ALU.add)
            step(v.tensor_scalar(up[:, 1, :], up_i[:, :], -1.0, float(PAIRS), ALU.mult, ALU.add))
            dve.wait_ge(turned, 6)
            for a in range(3):
                step(v.tensor_copy(cols[0:TILE, a, :], psum[0:TILE, a * BANK:a * BANK + ETILES]))
            w, r = cols[0:TILE, 2, :], rest[0:TILE]
            step(v.tensor_copy(parts[0:TILE, :, 0], w))
            step(v.tensor_tensor(r[:, 0, :], w, parts[0:TILE, :, 0], ALU.subtract))
            step(v.tensor_copy(parts[0:TILE, :, 1], r[:, 0, :]))
            step(v.tensor_tensor(r[:, 1, :], r[:, 0, :], parts[0:TILE, :, 1], ALU.subtract))
            step(v.tensor_copy(parts[0:TILE, :, 2], r[:, 1, :]))
            dve.wait_ge(spread, 8)
            low = psum[0:BANDS, 3 * BANK:3 * BANK + ETILES]
            high = psum[0:BANDS, 4 * BANK:4 * BANK + ETILES]
            h = hit[0:BANDS]
            step(v.tensor_scalar(h[:, 0, :], high, band_at[0:BANDS, 0:1], None, ALU.is_ge))
            step(v.scalar_tensor_tensor(h[:, 1, :], low, band_at[0:BANDS, 1:2], h[:, 0, :], ALU.is_le, ALU.mult))
            step(v.tensor_tensor(h[:, 0, :], h[:, 1, :], up[0:BANDS, 1, :], ALU.mult))
            step(v.tensor_tensor(h[:, 2, :], h[:, 1, :], up[0:BANDS, 0, :], ALU.mult))
            step(v.tensor_reduce(span[0:BANDS, 2:3], h[:, 0, :], AX.X, ALU.max))
            step(v.tensor_reduce(span[0:BANDS, 3:4], h[:, 2, :], AX.X, ALU.max))
            step(v.tensor_scalar(span[0:BANDS, 2:3], span[0:BANDS, 2:3], -1.0, float(PAIRS), ALU.mult, ALU.add))
            step(v.tensor_scalar(span[0:BANDS, 0:1], span[0:BANDS, 2:3], float(PAIRS - 2), None, ALU.min))
            step(v.tensor_scalar(span[0:BANDS, 2:3], span[0:BANDS, 0:1], 2.0, None, ALU.add))
            v.tensor_tensor(span[0:BANDS, 1:2], span[0:BANDS, 2:3], span[0:BANDS, 3:4], ALU.max).then_inc(spanned, 1)
            dve.wait_ge(spanned, 3)
            for k in range(2):
                step(v.tensor_copy(row[0:1, k, :], psum[0:1, 5 * BANK + 64 * k:5 * BANK + 64 * k + BANDS]))
            step(v.tensor_tensor(row[0:1, 2, :], row[0:1, 1, :], row[0:1, 0, :], ALU.subtract))
            step(v.memset(row[0:1, 3, :], 1.0))
            step(v.tensor_tensor_scan(row[0:1, 4, :], row[0:1, 3, :], row[0:1, 2, :], 0.0, ALU.mult, ALU.add))
            step(v.tensor_tensor(row[0:1, 5, :], row[0:1, 4, :], row[0:1, 2, :], ALU.subtract))
            step(v.tensor_tensor(row[0:1, 2, :], row[0:1, 5, :], row[0:1, 0, :], ALU.subtract))
            step(v.tensor_scalar(row[0:1, 2, :], row[0:1, 2, :], float(PAIRS), None, ALU.add))
            step(v.tensor_copy(row_i[0:1, 0, :], row[0:1, 5, :]))
            step(v.tensor_copy(row_i[0:1, 1, :], row[0:1, 4, :]))
            step(v.tensor_copy(row_i[0:1, 2, :], row[0:1, 2, :]))
            v.memset(row[0:1, 3, :], 1.0).then_inc(ready, 1)

            with dve.Fori(0, BANDS // 2) as i:
                begin = load(dve, 0, 2 * i)
                for s in range(2):
                    b = 2 * i + s
                    end, skew = load(dve, 1, b), load(dve, 2, b)
                    with dve.Fori(begin, end) as n:
                        at = n % SETS
                        t = 2 * nc.s_assert_within(n + PAIRS - skew, 0, PAIRS - 1,
                                                   skip_runtime_bounds_check_because="n runs over the pairs of the band")
                        plain = station[0:TILE, bass.ds(at, 1), :, 0, :].rearrange("p a q j -> p (a q) j")
                        dve.wait_ge(oh_free, n + 1)
                        v.tensor_tensor(plain, ids[0:TILE, bass.ds(b * BAND, BAND)].unsqueeze(1).broadcast_to([TILE, 2, BAND]),
                                        cols[0:TILE, 1, bass.ds(t, 2)].unsqueeze(2).broadcast_to([TILE, 2, BAND]),
                                        ALU.is_equal).then_inc(band_half, 1)
                        v.tensor_scalar(onehot[0:TILE, bass.ds(at, 1), 0, :], ids[0:TILE, 0:NODES],
                                        cols[0:TILE, 0, bass.ds(t, 1)], None, ALU.is_equal).then_inc(oh_ready, 1)
                        dve.wait_ge(band_half, n + 1)
                        v.tensor_tensor(
                            station[0:TILE, bass.ds(at, 1), :, 1:4, :].rearrange("p a q k j -> p (a q) k j"),
                            plain.unsqueeze(2).broadcast_to([TILE, 2, 3, BAND]),
                            parts[0:TILE, bass.ds(t, 2), :].unsqueeze(3).broadcast_to([TILE, 2, 3, BAND]),
                            ALU.mult).then_inc(oh_ready, 1)
                        v.tensor_scalar(onehot[0:TILE, bass.ds(at, 1), 1, :], ids[0:TILE, 0:NODES],
                                        cols[0:TILE, 0, bass.ds(t + 1, 1)], None, ALU.is_equal).then_inc(oh_ready, 1)
                    begin = end

        @block.tensor
        def _(pe):
            pe.wait_ge(consts, 3)
            pe.wait_ge(floats, 6)
            for a in range(3):
                pe.transpose(psum[0:TILE, a * BANK:a * BANK + 128], rows_f[:, a, 0, :], ident[:, :]).then_inc(turned, 1)
                pe.transpose(psum[0:TILE, a * BANK + 128:a * BANK + ETILES], rows_f[0:32, a, 1, :],
                             ident[0:32, 0:32]).then_inc(turned, 1)
            pe.wait_ge(spread, 4)
            for e in range(2):
                for c, n in ((0, 128), (1, 32)):
                    pe.matmul(psum[0:BANDS, (3 + e) * BANK + 128 * c:(3 + e) * BANK + 128 * c + n], ext_b[0:n, e, c, :],
                              ident[0:n, 0:n], start=True, stop=True).then_inc(spread, 1)
            pe.wait_ge(spanned, 1)
            for k in range(2):
                mm = pe.matmul(psum[0:1, 5 * BANK + 64 * k:5 * BANK + 64 * k + BANDS], span[0:BANDS, k:k + 1],
                               ident[0:BANDS, 0:BANDS], start=True, stop=True)
                mm.then_inc(spanned, 1)
            pe.wait_ge(ready, 1)
            pe.wait_ge(oh_free, SETS)

            def product(s, n, start):
                at = n % SETS
                for q in range(2):
                    pe.wait_ge(oh_ready, 3 * n + 2 + q)
                    for a, z in CUTS:
                        mm = pe.matmul(region(s)[:, a:z], station[0:TILE, bass.ds(at, 1), q, :, :].rearrange("p a k j -> p (a k j)"),
                                       onehot[0:TILE, bass.ds(at, 1), q, a:z], start=start and q == 0, stop=True,
                                       skip_group_check=True)
                mm.then_inc(oh_free, 1)

            def turn_band(b, s, first):
                pe.wait_ge(band_copied, b + 1)
                for u in range(3):
                    if u >= 2 or not first:
                        pe.wait_ge(unturn, 3 * b + u - 1)
                    for j in range(4 * u, min(4 * u + 4, TILES)):
                        mm = pe.transpose(unit(s + u)[0:TILE, (j % 4) * 128:(j % 4) * 128 + 128],
                                          bands[:, s, j * TILE:(j + 1) * TILE], ident[:, :])
                    mm.then_inc(turn, 1)

            def pair_of(i, first_pair):
                begin = load(pe, 0, 2 * i)
                for s in range(2):
                    end = load(pe, 1, 2 * i + s)
                    product(s, begin, True)
                    if s == 1 or not first_pair:
                        turn_band(2 * i + s - 1, 1 - s, first_pair)
                    with pe.Fori(begin + 1, end) as n:
                        product(s, n, False)
                    begin = end

            pair_of(0, True)
            with pe.Fori(1, BANDS // 2) as i:
                pair_of(i, False)
            turn_band(BANDS - 1, 1, False)

        @block.scalar
        def _(act):
            act.wait_ge(consts, 3)
            for k in range(SETS):
                nc.scalar.activation(bands[0:1, 0, k:k + 1], ones[0:1, 0:1], ACT.Copy).then_inc(oh_free, 1)
            act.wait_ge(ready, 1)

            def copy_units(b, s, wait_sums):
                if wait_sums:
                    act.wait_ge(summed, 2 * b)
                for u in range(3):
                    act.wait_ge(turn, 3 * b + u + 1)
                    n = min(4, TILES - 4 * u)
                    view = unit(s + u)[0:TILE, 0:n * 128].rearrange("p (j k d) -> p j k d", k=4, d=BAND)
                    nc.scalar.activation(count_src[0:TILE, 4 * u:4 * u + n, bass.ds(b * BAND, BAND)], view[:, :, 0, :],
                                         ACT.Copy)
                    nc.scalar.activation(split[0:TILE, s, 4 * u:4 * u + n, :, :], view[:, :, 1:4, :],
                                         ACT.Copy).then_inc(unturn, 1)

            def pair_of(i, first_pair):
                for s in range(2):
                    b = 2 * i + s
                    end = load(act, 1, b)
                    if s == 1 or not first_pair:
                        copy_units(b - 1, 1 - s, not first_pair)
                    if not first_pair:
                        act.wait_ge(stored[s], 16 * i)
                        act.wait_ge(turn, 3 * b - 3)
                    act.wait_ge(oh_free, end + SETS)
                    nc.scalar.activation(bands[:, s, :], region(s), ACT.Copy).then_inc(band_copied, 1)

            pair_of(0, True)
            with act.Fori(1, BANDS // 2) as i:
                pair_of(i, False)
            copy_units(BANDS - 1, 1, True)


PLANE = CHUNKS * NODES * 4
LOGS_AT = 0
TURNED_AT = LOGS_AT + TILES * WIDE * 4
SLOT_A_AT = TURNED_AT + 2 * PLANE
SLOT_B_AT = SLOT_A_AT + PLANE
VALUES_AT = SLOT_B_AT + 4 * 5024
WORK_AT = VALUES_AT + TILES * DIM * 4
WORK_SIZE = 33280
HEADW_AT = WORK_AT + WORK_SIZE
CONDS_AT = HEADW_AT + 8192
FIXED_AT = CONDS_AT + 5024 + 4096 + 4096 + 4096
LAST_AT = WORK_AT + TILES * DIM * 4 + 640
ROW_TAIL = 2 * CHUNKS * DIM * 4
PI = float(np.pi)


class LastWeights:

    def __init__(self, nc):
        place = packer(nc, WORK_AT + TILES * DIM * 4)
        self.target = place("target_scores", [128, TILES, HEADS3], F32)
        self.bias_a = place("score_bias_row", [128, HEADS3], F32)
        self.col_b = place("projection_bias_columns", [128, CHUNKS], F32)
        self.a_src = place("source_vectors", [128, HEADS3], F32)
        self.a_tgt = place("target_vectors", [128, CHUNKS, HEADS3], F32)
        place = packer(nc, LAST_AT)
        self.w_sb = place("projection_weights", [128, CHUNKS, DIM], F32)
        self.row_b = place("projection_bias_row", [128, DIM], F32)


class Fixed:

    def __init__(self, nc):
        place = packer(nc, FIXED_AT)
        self.passed = nc.alloc_semaphore("waits_passed")
        self.ident = place("identity", [128, 128], F32)
        self.ones = place("all_ones", [128, 128], F32)
        self.eps = place("norm_eps", [128, 1], F32)
        self.tiny = place("log_floor", [128, 1], F32)
        self.stats = place("norm_stats", [128, 2, 6], F32)
        self.moments = place("norm_moments", [128, 2, 2], F32)
        self.std = place("norm_std", [128, 2], F32)
        self.rstd = place("norm_rstd", [128, 2], F32)
        self.shift = place("norm_shift", [128, 2], F32)
        self.qkb = place("head_biases", [128, 3, LAYERS1 * HEADS1], F32)
        self.peak = place("row_peaks", [128, 2, 2], F32)
        self.mass = place("row_masses", [128, TILES, 3], F32)
        self.nodes = packer(nc, WORK_AT)("nodes", [128, TILES, DIM], F32)
        self.count_src = packer(nc, LOGS_AT)("counts", [128, TILES, WIDE], F32)
        self.count_dst = packer(nc, LOGS_AT)("counts_by_target", [128, TILES, WIDE], F32)
        self.before = packer(nc, HEADW_AT)("layer_input", [128, TILES, DIM], F32)
        self.weight_src = packer(nc, TURNED_AT)("weights", [128, TILES, WIDE], F32)
        self.cond = packer(nc, CONDS_AT)("condition_parts", [96, NODES], F32R)


def wait_apart(eng, fx, sem, value):
    eng.wait_ge(sem, value)
    eng.sem_inc(fx.passed, 1)


def norm_stats(dve, fx, at, rows, own, own_value, var_ready):
    dve.bn_stats(fx.stats[0:TILE, at, :], rows).then_inc(own, 1)
    wait_apart(dve, fx, own, own_value)
    dve.bn_aggr(fx.moments[0:TILE, at, :], fx.stats[0:TILE, at, :]).then_inc(var_ready, 1)


def norm_std(nc, fx, at, std_ready):
    nc.scalar.activation(fx.std[0:TILE, at:at + 1], fx.moments[0:TILE, at, 1:2], ACT.Sqrt,
                         bias=fx.eps[0:TILE, :]).then_inc(std_ready, 1)


def norm_rows(dve, fx, at, out, rows, own, own_value):
    dve.reciprocal(fx.rstd[0:TILE, at:at + 1], fx.std[0:TILE, at:at + 1]).then_inc(own, 1)
    dve.wait_ge(own, own_value)
    return dve.tensor_scalar(out, rows, fx.moments[0:TILE, at, 0:1], fx.rstd[0:TILE, at:at + 1],
                             ALU.subtract, ALU.mult)


def log_counts(dve, counts, logs, scale, ready, own, steps):
    steps[0] += 1
    dve.tensor_scalar(counts, counts, 0.0, MASKED, ALU.is_equal, ALU.mult).then_inc(own, 1)
    dve.wait_ge(own, steps[0])
    dve.scalar_tensor_tensor(counts, logs, scale, counts, ALU.mult, ALU.add).then_inc(ready, 1)


def first_layer(nc, fx, psum, w0, noise, f_w1, f_b1, f_w2, f_b2, bq, bk, b1):
    with ExitStack() as ctx:
        def sem(name):
            return ctx.enter_context(nc.semaphore(name))

        place = packer(nc, TURNED_AT + TILES * WIDE * 4)
        sum_t = place("edge_sums_turned", [128, CHUNKS, NODES], F32)
        w_sb = place("first_weight", [128, CHUNKS, DIM], F32)
        place = packer(nc, VALUES_AT)
        phase = place("noise_phase", [2 * FREQS, NODES], F32)
        turns = place("noise_turns", [2 * FREQS, NODES], F32)
        inner = place("condition_inner", [COND, NODES], F32)
        plain = place("condition_plain", [96, NODES], F32)
        logs = packer(nc, WORK_AT + TILES * DIM * 4)("plain_logs", [128, 2, NODES], F32)
        place = packer(nc, HEADW_AT)
        fw1 = place("noise_weight_1", [2 * FREQS, COND], F32)
        fw2 = place("noise_weight_2", [COND, 96], F32)
        fb1 = place("noise_bias_1", [COND, 1], F32)
        fb2 = place("noise_bias_2", [96, 1], F32)
        lane_i = place("lane_number_int", [2 * FREQS, 1], I32)
        lane = place("lane_number", [2 * FREQS, 4], F32)

        w_loaded = sem("first_weight_loaded")
        n_loaded = sem("noise_loaded")
        zeroed = sem("noise_buffers_set")
        small = sem("biases_loaded")
        own = sem("noise_step")
        emb_ready = sem("embedding_ready")
        inner_prod = sem("inner_product")
        inner_ready = sem("inner_ready")
        cond_prod = sem("condition_product")
        cond_ready = sem("condition_plain_ready")
        log_plain = sem("logs_plain")
        log_ready = sem("logs_ready")
        sums = sem("edge_sums")
        sums_ready = sem("edge_sums_copied")
        prod = sem("first_products")
        added = sem("relu_added")
        stat_own = sem("stats_step")
        var_ready = sem("variance_ready")
        std_ready = sem("std_ready")
        rstd_own = sem("rstd_step")

        block = ctx.enter_context(nc.Block())

        @block.sync
        def _(sp):
            sp.wait_ge(zeroed, 2)
            sp.dma_start(phase[:, :], noise.rearrange("n a -> a n").broadcast_to([2 * FREQS, NODES])).then_inc(n_loaded, 16)
            sp.dma_start(fw1[:, :], f_w1).then_inc(n_loaded, 16)
            sp.dma_start(fb1[:, :], f_b1.rearrange("(p a) -> p a", a=1)).then_inc(n_loaded, 16)
            for g in range(3):
                sp.dma_start(fw2[:, 32 * g:32 * g + COND], f_w2).then_inc(n_loaded, 16)
                sp.dma_start(fb2[32 * g:32 * g + COND, :], f_b2.rearrange("(p a) -> p a", a=1)).then_inc(n_loaded, 16)
            sp.dma_start(w_sb[:, :, :], w0.rearrange("(c p) n -> p c n", p=128)).then_inc(w_loaded, 16)
            for k, v in enumerate((bq, bk, b1)):
                sp.dma_start(fx.qkb[:, k, :], v.rearrange("i (c p) -> p (i c)", p=128),
                             allow_slow_non_contiguous=True).then_inc(small, 16)
            sp.wait_ge(small, 48)

        @block.gpsimd
        def _(pool):
            pool.memset(fw2[:, :], 0.0).then_inc(zeroed, 1)
            pool.memset(fb2[:, :], 1.0).then_inc(zeroed, 1)
            pool.memset(fx.eps[:, :], EPS).then_inc(zeroed, 1)
            pool.memset(fx.tiny[:, :], 2.0 ** -60).then_inc(zeroed, 1)
            pool.iota(lane_i[:, :], [[0, 1]], base=0, channel_multiplier=1).then_inc(zeroed, 1)

        @block.vector
        def _(dve):
            steps = [0]

            def step(ins):
                steps[0] += 1
                ins.then_inc(own, 1)
                dve.wait_ge(own, steps[0])

            dve.wait_ge(zeroed, 5)
            step(dve.tensor_copy(lane[:, 3:4], lane_i[:, :]))
            rate = 2.0 * PI / 16.0
            dve.tensor_scalar(lane[0:FREQS, 0:1], lane[0:FREQS, 3:4], 1.0, rate, ALU.add, ALU.mult)
            dve.tensor_scalar(lane[FREQS:, 0:1], lane[FREQS:, 3:4], 1.0 - FREQS, rate, ALU.add, ALU.mult)
            dve.memset(lane[0:FREQS, 1:2], 0.0)
            dve.memset(lane[FREQS:, 1:2], 0.25)
            dve.memset(lane[0:FREQS, 2:3], 0.0)
            step(dve.memset(lane[FREQS:, 2:3], PI / 2))
            dve.wait_ge(n_loaded, 144)
            step(dve.tensor_scalar(phase[:, :], phase[:, :], lane[:, 0:1], None, ALU.mult))
            step(dve.tensor_scalar(turns[:, :], phase[:, :], 0.5 / PI, lane[:, 1:2], ALU.mult, ALU.add))
            step(dve.tensor_scalar(turns[:, :], turns[:, :], 12582912.0, None, ALU.add))
            step(dve.tensor_scalar(turns[:, :], turns[:, :], -12582912.0, None, ALU.add))
            step(dve.scalar_tensor_tensor(phase[:, :], turns[:, :], -6.28125, phase[:, :], ALU.mult, ALU.add))
            step(dve.scalar_tensor_tensor(phase[:, :], turns[:, :], -(2 * PI - 6.28125), phase[:, :], ALU.mult, ALU.add))
            step(dve.tensor_scalar(phase[:, :], phase[:, :], lane[:, 2:3], 3.1415925, ALU.add, ALU.min))
            dve.tensor_scalar(phase[:, :], phase[:, :], -3.1415925, None, ALU.max).then_inc(emb_ready, 1)
            dve.wait_ge(cond_ready, 1)
            step(dve.tensor_copy(fx.cond[:, :], plain[:, :]))
            step(dve.tensor_tensor(fx.cond[64:96, :], plain[64:96, :], fx.cond[64:96, :].bitcast(F32), ALU.subtract))
            for t in range(TILES):
                counts = fx.count_src[0:TILE, t, 0:NODES]
                dve.wait_ge(log_plain, t + 1)
                log_counts(dve, counts, logs[0:TILE, t % 2, :], HDIM1 ** 0.5, log_ready, own, steps)

            for i in range(TILES + 1):
                if i < TILES:
                    row = fx.nodes[0:TILE, i, :]
                    dve.wait_ge(prod, i + 1)
                    dve.scalar_tensor_tensor(row, psum[0:TILE, (6 + i % 2) * BANK:(7 + i % 2) * BANK], 0.0, row,
                                             ALU.max, ALU.add).then_inc(added, 1)
                    dve.wait_ge(added, i + 1)
                    norm_stats(dve, fx, i % 2, row, stat_own, i + 1, var_ready)
                if i >= 1:
                    row = fx.nodes[0:TILE, i - 1, :]
                    dve.wait_ge(std_ready, i)
                    norm_rows(dve, fx, (i - 1) % 2, row, row, rstd_own, i)

        @block.scalar
        def _(act):
            act.wait_ge(emb_ready, 1)
            nc.scalar.activation(turns[:, :], phase[:, :], ACT.Sin).then_inc(emb_ready, 1)
            act.wait_ge(inner_prod, 1)
            nc.scalar.activation(inner[:, :], psum[0:COND, 3 * BANK:3 * BANK + NODES], ACT.Silu,
                                 bias=fb1[:, :]).then_inc(inner_ready, 1)
            act.wait_ge(cond_prod, 1)
            nc.scalar.activation(plain[:, :], psum[0:96, 3 * BANK:3 * BANK + NODES], ACT.Identity, bias=fb2[:, :]).then_inc(cond_ready, 1)
            for t in range(TILES):
                if t >= 2:
                    act.wait_ge(log_ready, t - 1)
                nc.scalar.activation(logs[0:TILE, t % 2, :], fx.count_src[0:TILE, t, 0:NODES], ACT.Ln,
                                     bias=fx.tiny[0:TILE, :]).then_inc(log_plain, 1)
            for c in range(CHUNKS):
                act.wait_ge(sums, c + 1)
                nc.scalar.activation(sum_t[:, c, :], psum[:, (c % 2) * 3 * BANK:(c % 2) * 3 * BANK + NODES],
                                     ACT.Copy).then_inc(sums_ready, 1)
            for t in range(TILES):
                act.wait_ge(var_ready, t + 1)
                norm_std(nc, fx, t % 2, std_ready)

        @block.tensor
        def _(pe):
            def edge_sum(c):
                for k in range(TILES):
                    for a, z in CUTS:
                        mm = pe.matmul(psum[:, (c % 2) * 3 * BANK + a:(c % 2) * 3 * BANK + z],
                                       fx.nodes[0:TILE, k, c * 128:(c + 1) * 128], fx.weight_src[0:TILE, k, a:z],
                                       start=(k == 0), stop=(k == TILES - 1))
                mm.then_inc(sums, 1)

            edge_sum(0)
            pe.wait_ge(n_loaded, 144)
            pe.wait_ge(emb_ready, 2)
            for a, z in CUTS:
                mm = pe.matmul(psum[0:COND, 3 * BANK + a:3 * BANK + z], fw1[:, :], turns[:, a:z], start=True, stop=True)
            mm.then_inc(inner_prod, 1)
            pe.wait_ge(inner_ready, 1)
            for a, z in CUTS:
                mm = pe.matmul(psum[0:96, 3 * BANK + a:3 * BANK + z], fw2[:, :], inner[:, a:z], start=True, stop=True)
            mm.then_inc(cond_prod, 1)
            pe.wait_ge(cond_ready, 1)
            for c in range(1, CHUNKS):
                if c >= 2:
                    pe.wait_ge(sums_ready, c - 1)
                edge_sum(c)
            pe.wait_ge(w_loaded, 16)
            pe.wait_ge(sums_ready, CHUNKS)
            for t in range(TILES):
                if t >= 2:
                    pe.wait_ge(added, t - 1)
                for c in range(CHUNKS):
                    mm = pe.matmul(psum[0:TILE, (6 + t % 2) * BANK:(7 + t % 2) * BANK],
                                   sum_t[:, c, t * TILE:(t + 1) * TILE], w_sb[:, c, :], start=(c == 0), stop=(c == CHUNKS - 1))
                mm.then_inc(prod, 1)




def three(pe, out, left, right, first, last):
    (lh, ll), (rh, rl) = left, right
    pe.matmul(out, lh, rh, start=first, stop=False, skip_group_check=True)
    pe.matmul(out, lh, rl, start=False, stop=False, skip_group_check=True)
    return pe.matmul(out, ll, rh, start=False, stop=last, skip_group_check=True)


def second_layer(nc, fx, psum, spill, count_rows, wq, wk, wv, wo, m1, m2, bv, bo, b2, s1, sb1, t1, tb1, s2, sb2, t2, tb2):
    with ExitStack() as ctx:
        def sem(name):
            return ctx.enter_context(nc.semaphore(name))

        place = packer(nc, TURNED_AT)
        y_h = place("turned_high", [128, CHUNKS, NODES], F32R)
        y_l = place("turned_low", [128, CHUNKS, NODES], F32R)
        place = packer(nc, SLOT_A_AT)
        wa = [place(f"slot_a_{p}", [128, CHUNKS, DIM], F32R) for p in ("high", "low")]
        row_a = place("slot_a_bias_row", [128, DIM], F32)
        attended = packer(nc, SLOT_A_AT)("attended_turned", [128, HEADS1, NODES], F32)
        place = packer(nc, SLOT_B_AT)
        wb = [place(f"slot_b_{p}", [128, CHUNKS, DIM], F32R) for p in ("high", "low")]
        row_b = place("slot_b_bias_row", [128, DIM], F32)
        place = packer(nc, SLOT_B_AT)
        qk = [[place(f"{w}_{p}", [128, NODES], F32R) for p in ("high", "low")] for w in ("queries", "keys")]
        place = packer(nc, VALUES_AT)
        v_h = place("values_high", [128, TILES, DIM], BF16)
        v_l = place("values_low", [128, TILES, DIM], BF16)
        hidden = packer(nc, VALUES_AT)("hidden_rows", [128, 2, CHUNKS, 250], F32)
        place = packer(nc, WORK_AT + TILES * DIM * 4)
        xn = place("normed_rows", [128, 2, DIM], F32)
        yr = place("conditioned_rows", [128, 2, DIM], F32)
        vf = place("value_rows", [128, 2, DIM], F32)
        place = packer(nc, WORK_AT)
        prob = place("probabilities", [128, 2, NODES], F32)
        pt_h = place("turned_probabilities_high", [128, 2, TILES, 250], BF16)
        pt_l = place("turned_probabilities_low", [128, 2, TILES, 250], BF16)
        mass_rows = place("inverse_mass_rows", [128, 2, 250], F32)
        mass_diag = place("inverse_mass_diagonal", [128, 2, TILE], F32)
        hw = packer(nc, HEADW_AT)("head_weights", [128, 2, 2, CHUNKS, HDIM1], F32R)
        place = packer(nc, CONDS_AT + 5024)
        sw = place("condition_weight_parts", [96, 2, DIM], F32R)
        raw = place("condition_weights", [32, 2, DIM], F32)
        stage = place("weight_stage", [128, 2, DIM], F32)
        pair_y = (y_h, y_l)

        def sem(name):
            return ctx.enter_context(nc.semaphore("L1_" + name))

        raw_loaded = sem("raw_loaded")
        conds_ready = sem("conds_ready")
        cond_own = sem("cond_own")
        stage_w0 = sem("stage_w0")
        stage_w1 = sem("stage_w1")
        split_high = sem("split_high")
        w_ready = sem("w_ready")
        bias_loaded = sem("bias_row_loaded")
        x_spilled = sem("x_spilled")
        x_back = [sem("x_back_0"), sem("x_back_1")]
        mod_ready = sem("mod_ready")
        stats_own = sem("stats_own")
        var_ready = sem("var_ready")
        std_ready = sem("std_ready")
        finish_own = sem("finish_own")
        rstd_own = sem("rstd_own")
        shift_ready = sem("norm_shift_ready")
        xn_ready = sem("normed_rows_ready")
        y_ready = sem("y_ready")
        y_turned = sem("y_turned")
        y_high = sem("y_high")
        y_low = sem("y_low")
        v_prod = sem("v_prod")
        v_copied = sem("v_copied")
        v_sum = sem("v_sum")
        v_high = sem("v_high")
        v_low = sem("v_low")
        proj_prod = sem("proj_prod")
        proj_high = sem("proj_high")
        proj_low = sem("proj_low")
        qk_done = sem("qk_done")
        scored = sem("scored")
        peaked = sem("peaked")
        exped = sem("exped")
        mass_own = sem("mass_own")
        inverted = sem("inverted")
        diagonal = sem("diagonal")
        rows_prod = sem("rows_prod")
        rows_copied = sem("rows_copied")
        turned = sem("turned")
        pt_high = sem("pt_high")
        pt_low = sem("pt_low")
        pv_done = sem("pv_done")
        o_done = sem("o_done")
        att_high = sem("att_high")
        att_low = sem("att_low")
        o_prod = sem("o_prod")
        x_biased = sem("x_biased")
        residual = sem("residual")
        h_prod = sem("h_prod")
        h_rows = sem("h_rows")
        h_high = sem("h_high")
        h_low = sem("h_low")
        m_prod = sem("m_prod")
        x_done = sem("x_done")
        x2_biased = sem("x2_biased")
        counts_loaded = sem("counts_loaded")
        stage_loaded = [stage_w0, stage_w1]
        GROUPS = TILES // 2
        PROJ_CUTS = ((0, 500), (500, 1000), (1000, NODES))

        def bank(n):
            return psum[:, n * BANK:(n + 1) * BANK]

        def cols(t):
            return slice(t * TILE, (t + 1) * TILE)

        def unit_views(source, pt, u, j):
            n = min(4, TILES - 4 * u)
            return (source[0:TILE, 0:n * TILE].rearrange("p (d n) -> p d n", d=n),
                    pt[0:TILE, (j // 2) % 2, 4 * u:4 * u + n, cols(j % 2)])

        def row_scores(dve, scores, i, T, scale):
            p = fx.peak[0:TILE, i % 2]
            dve.tensor_tensor_reduce(prob[0:TILE, i % 2, :], scores, fx.count_src[0:TILE, i, 0:NODES], scale, MASKED,
                                     ALU.add, ALU.max, p[:, 0:1]).then_inc(scored, 1)
            dve.wait_ge(scored, T + 1)
            dve.tensor_scalar(p[:, 1:2], p[:, 0:1], MASKED * 1e-5, -1.0, ALU.max, ALU.mult).then_inc(peaked, 1)

        def row_mass(dve, i, T):
            m = fx.mass[0:TILE, i]
            dve.wait_ge(exped, T + 1)
            dve.tensor_scalar(m[:, 1:2], m[:, 0:1], 1e-30, None, ALU.max).then_inc(mass_own, 1)
            dve.wait_ge(mass_own, T + 1)
            dve.reciprocal(m[:, 2:3], m[:, 1:2]).then_inc(inverted, 1)

        block = ctx.enter_context(nc.Block())

        @block.sync
        def _(sp):
            def weight(b, i, src):
                sp.wait_ge(w_ready, 24 * b + i + 1)
                sp.dma_start(stage[:, i % 2, :] if len(src.shape) == 2 else
                             stage[:, i % 2, :].rearrange("p (c n) -> p c n", c=CHUNKS), src).then_inc(stage_loaded[i % 2], 16)

            def rows_of(w, b, c):
                return w[bass.ds(b, 1), c * 128:(c + 1) * 128, :].rearrange("a p n -> (a p) n")

            def head_of(w, b, h):
                return w[bass.ds(b, 1), :, h * HDIM1:(h + 1) * HDIM1].rearrange("a (c p) n -> p (a c) n", p=128)

            def condition(b, mats, ph):
                if ph == 1:
                    sp.wait_ge(conds_ready, 2 * b + 1)
                for k, (w, bias) in enumerate(mats):
                    sp.dma_start(raw[0:COND, k, :], w[bass.ds(b, 1)].rearrange("a c n -> (a c) n")).then_inc(raw_loaded, 16)
                    sp.dma_start(raw[COND:COND + 1, k, :], bias[bass.ds(b, 1), :]).then_inc(raw_loaded, 16)

            def bias_row(out, v, b):
                sp.dma_start(out[:, :], v[bass.ds(b, 1), :].broadcast_to([128, DIM])).then_inc(bias_loaded, 16)

            sp.wait_ge(w_ready, 2)
            with sp.Fori(0, LAYERS1) as b:
                condition(b, ((s1, sb1), (t1, tb1)), 0)
                for i in range(4):
                    weight(b, i, rows_of(wv, b, i))
                bias_row(row_b, bv, b)
                for i in (0, 1):
                    weight(b, 4 + i, head_of((wq, wk)[i], b, 0))
                sp.wait_ge(y_ready, 20 * b + 10)
                sp.dma_start(spill[bass.ds(b, 1)].rearrange("a (t p) d -> p (a t) d", p=TILE), fx.nodes[0:TILE]).then_inc(x_spilled, 16)
                for i in range(2, 8):
                    weight(b, 4 + i, head_of((wq, wk)[i % 2], b, i // 2))
                    if i == 3:
                        condition(b, ((s2, sb2), (t2, tb2)), 1)
                for i in (0, 1):
                    weight(b, 12 + i, rows_of(wo, b, i))
                sp.wait_ge(qk_done, 40 * b + 40)
                bias_row(row_b, bo, b)
                for i in (2, 3):
                    weight(b, 12 + i, rows_of(wo, b, i))
                sp.wait_ge(o_done, 20 * b + 20)
                sp.wait_ge(x_spilled, 16 * b + 16)
                for k, t in enumerate((0, TILES // 2)):
                    sp.dma_start(fx.nodes[0:TILE, t:t + TILES // 2],
                                 spill[bass.ds(b, 1), t * TILE:(t + TILES // 2) * TILE].rearrange("a (t p) d -> p (a t) d", p=TILE)).then_inc(x_back[k], 16)
                for i in (0, 1):
                    weight(b, 16 + i, rows_of(m1, b, i))
                sp.wait_ge(att_low, 4 * b + 4)
                sp.wait_ge(bias_loaded, 48 * b + 32)
                bias_row(row_a, b2, b)
                for i in (2, 3):
                    weight(b, 16 + i, rows_of(m1, b, i))
                for i in range(4):
                    weight(b, 20 + i, rows_of(m2, b, i))
            sp.wait_ge(scored, 40 * LAYERS1)
            sp.dma_start(fx.count_dst[0:TILE, :, 0:NODES],
                         count_rows[0:NODES, :].rearrange("(t p) s -> p t s", p=TILE)).then_inc(counts_loaded, 16)
            sp.wait_ge(mod_ready, 20 * LAYERS1)
            sp.wait_ge(conds_ready, 2 * LAYERS1)
            sp.dma_start(fx.before[0:TILE], spill[0].rearrange("(t p) d -> p t d", p=TILE)).then_inc(counts_loaded, 16)
            sp.wait_ge(counts_loaded, 32)

        @block.gpsimd
        def _(pool):
            def split(b, i, high, low):
                st = stage[:, i % 2, :]
                wait_apart(pool, fx, stage_loaded[i % 2], 16 * (12 * b + i // 2 + 1))
                if len(high.shape) == 3:
                    st = st.rearrange("p (c n) -> p c n", c=CHUNKS)
                nc.gpsimd.tensor_copy(high, st).then_inc(split_high, 1)
                pool.wait_ge(split_high, 24 * b + i + 1)
                nc.gpsimd.tensor_tensor(low, st, high.bitcast(F32), ALU.subtract).then_inc(w_ready, 1)

            def condition(b, ph):
                if ph == 1:
                    wait_apart(pool, fx, raw_loaded, 64 * (2 * b + ph + 1))
                    nc.gpsimd.tensor_copy(sw[64:96], raw[:, :, :]).then_inc(cond_own, 1)
                    wait_apart(pool, fx, cond_own, 4 * b + 2 * ph + 1)
                    nc.gpsimd.tensor_copy(sw[0:32], raw[:, :, :]).then_inc(cond_own, 1)
                pool.wait_ge(cond_own, 4 * b + 2 * ph + 2)
                nc.gpsimd.tensor_tensor(sw[32:64], raw[:, :, :], sw[0:32].bitcast(F32), ALU.subtract).then_inc(conds_ready, 1)
                pool.wait_ge(conds_ready, 2 * b + ph + 1)

            pool.memset(raw[:, :, :], 0.0).then_inc(w_ready, 1)
            pool.memset(mass_diag[0:1, 0, 0:1], 0.0).then_inc(w_ready, 1)
            pool.wait_ge(w_ready, 2)
            with pool.Fori(0, LAYERS1) as b:
                condition(b, 0)
                for i in range(4):
                    split(b, i, wa[0][:, i, :], wa[1][:, i, :])
                for i in (0, 1):
                    split(b, 4 + i, hw[:, 0, i], hw[:, 1, i])
                pool.wait_ge(bias_loaded, 48 * b + 16)
                for i in range(TILES + 1):
                    if i < TILES:
                        pool.wait_ge(v_copied, 10 * b + i + 1)
                        nc.gpsimd.tensor_tensor(vf[0:TILE, i % 2, :], vf[0:TILE, i % 2, :], row_b[0:TILE, :],
                                                ALU.add).then_inc(v_sum, 1)
                    if i >= 1:
                        t = i - 1
                        pool.wait_ge(v_high, 10 * b + t + 1)
                        nc.gpsimd.tensor_tensor(v_l[0:TILE, t, :], vf[0:TILE, t % 2, :], v_h[0:TILE, t, :],
                                                ALU.subtract).then_inc(v_low, 1)
                for h in range(HEADS1):
                    for j in range(TILES):
                        T = 40 * b + 10 * h + j
                        if h > 0 or j >= 2:
                            pool.wait_ge(rows_prod, T - 1)
                        wait_apart(pool, fx, inverted, T + 1)
                        nc.gpsimd.tensor_scalar(mass_diag[0:TILE, j % 2, :], fx.ident[0:TILE, 0:TILE],
                                                fx.mass[0:TILE, j, 2:3], None, ALU.mult).then_inc(diagonal, 1)
                        if h < HEADS1 - 1 and j in (3, 6):
                            i = 6 + 2 * h + (j == 6)
                            pool.wait_ge(proj_prod, 24 * b + 6 * h + 6)
                            split(b, i, hw[:, 0, i % 2], hw[:, 1, i % 2])
                    if h == 1:
                        pool.wait_ge(mod_ready, 20 * b + 10)
                        pool.wait_ge(diagonal, 40 * b + 20)
                        condition(b, 1)
                for i in range(12, 16):
                    pool.wait_ge(split_high, 24 * b + i + 1)
                    nc.gpsimd.tensor_tensor(wb[1][:, i - 12, :], stage[:, i % 2, :], wb[0][:, i - 12, :].bitcast(F32),
                                            ALU.subtract).then_inc(w_ready, 1)
                pool.wait_ge(bias_loaded, 48 * b + 32)
                for t in range(TILES):
                    if t % (TILES // 2) == 0:
                        pool.wait_ge(x_back[2 * t // TILES], 16 * b + 16)
                    nc.gpsimd.tensor_tensor(fx.nodes[0:TILE, t, :], fx.nodes[0:TILE, t, :], row_b[0:TILE, :],
                                            ALU.add).then_inc(x_biased, 1)
                pool.wait_ge(att_low, 4 * b + 4)
                for i in range(4):
                    split(b, 16 + i, wa[0][:, i, :], wa[1][:, i, :])
                pool.wait_ge(o_prod, 10 * b + 10)
                for i in range(4):
                    split(b, 20 + i, wb[0][:, i, :], wb[1][:, i, :])
                pool.wait_ge(bias_loaded, 48 * b + 48)
                for t in range(TILES):
                    pool.wait_ge(y_ready, 20 * b + 10 + t + 1)
                    nc.gpsimd.tensor_tensor(fx.nodes[0:TILE, t, :], fx.nodes[0:TILE, t, :], row_a[0:TILE, :],
                                            ALU.add).then_inc(x2_biased, 1)
                pool.wait_ge(x2_biased, 10 * b + 10)
                pool.wait_ge(h_prod, 20 * b + 20)

        @block.tensor
        def _(pe):
            def modulation(b, ph, t):
                pe.wait_ge(conds_ready, 2 * b + ph + 1)
                if t >= 2:
                    pe.wait_ge(y_ready, 20 * b + 10 * ph + t - 1)
                for k in range(2):
                    mm = pe.matmul(bank(4 * (t % 2) + k)[0:TILE], fx.cond[:, cols(t)], sw[:, k, :], start=True, stop=True)
                mm.then_inc(mod_ready, 1)

            def turn_rows(b, ph, t):
                pe.wait_ge(y_ready, 20 * b + 10 * ph + t + 1)
                if t >= 2:
                    pe.wait_ge(y_low, 20 * b + 10 * ph + t - 1)
                for c in range(CHUNKS):
                    mm = pe.transpose(bank(4 * (t % 2) + 2)[:, c * TILE:(c + 1) * TILE], yr[0:TILE, t % 2, c * 128:(c + 1) * 128],
                                      fx.ident[0:TILE, 0:TILE])
                mm.then_inc(y_turned, 1)

            def rows_product(t, n, weights, split=None, attended=None):
                for c in range(CHUNKS):
                    if split is not None:
                        pe.wait_ge(w_ready, split + c + 1)
                    if attended is not None:
                        pe.wait_ge(att_low, attended + c + 1)
                    mm = three(pe, bank(n)[0:TILE], [p[:, c, cols(t)] for p in pair_y], [p[:, c, :] for p in weights],
                               c == 0, c == CHUNKS - 1)
                return mm

            def hidden_product(n, j):
                for c in range(CHUNKS):
                    mm = three(pe, bank(4 * (n % 2) + j)[:, 0:250], [p[:, c, j * 128:(j + 1) * 128] for p in wa],
                               [p[:, c, 250 * n:250 * n + 250] for p in pair_y], c == 0, c == CHUNKS - 1)
                mm.then_inc(h_prod, 1)

            with pe.Fori(0, LAYERS1) as b:
                pe.wait_ge(x_done, 10 * b + 10)
                for i in range(1, TILES + 4):
                    if i >= 4:
                        t = i - 4
                        pe.wait_ge(y_low, 20 * b + t + 1)
                        if t >= 2:
                            pe.wait_ge(v_copied, 10 * b + t - 1)
                        rows_product(t, 4 * (t % 2) + 3, wa, 24 * b + 2 if t == 0 else None).then_inc(v_prod, 1)
                    if 2 <= i <= TILES + 1:
                        turn_rows(b, 0, i - 2)
                    if i <= TILES:
                        modulation(b, 0, i - 1)

                def project(h, chunks):
                    for c in chunks:
                        w, (a, z) = c // 3, PROJ_CUTS[c % 3]
                        if c == 0:
                            pe.wait_ge(w_ready, 24 * b + 6 + 2 * h + 2)
                            if h == 0:
                                pe.wait_ge(v_copied, 10 * b + 10)
                            else:
                                pe.wait_ge(scored, 40 * b + 10 * h)
                        if c >= 3:
                            pe.wait_ge(proj_low, 24 * b + 6 * h + c - 2)
                        for k in range(CHUNKS):
                            mm = three(pe, bank(c % 3)[:, 0:z - a], [hw[:, p, w, k, :] for p in range(2)],
                                       [p[:, k, a:z] for p in pair_y], k == 0, k == CHUNKS - 1)
                        mm.then_inc(proj_prod, 1)

                def scores(h, i):
                    T = 40 * b + 10 * h + i
                    if h > 0 or i > 0:
                        pe.wait_ge(scored, T)
                    for a, z in CUTS:
                        mm = three(pe, psum[0:TILE, a:z], [p[:, cols(i)] for p in qk[0]],
                                   [p[:, a:z] for p in qk[1]], True, True)
                    mm.then_inc(qk_done, 1)

                def weighted(h, j):
                    g, half = j // 2, j % 2
                    if half == 0:
                        pe.wait_ge(pt_low, 120 * b + 30 * h + 6 * g + 6)
                        if h > 0 or g > 0:
                            pe.wait_ge(o_done, 20 * b + 5 * h + g)
                    for d in range(5 * half, 5 * half + 5):
                        mm = three(pe, bank(5)[:, 0:250], [p[0:TILE, d, h * HDIM1:(h + 1) * HDIM1] for p in (v_h, v_l)],
                                   [p[0:TILE, g % 2, d, :] for p in (pt_h, pt_l)], d == 0, d == TILES - 1)
                    if half == 1:
                        mm.then_inc(pv_done, 1)

                def turn(h, j):
                    pe.wait_ge(exped, 40 * b + 10 * h + j + 1)
                    for u in range(3):
                        U = 3 * j + u
                        if h > 0 or U >= 3:
                            pe.wait_ge(pt_low, 120 * b + 30 * h + U - 2)
                        for d in range(4 * u, min(4 * u + 4, TILES)):
                            mm = pe.transpose(bank((3, 4, 7)[u])[0:TILE, cols(d - 4 * u)], prob[0:TILE, j % 2, cols(d)],
                                              fx.ident[0:TILE, 0:TILE])
                        mm.then_inc(turned, 1)

                def mass_on_rows(h, j):
                    pe.wait_ge(diagonal, 40 * b + 10 * h + j + 1)
                    if j % 2 == 0 and (h > 0 or j > 0):
                        pe.wait_ge(rows_copied, 20 * b + 5 * h + j // 2)
                    pe.matmul(bank(6)[:, cols(j % 2)], fx.ones[0:TILE, :], mass_diag[0:TILE, j % 2, :], start=True,
                              stop=True, skip_group_check=True).then_inc(rows_prod, 1)

                project(0, range(6))
                pe.wait_ge(proj_low, 24 * b + 6)
                for h in range(HEADS1):
                    more = h < HEADS1 - 1
                    for i in range(TILES + 2):
                        if i < TILES:
                            scores(h, i)
                        if i == 0 and h > 0:
                            weighted(h - 1, TILES - 1)
                        if 3 <= i <= TILES:
                            weighted(h, i - 3)
                        if i >= TILES and more:
                            project(h + 1, (i - TILES,))
                        if 1 <= i <= TILES:
                            turn(h, i - 1)
                        if i >= 2:
                            mass_on_rows(h, i - 2)
                    if more:
                        project(h + 1, range(2, 6))
                    weighted(h, TILES - 2)
                    if more:
                        pe.wait_ge(proj_low, 24 * b + 6 * h + 12)
                    else:
                        weighted(h, TILES - 1)

                pe.wait_ge(pt_low, 120 * b + 120)
                for i in range(TILES + 2):
                    if i < TILES:
                        if i >= 2:
                            pe.wait_ge(residual, 10 * b + i - 1)
                        if i == 0:
                            rows_product(i, 3, wb, 24 * b + 12 + 2, 4 * b).then_inc(o_prod, 1)
                        else:
                            if i == 1:
                                pe.wait_ge(o_done, 20 * b + 20)
                            rows_product(i, 4 * (i % 2) + 3, wb).then_inc(o_prod, 1)
                    if i == TILES + 1:
                        pe.wait_ge(w_ready, 24 * b + 20 + 2)
                        pe.wait_ge(y_low, 20 * b + 12)
                        pe.wait_ge(y_ready, 20 * b + 19)
                        hidden_product(0, 0)
                        hidden_product(0, 1)
                    if i >= 2:
                        turn_rows(b, 1, i - 2)
                    if 1 <= i <= TILES:
                        modulation(b, 1, i - 1)
                pe.wait_ge(y_low, 20 * b + 19)
                for n in range(GROUPS):
                    if n == 1:
                        pe.wait_ge(y_low, 20 * b + 20)
                    if n >= 2:
                        pe.wait_ge(h_rows, 20 * b + 4 * n - 4)
                    for j in range(2 if n == 0 else 0, CHUNKS):
                        hidden_product(n, j)
                pe.wait_ge(w_ready, 24 * b + 24 + 2)
                for t in range(TILES):
                    pe.wait_ge(h_low, 5 * b + t // 2 + 1)
                    if t == 0:
                        pe.wait_ge(h_rows, 20 * b + 16)
                    if t >= 4:
                        pe.wait_ge(x_done, 10 * b + 10 + t - 3)
                    rows_product(t, 4 + t % 4, wb).then_inc(m_prod, 1)

        @block.scalar
        def _(act):
            def turned_high(b, ph, t):
                act.wait_ge(y_turned, 20 * b + 10 * ph + t + 1)
                nc.scalar.activation(y_h[:, :, cols(t)], bank(4 * (t % 2) + 2)[:, 0:4 * TILE].rearrange("p (c n) -> p c n", c=4),
                                     ACT.Copy).then_inc(y_high, 1)

            def std(b, ph, t):
                act.wait_ge(var_ready, 20 * b + 10 * ph + t + 1)
                norm_std(nc, fx, t % 2, std_ready)

            def normed(b, ph, t):
                act.wait_ge(shift_ready, 20 * b + 10 * ph + t + 1)
                nc.scalar.activation(xn[0:TILE, t % 2, :], fx.nodes[0:TILE, t, :], ACT.Identity,
                                     bias=fx.shift[0:TILE, t % 2:t % 2 + 1],
                                     scale=fx.rstd[0:TILE, t % 2:t % 2 + 1]).then_inc(xn_ready, 1)

            with act.Fori(0, LAYERS1) as b:
                act.wait_ge(raw_loaded, 128 * b + 64)
                nc.scalar.activation(sw[64:96], raw[:, :, :], ACT.Copy).then_inc(cond_own, 1)
                nc.scalar.activation(sw[0:32], raw[:, :, :], ACT.Copy).then_inc(cond_own, 1)
                for i in range(TILES + 5):
                    if i < TILES:
                        std(b, 0, i)
                    if 1 <= i <= TILES:
                        normed(b, 0, i - 1)
                    if 2 <= i <= TILES + 1:
                        turned_high(b, 0, i - 2)
                    if 4 <= i <= TILES + 3:
                        t = i - 4
                        act.wait_ge(v_prod, 10 * b + t + 1)
                        if t >= 2:
                            act.wait_ge(v_low, 10 * b + t - 1)
                        nc.scalar.activation(vf[0:TILE, t % 2, :], bank(4 * (t % 2) + 3)[0:TILE], ACT.Copy).then_inc(v_copied, 1)
                    if i >= 5:
                        t = i - 5
                        act.wait_ge(v_sum, 10 * b + t + 1)
                        nc.scalar.activation(v_h[0:TILE, t, :], vf[0:TILE, t % 2, :], ACT.Copy).then_inc(v_high, 1)
                act.wait_ge(v_low, 10 * b + 10)
                act.wait_ge(x_spilled, 16 * b + 16)
                def projected_high(h, chunks):
                    for c in chunks:
                        w, (a, z) = c // 3, PROJ_CUTS[c % 3]
                        wait_apart(act, fx, proj_prod, 24 * b + 6 * h + c + 1)
                        nc.scalar.activation(qk[w][0][:, a:z], bank(c % 3)[:, 0:z - a], ACT.Identity,
                                             bias=fx.qkb[:, w, bass.ds(HEADS1 * b + h, 1)]).then_inc(proj_high, 1)

                def attended_high(c):
                    act.wait_ge(o_done, 20 * b + 5 * c + 5)
                    nc.scalar.activation(y_h[:, c, :], attended[:, c, :], ACT.Copy).then_inc(att_high, 1)

                def output_weights_high(i):
                    act.wait_ge(qk_done, 40 * b + 40)
                    act.wait_ge(stage_loaded[i % 2], 16 * (12 * b + i // 2 + 1))
                    nc.scalar.activation(wb[0][:, i - 12, :], stage[:, i % 2, :], ACT.Copy).then_inc(split_high, 1)

                projected_high(0, range(6))
                for h in range(HEADS1):
                    more = h < HEADS1 - 1
                    for i in range(TILES + 2):
                        T = 40 * b + 10 * h + i
                        if i >= TILES and more:
                            projected_high(h + 1, (i - TILES,))
                        if 1 <= i <= TILES:
                            j = i - 1
                            for u in range(3):
                                U = 3 * j + u
                                act.wait_ge(turned, 120 * b + 30 * h + U + 1)
                                src, dst = unit_views(bank((3, 4, 7)[u]), pt_h, u, j)
                                nc.scalar.activation(dst, src, ACT.Copy).then_inc(pt_high, 1)
                        if i < TILES:
                            act.wait_ge(peaked, T + 1)
                            nc.scalar.activation(prob[0:TILE, i % 2, :], prob[0:TILE, i % 2, :], ACT.Exp,
                                                 bias=fx.peak[0:TILE, i % 2, 1:2],
                                                 accum_out=fx.mass[0:TILE, i, 0:1]).then_inc(exped, 1)
                        if i >= 3 and i % 2 == 1:
                            g = (i - 3) // 2
                            act.wait_ge(rows_prod, 40 * b + 10 * h + 2 * g + 2)
                            if h > 0 or g >= 2:
                                act.wait_ge(o_done, 20 * b + 5 * h + max(g - 1, 0))
                            nc.scalar.activation(mass_rows[:, g % 2, :], bank(6)[:, 0:250],
                                                 ACT.Copy).then_inc(rows_copied, 1)
                        if not more and i in (2, 4, 6):
                            attended_high(i // 2 - 1)
                        if not more and i == TILES:
                            output_weights_high(12)
                            output_weights_high(13)
                    if more:
                        projected_high(h + 1, range(2, 6))
                attended_high(3)
                output_weights_high(14)
                output_weights_high(15)
                for i in range(TILES + 2):
                    if i < TILES:
                        std(b, 1, i)
                    if 1 <= i <= TILES:
                        normed(b, 1, i - 1)
                    if i >= 2:
                        turned_high(b, 1, i - 2)
                for n in range(GROUPS):
                    if n >= 2:
                        act.wait_ge(h_low, 5 * b + n - 1)
                    for j in range(CHUNKS):
                        wait_apart(act, fx, h_prod, 20 * b + 4 * n + j + 1)
                        nc.scalar.activation(hidden[:, n % 2, j, :], bank(4 * (n % 2) + j)[:, 0:250], ACT.Relu,
                                             bias=fx.qkb[:, 2, bass.ds(CHUNKS * b + j, 1)]).then_inc(h_rows, 1)

        @block.vector
        def _(dve):
            def stats(b, ph, t):
                L = 20 * b + 10 * ph + t
                norm_stats(dve, fx, t % 2, fx.nodes[0:TILE, t, :], stats_own, L + 1, var_ready)

            def scale(b, ph, t):
                L = 20 * b + 10 * ph + t
                k = slice(t % 2, t % 2 + 1)
                dve.wait_ge(std_ready, L + 1)
                dve.reciprocal(fx.rstd[0:TILE, k], fx.std[0:TILE, k]).then_inc(rstd_own, 1)
                dve.wait_ge(rstd_own, L + 1)
                dve.scalar_tensor_tensor(fx.shift[0:TILE, k], fx.moments[0:TILE, t % 2, 0:1], -1.0, fx.rstd[0:TILE, k],
                                         ALU.mult, ALU.mult).then_inc(shift_ready, 1)

            def finish(b, ph, t):
                L = 20 * b + 10 * ph + t
                dve.wait_ge(xn_ready, L + 1)
                if t >= 2:
                    dve.wait_ge(y_turned, L - 1)
                dve.wait_ge(mod_ready, L + 1)
                dve.scalar_tensor_tensor(yr[0:TILE, t % 2, :], bank(4 * (t % 2))[0:TILE], 1.0, xn[0:TILE, t % 2, :],
                                         ALU.add, ALU.mult).then_inc(finish_own, 1)
                dve.wait_ge(finish_own, L + 1)
                dve.tensor_tensor(yr[0:TILE, t % 2, :], yr[0:TILE, t % 2, :], bank(4 * (t % 2) + 1)[0:TILE],
                                  ALU.add).then_inc(y_ready, 1)

            def turned_low(b, ph, t):
                dve.wait_ge(y_high, 20 * b + 10 * ph + t + 1)
                dve.tensor_tensor(y_l[:, :, cols(t)], bank(4 * (t % 2) + 2)[:, 0:4 * TILE].rearrange("p (c n) -> p c n", c=4),
                                  y_h[:, :, cols(t)].bitcast(F32), ALU.subtract).then_inc(y_low, 1)

            dve.memset(fx.peak[0:1, 0, 0:1], 0.0).then_inc(x_done, TILES)
            with dve.Fori(0, LAYERS1) as b:
                dve.wait_ge(x_done, 10 * b + 10)
                for i in range(TILES + 3):
                    if 2 <= i <= TILES + 1:
                        finish(b, 0, i - 2)
                    if i < TILES:
                        stats(b, 0, i)
                    if 1 <= i <= TILES:
                        scale(b, 0, i - 1)
                    if i >= 3:
                        turned_low(b, 0, i - 3)
                dve.wait_ge(x_spilled, 16 * b + 16)
                def projected_low(h, chunks):
                    for c in chunks:
                        w, (a, z) = c // 3, PROJ_CUTS[c % 3]
                        dve.wait_ge(proj_high, 24 * b + 6 * h + c + 1)
                        dve.scalar_tensor_tensor(qk[w][1][:, a:z], bank(c % 3)[:, 0:z - a],
                                                 fx.qkb[:, w, bass.ds(HEADS1 * b + h, 1)], qk[w][0][:, a:z].bitcast(F32),
                                                 ALU.add, ALU.subtract).then_inc(proj_low, 1)

                def attend(h, g):
                    dve.wait_ge(pv_done, 20 * b + 5 * h + g + 1)
                    dve.wait_ge(rows_copied, 20 * b + 5 * h + g + 1)
                    dve.tensor_tensor(attended[:, h, 250 * g:250 * g + 250], bank(5)[:, 0:250], mass_rows[:, g % 2, :],
                                      ALU.mult).then_inc(o_done, 1)

                def attended_low(c):
                    dve.wait_ge(att_high, 4 * b + c + 1)
                    dve.tensor_tensor(y_l[:, c, :], attended[:, c, :], y_h[:, c, :].bitcast(F32),
                                      ALU.subtract).then_inc(att_low, 1)

                projected_low(0, range(6))
                for h in range(HEADS1):
                    more = h < HEADS1 - 1
                    for i in range(TILES + 2):
                        T = 40 * b + 10 * h + i
                        if i < TILES:
                            if h > 0 or i >= 2:
                                dve.wait_ge(turned, 120 * b + 30 * h + 3 * (i - 1))
                            wait_apart(dve, fx, qk_done, T + 1)
                            row_scores(dve, psum[0:TILE, 0:NODES], i, T, HDIM1 ** -0.5)
                        if 1 <= i <= TILES:
                            row_mass(dve, i - 1, T - 1)
                        if i == 0 and h > 0:
                            attend(h - 1, GROUPS - 1)
                        if i >= TILES and more:
                            projected_low(h + 1, (i - TILES,))
                        if 1 <= i <= TILES:
                            j = i - 1
                            for u in range(3):
                                U = 3 * j + u
                                dve.wait_ge(pt_high, 120 * b + 30 * h + U + 1)
                                src, dst = unit_views(bank((3, 4, 7)[u]), pt_l, u, j)
                                _, high = unit_views(bank((3, 4, 7)[u]), pt_h, u, j)
                                dve.tensor_tensor(dst, src, high, ALU.subtract).then_inc(pt_low, 1)
                        if i >= 4 and i % 2 == 0:
                            attend(h, (i - 4) // 2)
                        if not more and i in (3, 5, 7):
                            attended_low((i - 3) // 2)
                    if more:
                        projected_low(h + 1, range(2, 6))
                    else:
                        attend(h, GROUPS - 1)
                attended_low(3)
                for i in range(TILES + 3):
                    if 2 <= i <= TILES + 1:
                        finish(b, 1, i - 2)
                    if i < TILES:
                        dve.wait_ge(o_prod, 10 * b + i + 1)
                        dve.wait_ge(x_biased, 10 * b + i + 1)
                        dve.tensor_tensor(fx.nodes[0:TILE, i, :], bank(4 * (i % 2) + 3)[0:TILE], fx.nodes[0:TILE, i, :],
                                          ALU.add).then_inc(residual, 1)
                        dve.wait_ge(residual, 10 * b + i + 1)
                        stats(b, 1, i)
                    if 1 <= i <= TILES:
                        scale(b, 1, i - 1)
                    if i >= 3:
                        turned_low(b, 1, i - 3)
                for n in range(GROUPS):
                    dve.wait_ge(h_rows, 20 * b + 4 * n + 4)
                    at = slice(250 * n, 250 * n + 250)
                    dve.tensor_copy(y_h[:, :, at], hidden[:, n % 2]).then_inc(h_high, 1)
                    dve.wait_ge(h_high, 5 * b + n + 1)
                    dve.tensor_tensor(y_l[:, :, at], hidden[:, n % 2], y_h[:, :, at].bitcast(F32),
                                      ALU.subtract).then_inc(h_low, 1)
                for t in range(TILES):
                    dve.wait_ge(m_prod, 10 * b + t + 1)
                    dve.wait_ge(x2_biased, 10 * b + t + 1)
                    dve.tensor_tensor(fx.nodes[0:TILE, t, :], bank(4 + t % 4)[0:TILE], fx.nodes[0:TILE, t, :],
                                      ALU.add).then_inc(x_done, 1)



def third_layer(nc, fx, lw, psum, eps, w1, b1, g1, be1, w2, b2, g2, be2, ws, wb, a_w, a_b):
    with ExitStack() as ctx:
        def sem(name):
            return ctx.enter_context(nc.semaphore("L2_" + name))

        before = fx.before
        counts = fx.count_dst
        place = packer(nc, TURNED_AT)
        plane = [place(f"batch_plane_{k}", [128, CHUNKS, NODES], F32) for k in range(2)]
        place = packer(nc, SLOT_A_AT)
        w = [place(f"batch_weight_{k}", [128, CHUNKS, DIM], F32) for k in range(2)]
        lanes = place("batch_vectors", [128, 6, CHUNKS], F32)
        factor = place("diagonal_factor", [128, 2], F32)
        diagonal = place("diagonal", [128, TILE], F32)
        stats = place("batch_stats", [128, 2, 3, 6], F32)
        moments = place("batch_moments", [128, 2, 2], F32)
        affine = place("batch_affine", [128, 2, 4], F32)

        set_zero, last_loaded = sem("vectors_zeroed"), sem("last_weights_loaded")
        eps_loaded, w_loaded = sem("eps_loaded"), sem("weights_loaded")
        joined, stat_own, var_ready = sem("inputs_joined"), sem("stats_step"), sem("variance_ready")
        std_ready, rstd_own, normed = sem("std_ready"), sem("rstd_step"), sem("nodes_normed")
        own, diag_ready = sem("diagonal_step"), sem("diagonal_ready")
        prod, copied = sem("products"), sem("products_copied")
        b_own, b_var, b_std, b_aff = sem("batch_step"), sem("batch_variance"), sem("batch_std"), sem("batch_affine_ready")
        applied, turned, added = sem("batch_applied"), sem("turned_back"), sem("output_added")

        def region(c):
            return psum[:, (c % 2) * 3 * BANK:(c % 2) * 3 * BANK + NODES]

        def bank(n):
            return psum[:, n * BANK:(n + 1) * BANK]

        block = ctx.enter_context(nc.Block())

        @block.sync
        def _(sp):
            sp.dma_start(factor[:, 0:1], eps.rearrange("(a b) -> a b", a=1).broadcast_to([128, 1])).then_inc(eps_loaded, 16)
            for k, v in enumerate((w1, w2)):
                sp.dma_start(w[k][:, :, :], v.rearrange("(c p) n -> p c n", p=128)).then_inc(w_loaded, 16)
            for k, v in enumerate((b1, g1, be1, b2, g2, be2)):
                sp.dma_start(lanes[:, k, :], v.rearrange("(c p) -> p c", p=128),
                             allow_slow_non_contiguous=True).then_inc(w_loaded, 16)
            for c in range(CHUNKS):
                sp.dma_start(lw.w_sb[:, c, :].rearrange("p (h d) -> p h d", h=HEADS3),
                             ws[:, c * 128:(c + 1) * 128, :].rearrange("h p d -> p h d")).then_inc(last_loaded, 16)
            sp.dma_start(lw.row_b[:, :], wb.rearrange("(a h) d -> a (h d)", a=1).broadcast_to([128, DIM])).then_inc(last_loaded, 16)
            sp.dma_start(lw.col_b[:, :], wb.rearrange("(c e) d -> (e d) c", e=2),
                         allow_slow_non_contiguous=True).then_inc(last_loaded, 16)
            sp.dma_start(lw.bias_a[:, :], a_b.rearrange("(a h) -> a h", a=1).broadcast_to([128, HEADS3])).then_inc(last_loaded, 16)
            sp.wait_ge(set_zero, 2)
            for h in range(HEADS3):
                lo = HDIM3 * (h % 2)
                sp.dma_start(lw.a_src[lo:lo + HDIM3, h:h + 1], a_w[h, HDIM3:2 * HDIM3].rearrange("(p a) -> p a", a=1),
                             allow_slow_non_contiguous=True).then_inc(last_loaded, 16)
                sp.dma_start(lw.a_tgt[lo:lo + HDIM3, h // 2, h:h + 1], a_w[h, 0:HDIM3].rearrange("(p a) -> p a", a=1),
                             allow_slow_non_contiguous=True).then_inc(last_loaded, 16)
            sp.wait_ge(last_loaded, 16 * (CHUNKS + 3 + 2 * HEADS3))

        @block.gpsimd
        def _(pool):
            pool.memset(lw.a_src[:, :], 0.0).then_inc(set_zero, 1)
            pool.memset(lw.a_tgt[:, :, :], 0.0).then_inc(set_zero, 1)

        @block.vector
        def _(dve):
            for i in range(TILES + 1):
                if i < TILES:
                    row = fx.nodes[0:TILE, i, :]
                    dve.tensor_tensor(row, row, before[0:TILE, i, :], ALU.add).then_inc(joined, 1)
                    dve.wait_ge(joined, i + 1)
                    norm_stats(dve, fx, i % 2, row, stat_own, i + 1, var_ready)
                    if i == 0:
                        dve.wait_ge(eps_loaded, 16)
                        dve.tensor_scalar(factor[:, 1:2], factor[:, 0:1], 1.0, None, ALU.add).then_inc(own, 1)
                        dve.wait_ge(own, 1)
                        dve.tensor_scalar(diagonal[:, :], fx.ident[:, 0:TILE], factor[:, 1:2], None, ALU.mult).then_inc(own, 1)
                        dve.wait_ge(own, 2)
                    at = counts[0:TILE, i, i * TILE:(i + 1) * TILE]
                    dve.tensor_tensor(at, at, diagonal[0:TILE, :], ALU.add).then_inc(diag_ready, 1)
                if i >= 1:
                    row = fx.nodes[0:TILE, i - 1, :]
                    dve.wait_ge(std_ready, i)
                    norm_rows(dve, fx, (i - 1) % 2, row, row, rstd_own, i).then_inc(normed, 1)
            dve.wait_ge(w_loaded, 128)
            for n in range(2 * CHUNKS):
                k, j = n // CHUNKS, n % CHUNKS
                u = plane[1 - k][:, j, :]
                at = n % 2
                dve.wait_ge(copied, CHUNKS + n + 1)
                for q, (a, z) in enumerate(((0, 500), (500, 1000), (1000, NODES))):
                    dve.bn_stats(stats[:, at, q, :], u[:, a:z]).then_inc(b_own, 1)
                wait_apart(dve, fx, b_own, 6 * n + 3)
                dve.bn_aggr(moments[:, at, :], stats[:, at].rearrange("p q s -> p (q s)")).then_inc(b_var, 1)
                dve.wait_ge(b_std, n + 1)
                f = affine[:, at]
                dve.reciprocal(f[:, 1:2], f[:, 0:1]).then_inc(b_own, 1)
                dve.wait_ge(b_own, 6 * n + 4)
                dve.tensor_tensor(f[:, 2:3], f[:, 1:2], lanes[:, 3 * k + 1, j:j + 1], ALU.mult).then_inc(b_own, 1)
                dve.wait_ge(b_own, 6 * n + 5)
                dve.tensor_tensor(f[:, 3:4], f[:, 2:3], moments[:, at, 0:1], ALU.mult).then_inc(b_own, 1)
                dve.wait_ge(b_own, 6 * n + 6)
                dve.tensor_tensor(f[:, 3:4], lanes[:, 3 * k + 2, j:j + 1], f[:, 3:4], ALU.subtract).then_inc(b_aff, 1)

            for i in range(TILES + 1):
                if i < TILES:
                    row = fx.nodes[0:TILE, i, :]
                    dve.wait_ge(turned, i + 1)
                    dve.tensor_tensor(row, bank(6 + i % 2)[0:TILE], row, ALU.add).then_inc(added, 1)
                    dve.wait_ge(added, i + 1)
                    norm_stats(dve, fx, i % 2, row, stat_own, TILES + i + 1, var_ready)
                if i >= 1:
                    row = fx.nodes[0:TILE, i - 1, :]
                    dve.wait_ge(std_ready, TILES + i)
                    norm_rows(dve, fx, (i - 1) % 2, row, row, rstd_own, TILES + i).then_inc(normed, 1)

        @block.scalar
        def _(act):
            for t in range(TILES):
                act.wait_ge(var_ready, t + 1)
                norm_std(nc, fx, t % 2, std_ready)
            for c in range(CHUNKS):
                act.wait_ge(prod, c + 1)
                nc.scalar.activation(plane[0][:, c, :], region(c), ACT.Copy).then_inc(copied, 1)
            act.wait_ge(w_loaded, 128)

            def apply(n):
                k, j = n // CHUNKS, n % CHUNKS
                u = plane[1 - k][:, j, :]
                act.wait_ge(b_var, n + 1)
                nc.scalar.activation(affine[:, n % 2, 0:1], moments[:, n % 2, 1:2], ACT.Sqrt, bias=fx.eps[:, :]).then_inc(b_std, 1)
                act.wait_ge(b_aff, n + 1)
                nc.scalar.activation(u, u, (ACT.Relu, ACT.Identity)[k], bias=affine[:, n % 2, 3:4],
                                     scale=affine[:, n % 2, 2:3]).then_inc(applied, 1)

            for n in range(2 * CHUNKS):
                k, j = n // CHUNKS, n % CHUNKS
                act.wait_ge(prod, CHUNKS + n + 1)
                nc.scalar.activation(plane[1 - k][:, j, :], region(n), ACT.Identity,
                                     bias=lanes[:, 3 * k, j:j + 1]).then_inc(copied, 1)
                apply(n)
            for t in range(TILES):
                act.wait_ge(var_ready, TILES + t + 1)
                norm_std(nc, fx, t % 2, std_ready)

        @block.tensor
        def _(pe):
            for c in range(CHUNKS):
                if c >= 2:
                    pe.wait_ge(copied, c - 1)
                for k in range(TILES):
                    if c == 0:
                        pe.wait_ge(normed, k + 1)
                        pe.wait_ge(diag_ready, k + 1)
                    for a, z in CUTS:
                        mm = pe.matmul(region(c)[:, a:z], fx.nodes[0:TILE, k, c * 128:(c + 1) * 128],
                                       counts[0:TILE, k, a:z], start=(k == 0), stop=(k == TILES - 1))
                mm.then_inc(prod, 1)
            for n in range(2 * CHUNKS):
                k, j = n // CHUNKS, n % CHUNKS
                if n == 0:
                    pe.wait_ge(w_loaded, 128)
                pe.wait_ge(copied, CHUNKS + n - 1)
                for c in range(CHUNKS):
                    if j == 0:
                        pe.wait_ge((copied, applied)[k], c + 1)
                    for a, z in CUTS:
                        mm = pe.matmul(region(n)[:, a:z], w[k][:, c, j * 128:(j + 1) * 128], plane[k][:, c, a:z],
                                       start=(c == 0), stop=(c == CHUNKS - 1))
                mm.then_inc(prod, 1)
            pe.wait_ge(applied, 2 * CHUNKS)
            for t in range(TILES):
                if t >= 2:
                    pe.wait_ge(added, t - 1)
                for c in range(CHUNKS):
                    mm = pe.transpose(bank(6 + t % 2)[0:TILE, c * 128:(c + 1) * 128], plane[0][:, c, t * TILE:(t + 1) * TILE],
                                      fx.ident[:, :])
                mm.then_inc(turned, 1)


def fourth_layer(nc, fx, lw, psum, count_rows, out):
    with ExitStack() as ctx:
        def sem(name):
            return ctx.enter_context(nc.semaphore("L3_" + name))

        logs = fx.count_dst
        place = packer(nc, TURNED_AT)
        x_t = place("nodes_turned", [128, CHUNKS, NODES], F32)
        wx_t = place("projected_turned", [128, CHUNKS, NODES], F32)
        spread = place("source_scores_spread", [128, HEADS3, NODES], F32)
        values = packer(nc, VALUES_AT)("projected_parts", [128, TILES, HEADS3, 2, HDIM3], BF16)
        after = LAST_AT
        place = packer(nc, after)
        prob = place("row_probabilities", [128, 2, NODES], F32)
        pt = [place(f"turned_{p}", [128, 2, TILES, TILE], BF16) for p in ("high", "low")]
        slope = place("source_slopes_spread", [128, 2, NODES], F32)
        part = place("output_part", [128, TILES, HDIM3], F32)
        offset = packer(nc, TURNED_AT)("logs_and_source_scores", [128, 2, NODES], F32)
        place = packer(nc, after + CHUNKS * DIM * 4 + DIM * 4)
        wf = place("projected_rows", [128, 2, DIM], F32)
        wide = place("source_vectors_spread", [128, HEADS3, 128], F32)
        plain = packer(nc, after + 18432)("plain_logs_by_target", [128, 2, NODES], F32)

        loaded, stored = sem("diagonal_loaded"), sem("stored")
        target, bias_a, col_b, a_src, a_tgt, w_sb, row_b = (lw.target, lw.bias_a, lw.col_b, lw.a_src, lw.a_tgt, lw.w_sb,
                                                            lw.row_b)
        log_plain, log_ready, own = sem("logs_plain"), sem("logs_ready"), sem("log_step")
        turned, x_copied, spread_ready = sem("nodes_turned"), sem("turned_copied"), sem("vectors_spread")
        prod, copied, v_prod, v_sum = sem("products"), sem("products_copied"), sem("value_products"), sem("values_summed")
        v_high, v_low, r_prod, r_ready = sem("values_high"), sem("values_low"), sem("target_products"), sem("targets_ready")
        slope_ready, bent, offset_ready = sem("slopes_ready"), sem("relu_of_slopes"), sem("offsets_ready")
        scored, peaked = sem("scored"), sem("peaked")
        exped, mass_own, inverted = sem("exped"), sem("mass_step"), sem("inverted")
        p_turned, p_high, p_low, pv = sem("p_turned"), sem("p_high"), sem("p_low"), sem("weighted")
        half, summed, joined = sem("half_scaled"), sem("halves_joined"), sem("nodes_joined")
        stat_own, var_ready, std_ready = sem("stats_step"), sem("variance_ready"), sem("std_ready")
        rstd_own, normed = sem("rstd_step"), sem("normed")

        def region(c):
            return psum[:, (c % 2) * 3 * BANK:(c % 2) * 3 * BANK + NODES]

        def bank(n):
            return psum[:, n * BANK:(n + 1) * BANK]

        def cols(t):
            return slice(t * TILE, (t + 1) * TILE)

        def unit_views(source, place_, u, j):
            n = min(4, TILES - 4 * u)
            return (source[0:TILE, 0:n * TILE].rearrange("p (d n) -> p d n", d=n), place_[0:TILE, j % 2, 4 * u:4 * u + n, :])

        BANKS = ((3, 4, 7), (2, 5, 6))

        def behind(h, i, k, first, last):
            if i >= k:
                return None if last else (h, i - k)
            return None if first else (h - 1, TILES + i - k)

        def run_heads(eng, step):
            for i in range(TILES):
                step(0, i, True, False)
            with eng.Fori(1, HEADS3) as h:
                for i in range(TILES):
                    step(h, i, False, False)
            for i in range(5):
                step(HEADS3, i, False, True)

        block = ctx.enter_context(nc.Block())

        @block.sync
        def _(sp):
            for t in range(TILES):
                at = slice(t * TILE, (t + 1) * TILE)
                sp.dma_start(logs[0:TILE, t, at], count_rows[at, at]).then_inc(loaded, 16)
            parts = ((0, TILES // 2), (TILES // 2, TILES - 2), (TILES - 2, TILES))
            for a, z in parts:
                sp.wait_ge(normed, z)
                sp.dma_start(out[a * TILE:z * TILE].rearrange("(t p) d -> p t d", p=TILE),
                             fx.nodes[0:TILE, a:z]).then_inc(stored, 16)
            sp.wait_ge(stored, 16 * len(parts))

        ALL = 16 * TILES

        @block.gpsimd
        def _(pool):
            for t in range(TILES):
                pool.wait_ge(v_high, t + 1)
                nc.gpsimd.tensor_tensor(values[0:TILE, t, :, 1, :], wf[0:TILE, t % 2, :].rearrange("p (h d) -> p h d", d=HDIM3),
                                        values[0:TILE, t, :, 0, :], ALU.subtract).then_inc(v_low, 1)
            pool.wait_ge(copied, CHUNKS + HEADS3)
            pool.wait_ge(r_prod, TILES)
            pool.wait_ge(log_ready, TILES)

            def step(h, i, first, last):
                T = 10 * h + i
                five_back = behind(h, i, 5, first, last)
                if not last:
                    if not first or i >= 2:
                        wait_apart(pool, fx, scored, T - 1)
                    nc.gpsimd.tensor_tensor(offset[0:TILE, i % 2, :], logs[0:TILE, i, 0:NODES],
                                            spread[0:TILE, bass.ds(h, 1), :].rearrange("p a n -> p (a n)"),
                                            ALU.add).then_inc(offset_ready, 1)
                if five_back:
                    hh, j = five_back
                    wait_apart(pool, fx, summed, T - 4)
                    at = fx.nodes[0:TILE, j, bass.ds(hh * HDIM3, HDIM3)]
                    nc.gpsimd.tensor_tensor(at, at, part[0:TILE, j, :], ALU.add).then_inc(joined, 1)

            run_heads(pool, step)

        @block.vector
        def _(dve):
            steps = [0]
            dve.wait_ge(loaded, ALL)
            for h in range(HEADS3):
                dve.tensor_scalar(wide[:, h, :], fx.ones[:, :], a_src[:, h:h + 1], None, ALU.mult).then_inc(spread_ready, 1)
            for t in range(TILES):
                dve.wait_ge(log_plain, t + 1)
                log_counts(dve, logs[0:TILE, t, 0:NODES], plain[0:TILE, t % 2, :], 1.0, log_ready, own, steps)
                dve.wait_ge(v_prod, t + 1)
                if t >= 2:
                    dve.wait_ge(v_low, t - 1)
                dve.tensor_tensor(wf[0:TILE, t % 2, :], bank(6 + t % 2)[0:TILE], row_b[0:TILE, :], ALU.add).then_inc(v_sum, 1)
            dve.wait_ge(r_prod, TILES)
            r = target[0:TILE].rearrange("p t h -> p (t h)")
            dve.tensor_tensor(target[0:TILE], bank(6)[0:TILE, 0:TILES * HEADS3].rearrange("p (t h) -> p t h", h=HEADS3),
                              bias_a[0:TILE, :].unsqueeze(1).broadcast_to([TILE, TILES, HEADS3]), ALU.add).then_inc(own, 1)
            dve.wait_ge(own, steps[0] + 1)
            dve.tensor_scalar(r, r, -0.8, None, ALU.mult).then_inc(r_ready, 1)
            dve.wait_ge(v_low, TILES)
            dve.wait_ge(copied, CHUNKS + HEADS3)

            def step(h, i, first, last):
                T = 10 * h + i
                one, two_back, four_back = (behind(h, i, k, first, last) for k in (1, 2, 4))
                p = fx.peak[0:TILE, i % 2]
                if not last:
                    dve.wait_ge(offset_ready, T + 1)
                    wait_apart(dve, fx, bent, T + 1)
                    dve.tensor_tensor_reduce(prob[0:TILE, i % 2, :], prob[0:TILE, i % 2, :], offset[0:TILE, i % 2, :], 1.0,
                                             MASKED, ALU.add, ALU.max, p[:, 0:1]).then_inc(scored, 1)
                if one:
                    m = fx.mass[0:TILE, one[1]]
                    dve.wait_ge(exped, T)
                    dve.tensor_scalar(m[:, 1:2], m[:, 0:1], 1e-30, None, ALU.max).then_inc(mass_own, 1)
                if not last:
                    dve.wait_ge(scored, T + 1)
                    dve.tensor_scalar(p[:, 1:2], p[:, 0:1], MASKED * 1e-5, -1.0, ALU.max, ALU.mult).then_inc(peaked, 1)
                if one:
                    dve.wait_ge(mass_own, T)
                    dve.reciprocal(m[:, 2:3], m[:, 1:2]).then_inc(inverted, 1)
                if four_back:
                    j = four_back[1]
                    dve.wait_ge(half, T - 3)
                    dve.scalar_tensor_tensor(part[0:TILE, j, :], bank(j % 2)[0:TILE, 0:HDIM3], fx.mass[0:TILE, j, 2:3],
                                             part[0:TILE, j, :], ALU.mult, ALU.add).then_inc(summed, 1)
                if two_back:
                    j = two_back[1]
                    for u in range(3):
                        dve.wait_ge(p_high, 3 * T - 5 + u)
                        src, dst = unit_views(bank(BANKS[j % 2][u]), pt[1], u, j)
                        high = unit_views(bank(BANKS[j % 2][u]), pt[0], u, j)[1]
                        dve.tensor_tensor(dst, src, high, ALU.subtract).then_inc(p_low, 1)

            run_heads(dve, step)
            dve.wait_ge(joined, TILES * HEADS3)
            for i in range(TILES + 1):
                if i < TILES:
                    norm_stats(dve, fx, i % 2, fx.nodes[0:TILE, i, :], stat_own, i + 1, var_ready)
                if i >= 1:
                    row = fx.nodes[0:TILE, i - 1, :]
                    dve.wait_ge(std_ready, i)
                    norm_rows(dve, fx, (i - 1) % 2, row, row, rstd_own, i).then_inc(normed, 1)

        @block.scalar
        def _(act):
            act.wait_ge(loaded, ALL)

            def log(t):
                if t >= 2:
                    act.wait_ge(log_ready, t - 1)
                nc.scalar.activation(plain[0:TILE, t % 2, :], logs[0:TILE, t, 0:NODES], ACT.Ln,
                                     bias=fx.tiny[0:TILE, :]).then_inc(log_plain, 1)

            for t in range(TILES):
                act.wait_ge(turned, t + 1)
                nc.scalar.activation(x_t[:, :, cols(t)], bank(6 + t % 2)[:, 0:4 * TILE].rearrange("p (c n) -> p c n", c=4),
                                     ACT.Copy).then_inc(x_copied, 1)
            for t in range(TILES):
                log(t)
                act.wait_ge(v_sum, t + 1)
                nc.scalar.activation(values[0:TILE, t, :, 0, :], wf[0:TILE, t % 2, :].rearrange("p (h d) -> p h d", d=HDIM3),
                                     ACT.Copy).then_inc(v_high, 1)
            for j in range(CHUNKS):
                act.wait_ge(prod, j + 1)
                nc.scalar.activation(wx_t[:, j, :], region(j), ACT.Identity, bias=col_b[:, j:j + 1]).then_inc(copied, 1)
            for h in range(HEADS3):
                act.wait_ge(prod, CHUNKS + h + 1)
                nc.scalar.activation(spread[:, h, :], region(h), ACT.Copy).then_inc(copied, 1)
            act.wait_ge(copied, CHUNKS + HEADS3)
            act.wait_ge(v_low, TILES)
            act.wait_ge(r_ready, 1)
            nc.scalar.activation(slope[0:TILE, 0, :], spread[0:TILE, 0, :], ACT.Copy, scale=-0.8).then_inc(slope_ready, 1)

            def step(h, i, first, last):
                T = 10 * h + i
                one, two_back, four_back = (behind(h, i, k, first, last) for k in (1, 2, 4))
                if four_back:
                    j = four_back[1]
                    if not first and not last and i >= 4:
                        act.wait_ge(joined, 10 * h if i == TILES - 1 else T - 13)
                    act.wait_ge(inverted, T - 3)
                    act.wait_ge(pv, T - 3)
                    nc.scalar.activation(part[0:TILE, j, :], bank(j % 2)[0:TILE, HDIM3:2 * HDIM3], ACT.Copy,
                                         scale=fx.mass[0:TILE, j, 2:3]).then_inc(half, 1)
                if two_back:
                    j = two_back[1]
                    for u in range(3):
                        act.wait_ge(p_turned, 3 * T - 5 + u)
                        src, dst = unit_views(bank(BANKS[j % 2][u]), pt[0], u, j)
                        nc.scalar.activation(dst, src, ACT.Copy).then_inc(p_high, 1)
                if not last:
                    if i == 0:
                        wait_apart(act, fx, slope_ready, h + 1)
                    nc.scalar.activation(prob[0:TILE, i % 2, :], slope[0:TILE, bass.ds(h % 2, 1), :].rearrange("p a n -> p (a n)"),
                                         ACT.Relu, bias=target[0:TILE, i, bass.ds(h, 1)]).then_inc(bent, 1)
                if one:
                    j = one[1]
                    act.wait_ge(peaked, T)
                    nc.scalar.activation(prob[0:TILE, j % 2, :], prob[0:TILE, j % 2, :], ACT.Exp,
                                         bias=fx.peak[0:TILE, j % 2, 1:2], accum_out=fx.mass[0:TILE, j, 0:1]).then_inc(exped, 1)
                if not last and i == 5:
                    nxt = (h + 1) % HEADS3
                    nc.scalar.activation(slope[0:TILE, bass.ds((h + 1) % 2, 1), :], spread[0:TILE, bass.ds(nxt, 1), :],
                                         ACT.Copy, scale=-0.8).then_inc(slope_ready, 1)

            run_heads(act, step)
            for t in range(TILES):
                act.wait_ge(var_ready, t + 1)
                norm_std(nc, fx, t % 2, std_ready)

        @block.tensor
        def _(pe):
            for t in range(TILES):
                if t >= 2:
                    pe.wait_ge(x_copied, t - 1)
                for c in range(CHUNKS):
                    mm = pe.transpose(bank(6 + t % 2)[:, cols(c)], fx.nodes[0:TILE, t, c * 128:(c + 1) * 128],
                                      fx.ident[0:TILE, 0:TILE])
                mm.then_inc(turned, 1)
            pe.wait_ge(x_copied, TILES)
            pe.wait_ge(loaded, ALL)
            for t in range(TILES):
                if t >= 2:
                    pe.wait_ge(v_sum, t - 1)
                for c in range(CHUNKS):
                    mm = pe.matmul(bank(6 + t % 2)[0:TILE], x_t[:, c, cols(t)], w_sb[:, c, :], start=(c == 0),
                                   stop=(c == CHUNKS - 1))
                mm.then_inc(v_prod, 1)
            for j in range(CHUNKS):
                if j >= 2:
                    pe.wait_ge(copied, j - 1)
                for c in range(CHUNKS):
                    for a, z in CUTS:
                        mm = pe.matmul(region(j)[:, a:z], w_sb[:, c, j * 128:(j + 1) * 128], x_t[:, c, a:z],
                                       start=(c == 0), stop=(c == CHUNKS - 1))
                mm.then_inc(prod, 1)
            pe.wait_ge(copied, CHUNKS)
            pe.wait_ge(spread_ready, HEADS3)
            for h in range(HEADS3):
                if h >= 2:
                    pe.wait_ge(copied, CHUNKS + h - 1)
                for a, z in CUTS:
                    mm = pe.matmul(region(h)[:, a:z], wide[:, h, :], wx_t[:, h // 2, a:z], start=True, stop=True)
                mm.then_inc(prod, 1)
            pe.wait_ge(v_sum, TILES)
            for t in range(TILES):
                for c in range(CHUNKS):
                    mm = pe.matmul(bank(6)[0:TILE, t * HEADS3:(t + 1) * HEADS3], wx_t[:, c, cols(t)], a_tgt[:, c, :],
                                   start=(c == 0), stop=(c == CHUNKS - 1))
                mm.then_inc(r_prod, 1)
            pe.wait_ge(copied, CHUNKS + HEADS3)
            pe.wait_ge(r_ready, 1)

            def step(h, i, first, last):
                T = 10 * h + i
                one, two_back = behind(h, i, 1, first, last), behind(h, i, 2, first, last)
                if one:
                    j = one[1]
                    pe.wait_ge(exped, T)
                    if not first or j >= 2:
                        pe.wait_ge(p_low, 3 * T - 6)
                    for u in range(3):
                        for d in range(4 * u, min(4 * u + 4, TILES)):
                            mm = pe.transpose(bank(BANKS[j % 2][u])[0:TILE, cols(d - 4 * u)], prob[0:TILE, j % 2, cols(d)],
                                              fx.ident[0:TILE, 0:TILE])
                        mm.then_inc(p_turned, 1)
                if two_back:
                    hh, j = two_back
                    pe.wait_ge(p_low, 3 * T - 3)
                    if not first or j >= 2:
                        pe.wait_ge(summed, T - 3)
                    for d in range(TILES):
                        both = values[0:TILE, d, bass.ds(hh, 1), :, :].rearrange("p a k n -> p (a k n)")
                        for k in range(2):
                            mm = pe.matmul(bank(j % 2)[0:TILE, 0:2 * HDIM3], pt[k][0:TILE, j % 2, d, :], both,
                                           start=(d == 0 and k == 0), stop=(d == TILES - 1 and k == 1))
                    mm.then_inc(pv, 1)

            run_heads(pe, step)


_INS = ("x", "src", "dst", "edge_weight", "node_vec1", "L0_gnn_W", "L1_gnn_f_w1", "L1_gnn_f_b1", "L1_gnn_f_w2",
        "L1_gnn_f_b2", "L1_gnn_s1_w", "L1_gnn_s1_b", "L1_gnn_b1_w", "L1_gnn_b1_b", "L1_gnn_wq", "L1_gnn_bq", "L1_gnn_wk",
        "L1_gnn_bk", "L1_gnn_wv", "L1_gnn_bv", "L1_gnn_wo", "L1_gnn_bo", "L1_gnn_s2_w", "L1_gnn_s2_b", "L1_gnn_b2_w",
        "L1_gnn_b2_b", "L1_gnn_m_w1", "L1_gnn_m_b1", "L1_gnn_m_w2", "L1_gnn_m_b2", "L2_gnn_eps", "L2_gnn_W1", "L2_gnn_b1",
        "L2_gnn_gamma1", "L2_gnn_beta1", "L2_gnn_W2", "L2_gnn_b2", "L2_gnn_gamma2", "L2_gnn_beta2", "L3_gnn_Ws", "L3_gnn_Wb",
        "L3_gnn_a_w", "L3_gnn_a_b")


def graph_network(nc, t, out):
    fx = Fixed(nc)
    lw = LastWeights(nc)
    psum = nc.alloc_psum_tensor("psum", [128, 8 * BANK], F32)
    spill = nc.dram_tensor("block_inputs_kept", [LAYERS1, NODES, DIM], F32, kind="Internal").ap()
    count_rows = nc.dram_tensor("counts_kept", [WIDE, NODES], F32, kind="Internal").ap()

    def l1(name):
        return t["L1_gnn_" + name]

    def l2(name):
        return t["L2_gnn_" + name]

    edge_bands(nc, fx, psum, t["src"], t["dst"], t["edge_weight"], count_rows, t["x"])
    first_layer(nc, fx, psum, t["L0_gnn_W"], t["node_vec1"], l1("f_w1"), l1("f_b1"), l1("f_w2"), l1("f_b2"),
                l1("bq"), l1("bk"), l1("m_b1"))
    second_layer(nc, fx, psum, spill, count_rows, l1("wq"), l1("wk"), l1("wv"), l1("wo"), l1("m_w1"), l1("m_w2"), l1("bv"), l1("bo"),
                 l1("m_b2"), l1("s1_w"), l1("s1_b"), l1("b1_w"), l1("b1_b"), l1("s2_w"), l1("s2_b"), l1("b2_w"), l1("b2_b"))
    third_layer(nc, fx, lw, psum, l2("eps"), l2("W1"), l2("b1"), l2("gamma1"), l2("beta1"), l2("W2"),
                l2("b2"), l2("gamma2"), l2("beta2"), t["L3_gnn_Ws"], t["L3_gnn_Wb"], t["L3_gnn_a_w"], t["L3_gnn_a_b"])
    fourth_layer(nc, fx, lw, psum, count_rows, out)


def kernel(**inputs):
    import numpy as _np
    import concourse.bacc as _bacc
    from concourse import mybir as _mybir
    from concourse.bass_utils import run_bass_kernel_spmd as _run

    nc = _bacc.Bacc("TRN2", target_bir_lowering=False, num_devices=1)
    arrays, handles = {}, {}
    for name in _INS:
        a = _np.ascontiguousarray(inputs[name])
        arrays[f"in_{name}"] = a
        handles[name] = nc.dram_tensor(f"in_{name}", a.shape, _mybir.dt.from_np(a.dtype), kind="ExternalInput").ap()
    out = nc.dram_tensor("out_nodes", (NODES, DIM), _mybir.dt.float32, kind="ExternalOutput").ap()
    graph_network(nc, handles, out)
    r = _run(nc, [arrays], core_ids=[0])
    return r.results[0]["out_nodes"]
```
